# Optimizing a Trainium2 kernel written in Bass

```python
import numpy as np
import jax
import jax.numpy as jnp

def _softmax(x, axis=-1):
    return jax.nn.softmax(x, axis=axis)

def _gelu(x):
    return jax.nn.gelu(x, approximate=True)

def _silu(x):
    return jax.nn.silu(x)

def _sigmoid(x):
    return jax.nn.sigmoid(x)

def _layernorm(x, axis=-1, eps=1e-05):
    m = jnp.mean(x, axis=axis, keepdims=True)
    v = jnp.var(x, axis=axis, keepdims=True)
    return (x - m) / jnp.sqrt(v + eps)

def _scatter_add(tgt, idx, src, axis=0):
    return tgt.at[idx].add(src)

def _segment_sum(src, seg, n):
    return jax.ops.segment_sum(src, seg, n)
kernel_name = 'mk_gnn_ffn_d2_gnn_r32_2df3e9'

def setup_inputs(seed: int=0):
    np.random.seed(seed)
    _w = jnp.asarray

    def _rec_inputs():
        import jax
        import jax.numpy as jnp
        _gk = jax.random.key(seed)
        x = -0.0003713 + 1 * jax.random.normal(jax.random.fold_in(_gk, 1), (3125, 256), jnp.float32)
        _s = jax.random.randint(jax.random.fold_in(_gk, 2), (25000,), 0, 3125, jnp.int32)
        _d = jax.random.randint(jax.random.fold_in(_gk, 3), (25000,), 0, 3125, jnp.int32)
        _loop = jnp.arange(3125, dtype=jnp.int32)
        src = jnp.concatenate([_s, _d, _loop])
        dst = jnp.concatenate([_d, _s, _loop])
        _o = jnp.argsort(dst, stable=True)
        src = src[_o]
        dst = dst[_o]
        edge_weight1 = 0.000937891 + 0.999965 * jax.random.normal(jax.random.fold_in(_gk, 13), (53125, 1), jnp.float32)
        return (x, src, dst, edge_weight1)
    x, src, dst, edge_weight1 = _rec_inputs()

    def _L0_gnn_setup():
        import jax, jax.numpy as jnp
        import numpy as np
        DIM = 256
        H = 8
        HD = DIM // H
        N = 50000
        E = 25000
        FFN = 4 * DIM
        EPS = 1e-05

        def layer_norm(x, g, b):
            mu = jnp.mean(x, axis=-1, keepdims=True)
            var = jnp.mean((x - mu) ** 2, axis=-1, keepdims=True)
            return (x - mu) * jax.lax.rsqrt(var + EPS) * g + b

        def _mhsa(h, edge_bias, src, dst, Wq, Wk, Wv, Wp, bp):
            n = h.shape[0]
            Q = (h @ Wq).reshape(n, H, HD)
            K = (h @ Wk).reshape(n, H, HD)
            V = (h @ Wv).reshape(n, H, HD)
            score = jnp.einsum('ehd,ehd->eh', K[src], Q[dst]) / np.sqrt(HD) + edge_bias
            m = jax.ops.segment_max(score, dst, num_segments=n)
            ex = jnp.exp(score - m[dst])
            denom = jax.ops.segment_sum(ex, dst, num_segments=n)
            attn = ex / denom[dst]
            out = jax.ops.segment_sum(attn[:, :, None] * V[src], dst, num_segments=n)
            return out.reshape(n, DIM) @ Wp + bp
        key = jax.random.key(seed)
        ks = jax.random.split(key, 16)
        s = 1.0 / np.sqrt(DIM)
        inp = {'h': jax.random.normal(ks[0], (N, DIM), jnp.float32), 'edge_bias': jax.random.normal(ks[1], (E, 1), jnp.float32), 'src': jax.random.randint(ks[2], (E,), 0, N, jnp.int32), 'dst': jax.random.randint(ks[3], (E,), 0, N, jnp.int32), 'Wq': jax.random.normal(ks[4], (DIM, DIM), jnp.float32) * s, 'Wk': jax.random.normal(ks[5], (DIM, DIM), jnp.float32) * s, 'Wv': jax.random.normal(ks[6], (DIM, DIM), jnp.float32) * s, 'Wp': jax.random.normal(ks[7], (DIM, DIM), jnp.float32) * s, 'bp': jnp.zeros((DIM,), jnp.float32), 'ln1_g': jnp.ones((DIM,), jnp.float32), 'ln1_b': jnp.zeros((DIM,), jnp.float32), 'ln2_g': jnp.ones((DIM,), jnp.float32), 'ln2_b': jnp.zeros((DIM,), jnp.float32), 'W1': jax.random.normal(ks[8], (DIM, FFN), jnp.float32) * s, 'b1': jnp.zeros((FFN,), jnp.float32), 'W2': jax.random.normal(ks[9], (FFN, DIM), jnp.float32) * (1.0 / np.sqrt(FFN)), 'b2': jnp.zeros((DIM,), jnp.float32)}
        return inp
    _L0_gnn_all = _L0_gnn_setup()
    _L0_gnn_in = {k: v for k, v in _L0_gnn_all.items() if k in ('Wq', 'Wk', 'Wv', 'Wp', 'bp', 'ln1_g', 'ln1_b', 'ln2_g', 'ln2_b', 'W1', 'b1', 'W2', 'b2')}
    del _L0_gnn_all

    def _L0_ffn_setup():
        import jax, jax.numpy as jnp
        import numpy as np
        NUM_EXPERTS = 8
        TOP_K = 2
        B, S, D = (8, 256, 256)

        def _moe(tokens, router_w, w1, b1, w2, b2):
            N = tokens.shape[0]
            E = router_w.shape[0]
            logits = tokens.astype(jnp.float32) @ router_w.astype(jnp.float32).T
            probs = jax.nn.softmax(logits, axis=-1)
            rw, re = jax.lax.top_k(probs, TOP_K)
            if TOP_K > 1:
                rw = rw / jnp.maximum(rw.sum(-1, keepdims=True), 1e-12)
            rw = rw.astype(tokens.dtype)
            combine = jnp.zeros((N, E), tokens.dtype).at[jnp.arange(N)[:, None], re].set(rw)
            out = tokens
            for e in range(E):
                h = jax.nn.gelu(tokens @ w1[e] + b1[e], approximate=False)
                y = h @ w2[e] + b2[e]
                out = out + combine[:, e:e + 1] * y
            return out
        key = jax.random.key(seed)
        ks = jax.random.split(key, 4)
        scale = 1.0 / np.sqrt(D).astype(np.float32)
        return {'input_embeddings': jax.random.normal(ks[0], (B, S, D), jnp.float32), 'router_w': jax.random.normal(ks[1], (NUM_EXPERTS, D), jnp.float32) * scale, 'w1': jax.random.normal(ks[2], (NUM_EXPERTS, D, D), jnp.float32) * scale, 'b1': jnp.zeros((NUM_EXPERTS, D), jnp.float32), 'w2': jax.random.normal(ks[3], (NUM_EXPERTS, D, D), jnp.float32) * scale, 'b2': jnp.zeros((NUM_EXPERTS, D), jnp.float32)}
    _L0_ffn_all = _L0_ffn_setup()
    _L0_ffn_in = {k: v for k, v in _L0_ffn_all.items() if k in ('router_w', 'w1', 'b1', 'w2', 'b2')}
    del _L0_ffn_all

    def _L1_gnn_setup():
        import jax, jax.numpy as jnp
        import numpy as np
        N = 50000
        E = 50000
        D = 256
        H = 256
        EPS = 1e-05

        def _gnn_layer(x, row, col, W, b, g, beta):
            n = x.shape[0]
            neigh = x[col]
            agg = jax.ops.segment_sum(neigh, row, num_segments=n)
            deg = jax.ops.segment_sum(jnp.ones((row.shape[0],), x.dtype), row, num_segments=n)
            deg = jnp.maximum(deg, 1.0)[:, None]
            h = (x + agg / deg) @ W.T + b
            mu = jnp.mean(h, axis=-1, keepdims=True)
            var = jnp.mean(jnp.square(h - mu), axis=-1, keepdims=True)
            hn = (h - mu) * jax.lax.rsqrt(var + EPS) * g + beta
            return jax.nn.silu(hn)
        key = jax.random.key(seed)
        ks = jax.random.split(key, 12)
        x = jax.random.normal(ks[0], (N, D), dtype=jnp.float32)
        edge_index = jax.random.randint(ks[1], (2, E), 0, N, dtype=jnp.int32)
        s0 = 1.0 / np.sqrt(D)
        s1 = 1.0 / np.sqrt(H)
        W0 = jax.random.uniform(ks[2], (H, D), jnp.float32, -s0, s0)
        b0 = jax.random.uniform(ks[3], (H,), jnp.float32, -s0, s0)
        g0 = jnp.ones((H,), jnp.float32)
        beta0 = jnp.zeros((H,), jnp.float32)
        W1 = jax.random.uniform(ks[4], (H, H), jnp.float32, -s1, s1)
        b1 = jax.random.uniform(ks[5], (H,), jnp.float32, -s1, s1)
        g1 = jnp.ones((H,), jnp.float32)
        beta1 = jnp.zeros((H,), jnp.float32)
        return {'x': x, 'edge_index': edge_index, 'W0': W0, 'b0': b0, 'g0': g0, 'beta0': beta0, 'W1': W1, 'b1': b1, 'g1': g1, 'beta1': beta1}
    _L1_gnn_all = _L1_gnn_setup()
    _L1_gnn_in = {k: v for k, v in _L1_gnn_all.items() if k in ('W0', 'b0', 'g0', 'beta0', 'W1', 'b1', 'g1', 'beta1')}
    del _L1_gnn_all

    def _L1_ffn_setup():
        import jax, jax.numpy as jnp
        import numpy as np
        TOP_K = 2
        LN_EPS = 1e-05
        key = jax.random.key(seed)
        ks = jax.random.split(key, 8)
        B, S, D, E, H = (16, 1024, 256, 8, 1024)
        x = jax.random.normal(ks[0], (B, S, D), dtype=jnp.float32)
        Wr = jax.random.normal(ks[1], (D, E), dtype=jnp.float32) * 0.1
        br = jnp.zeros((E,), dtype=jnp.float32)
        ln_g = jnp.ones((E, D), dtype=jnp.float32)
        ln_b = jnp.zeros((E, D), dtype=jnp.float32)
        W1 = jax.random.normal(ks[2], (E, D, H), dtype=jnp.float32) * (1.0 / np.sqrt(D))
        b1 = jnp.zeros((E, H), dtype=jnp.float32)
        W2 = jax.random.normal(ks[3], (E, H, D), dtype=jnp.float32) * (1.0 / np.sqrt(H))
        b2 = jnp.zeros((E, D), dtype=jnp.float32)
        return {'x': x, 'Wr': Wr, 'br': br, 'ln_g': ln_g, 'ln_b': ln_b, 'W1': W1, 'b1': b1, 'W2': W2, 'b2': b2}
    _L1_ffn_all = _L1_ffn_setup()
    _L1_ffn_in = {k: v for k, v in _L1_ffn_all.items() if k in ('Wr', 'br', 'ln_g', 'ln_b', 'W1', 'b1', 'W2', 'b2')}
    del _L1_ffn_all
    return {'x': x, 'src': src, 'dst': dst, 'edge_weight1': edge_weight1, 'L0_gnn_Wq': _L0_gnn_in['Wq'], 'L0_gnn_Wk': _L0_gnn_in['Wk'], 'L0_gnn_Wv': _L0_gnn_in['Wv'], 'L0_gnn_Wp': _L0_gnn_in['Wp'], 'L0_gnn_bp': _L0_gnn_in['bp'], 'L0_gnn_ln1_g': _L0_gnn_in['ln1_g'], 'L0_gnn_ln1_b': _L0_gnn_in['ln1_b'], 'L0_gnn_ln2_g': _L0_gnn_in['ln2_g'], 'L0_gnn_ln2_b': _L0_gnn_in['ln2_b'], 'L0_gnn_W1': _L0_gnn_in['W1'], 'L0_gnn_b1': _L0_gnn_in['b1'], 'L0_gnn_W2': _L0_gnn_in['W2'], 'L0_gnn_b2': _L0_gnn_in['b2'], 'L0_ffn_router_w': _L0_ffn_in['router_w'], 'L0_ffn_w1': _L0_ffn_in['w1'], 'L0_ffn_b1': _L0_ffn_in['b1'], 'L0_ffn_w2': _L0_ffn_in['w2'], 'L0_ffn_b2': _L0_ffn_in['b2'], 'L1_gnn_W0': _L1_gnn_in['W0'], 'L1_gnn_b0': _L1_gnn_in['b0'], 'L1_gnn_g0': _L1_gnn_in['g0'], 'L1_gnn_beta0': _L1_gnn_in['beta0'], 'L1_gnn_W1': _L1_gnn_in['W1'], 'L1_gnn_b1': _L1_gnn_in['b1'], 'L1_gnn_g1': _L1_gnn_in['g1'], 'L1_gnn_beta1': _L1_gnn_in['beta1'], 'L1_ffn_Wr': _L1_ffn_in['Wr'], 'L1_ffn_br': _L1_ffn_in['br'], 'L1_ffn_ln_g': _L1_ffn_in['ln_g'], 'L1_ffn_ln_b': _L1_ffn_in['ln_b'], 'L1_ffn_W1': _L1_ffn_in['W1'], 'L1_ffn_b1': _L1_ffn_in['b1'], 'L1_ffn_W2': _L1_ffn_in['W2'], 'L1_ffn_b2': _L1_ffn_in['b2']}

def reference(x, src, dst, edge_weight1, L0_gnn_Wq, L0_gnn_Wk, L0_gnn_Wv, L0_gnn_Wp, L0_gnn_bp, L0_gnn_ln1_g, L0_gnn_ln1_b, L0_gnn_ln2_g, L0_gnn_ln2_b, L0_gnn_W1, L0_gnn_b1, L0_gnn_W2, L0_gnn_b2, L0_ffn_router_w, L0_ffn_w1, L0_ffn_b1, L0_ffn_w2, L0_ffn_b2, L1_gnn_W0, L1_gnn_b0, L1_gnn_g0, L1_gnn_beta0, L1_gnn_W1, L1_gnn_b1, L1_gnn_g1, L1_gnn_beta1, L1_ffn_Wr, L1_ffn_br, L1_ffn_ln_g, L1_ffn_ln_b, L1_ffn_W1, L1_ffn_b1, L1_ffn_W2, L1_ffn_b2):
    import jax
    import jax.numpy as jnp

    def _L0_gnn_ref(h, edge_bias, src, dst, Wq, Wk, Wv, Wp, bp, ln1_g, ln1_b, ln2_g, ln2_b, W1, b1, W2, b2):
        import jax, jax.numpy as jnp
        import numpy as np
        DIM = 256
        H = 8
        HD = DIM // H
        N = 50000
        E = 25000
        FFN = 4 * DIM
        EPS = 1e-05

        def layer_norm(x, g, b):
            mu = jnp.mean(x, axis=-1, keepdims=True)
            var = jnp.mean((x - mu) ** 2, axis=-1, keepdims=True)
            return (x - mu) * jax.lax.rsqrt(var + EPS) * g + b

        def _mhsa(h, edge_bias, src, dst, Wq, Wk, Wv, Wp, bp):
            n = h.shape[0]
            Q = (h @ Wq).reshape(n, H, HD)
            K = (h @ Wk).reshape(n, H, HD)
            V = (h @ Wv).reshape(n, H, HD)
            score = jnp.einsum('ehd,ehd->eh', K[src], Q[dst]) / np.sqrt(HD) + edge_bias
            m = jax.ops.segment_max(score, dst, num_segments=n)
            ex = jnp.exp(score - m[dst])
            denom = jax.ops.segment_sum(ex, dst, num_segments=n)
            attn = ex / denom[dst]
            out = jax.ops.segment_sum(attn[:, :, None] * V[src], dst, num_segments=n)
            return out.reshape(n, DIM) @ Wp + bp
        attn_out = _mhsa(h, edge_bias, src, dst, Wq, Wk, Wv, Wp, bp)
        h1 = layer_norm(h + attn_out, ln1_g, ln1_b)
        ffn_out = jax.nn.gelu(h1 @ W1 + b1, approximate=False) @ W2 + b2
        return layer_norm(h1 + ffn_out, ln2_g, ln2_b)

    def _L0_ffn_ref(input_embeddings, router_w, w1, b1, w2, b2):
        import jax, jax.numpy as jnp
        import numpy as np
        NUM_EXPERTS = 8
        TOP_K = 2
        B, S, D = (8, 256, 256)

        def _moe(tokens, router_w, w1, b1, w2, b2):
            N = tokens.shape[0]
            E = router_w.shape[0]
            logits = tokens.astype(jnp.float32) @ router_w.astype(jnp.float32).T
            probs = jax.nn.softmax(logits, axis=-1)
            rw, re = jax.lax.top_k(probs, TOP_K)
            if TOP_K > 1:
                rw = rw / jnp.maximum(rw.sum(-1, keepdims=True), 1e-12)
            rw = rw.astype(tokens.dtype)
            combine = jnp.zeros((N, E), tokens.dtype).at[jnp.arange(N)[:, None], re].set(rw)
            out = tokens
            for e in range(E):
                h = jax.nn.gelu(tokens @ w1[e] + b1[e], approximate=False)
                y = h @ w2[e] + b2[e]
                out = out + combine[:, e:e + 1] * y
            return out
        b, s, d = input_embeddings.shape
        tokens = input_embeddings.reshape(b * s, d)
        return _moe(tokens, router_w, w1, b1, w2, b2).reshape(b, s, d)

    def _L1_gnn_ref(x, edge_index, W0, b0, g0, beta0, W1, b1, g1, beta1):
        import jax, jax.numpy as jnp
        import numpy as np
        N = 50000
        E = 50000
        D = 256
        H = 256
        EPS = 1e-05

        def _gnn_layer(x, row, col, W, b, g, beta):
            n = x.shape[0]
            neigh = x[col]
            agg = jax.ops.segment_sum(neigh, row, num_segments=n)
            deg = jax.ops.segment_sum(jnp.ones((row.shape[0],), x.dtype), row, num_segments=n)
            deg = jnp.maximum(deg, 1.0)[:, None]
            h = (x + agg / deg) @ W.T + b
            mu = jnp.mean(h, axis=-1, keepdims=True)
            var = jnp.mean(jnp.square(h - mu), axis=-1, keepdims=True)
            hn = (h - mu) * jax.lax.rsqrt(var + EPS) * g + beta
            return jax.nn.silu(hn)
        row, col = (edge_index[0], edge_index[1])
        x = _gnn_layer(x, row, col, W0, b0, g0, beta0)
        x = _gnn_layer(x, row, col, W1, b1, g1, beta1)
        return x

    def _L1_ffn_ref(x, Wr, br, ln_g, ln_b, W1, b1, W2, b2):
        import jax, jax.numpy as jnp
        import numpy as np
        TOP_K = 2
        LN_EPS = 1e-05
        B, S, D = x.shape
        N = B * S
        xt = x.reshape(N, D)
        logits = xt @ Wr + br
        probs = jax.nn.softmax(logits, axis=-1)
        top_p, top_idx = jax.lax.top_k(probs, TOP_K)
        weights = top_p / top_p.sum(axis=-1, keepdims=True)
        mu = xt.mean(axis=-1, keepdims=True)
        var = ((xt - mu) ** 2).mean(axis=-1, keepdims=True)
        xn = (xt - mu) * jax.lax.rsqrt(var + LN_EPS)
        xe = xn[None, :, :] * ln_g[:, None, :] + ln_b[:, None, :]
        h = jax.nn.gelu(jnp.einsum('end,edh->enh', xe, W1) + b1[:, None, :], approximate=False)
        y = jnp.einsum('enh,ehd->end', h, W2) + b2[:, None, :]
        y_tok = jnp.transpose(y, (1, 0, 2))
        sel = jnp.take_along_axis(y_tok, top_idx[:, :, None], axis=1)
        out = (weights[:, :, None] * sel).sum(axis=1)
        return out.reshape(B, S, D)
    edge_index = jnp.stack([src, dst])
    x = x + _L0_gnn_ref(_layernorm(x, axis=-1), edge_weight1, src, dst, L0_gnn_Wq, L0_gnn_Wk, L0_gnn_Wv, L0_gnn_Wp, L0_gnn_bp, L0_gnn_ln1_g, L0_gnn_ln1_b, L0_gnn_ln2_g, L0_gnn_ln2_b, L0_gnn_W1, L0_gnn_b1, L0_gnn_W2, L0_gnn_b2)
    x = x + _L0_ffn_ref(_layernorm(x, axis=-1)[None], L0_ffn_router_w, L0_ffn_w1, L0_ffn_b1, L0_ffn_w2, L0_ffn_b2)[0]
    x = x + _L1_gnn_ref(_layernorm(x, axis=-1), edge_index, L1_gnn_W0, L1_gnn_b0, L1_gnn_g0, L1_gnn_beta0, L1_gnn_W1, L1_gnn_b1, L1_gnn_g1, L1_gnn_beta1)
    x = x + _L1_ffn_ref(_layernorm(x, axis=-1)[None], L1_ffn_Wr, L1_ffn_br, L1_ffn_ln_g, L1_ffn_ln_b, L1_ffn_W1, L1_ffn_b1, L1_ffn_W2, L1_ffn_b2)[0]
    return x

_drawn_inputs = setup_inputs


def setup_inputs(seed=0):
    import zlib

    import numpy as np

    out = dict(_drawn_inputs(seed))
    spreads = {'L0_gnn_bp': (0.0, 0.1),
     'L0_gnn_ln1_g': (1.0, 0.2),
     'L0_gnn_ln1_b': (0.0, 0.1),
     'L0_gnn_ln2_g': (1.0, 0.2),
     'L0_gnn_ln2_b': (0.0, 0.1),
     'L0_gnn_b1': (0.0, 0.1),
     'L0_gnn_b2': (0.0, 0.1),
     'L0_ffn_b1': (0.0, 0.355),
     'L0_ffn_b2': (0.0, 0.1),
     'L1_gnn_g0': (1.0, 0.2),
     'L1_gnn_beta0': (0.0, 0.1),
     'L1_gnn_g1': (1.0, 0.2),
     'L1_gnn_beta1': (0.0, 0.286),
     'L1_ffn_br': (0.0, 0.293),
     'L1_ffn_ln_g': (1.0, 0.2),
     'L1_ffn_ln_b': (0.0, 0.434),
     'L1_ffn_b1': (0.0, 0.455),
     'L1_ffn_b2': (0.0, 0.311)}
    factors = {'L1_gnn_b0': 2.77, 'L1_gnn_b1': 2.793}
    for name, (base, spread) in spreads.items():
        noise = np.random.default_rng([zlib.crc32(name.encode()), seed]).standard_normal(out[name].shape)
        drawn = base * np.exp(spread * noise) if base else spread * noise
        out[name] = jnp.asarray(drawn.astype(out[name].dtype))
    for name, factor in factors.items():
        out[name] = (out[name] * factor).astype(out[name].dtype)
    return out
```

```python
import math

import numpy as np

import concourse.bass as bass
from concourse import mybir
from contextlib import ExitStack

F32 = mybir.dt.float32
I32 = mybir.dt.int32
ALU = mybir.AluOpType
ACT = mybir.ActivationFunctionType
AX = mybir.AxisListType
ALL_MAX = bass.bass_isa.ReduceOp.max

P = 128
N = 3125
D = 256
KD = D // P
NT = -(-N // P)
E = 53125
ET = -(-E // P)
ETP = ET + 4
GT = 4
HEADS, HD = 8, 32
FFN = 1024
EPS = 1e-5
NEXP, TOPK = 8, 2
BT = 256
NBLK = (N * TOPK + NEXP * (BT - 1)) // BT
NSLOT = NBLK * BT
PAD_DST = NT * P
GK = -(-(NT * -(-ET // GT) + 4) // P)
NG = GK * P
VW = D + HEADS
SGT = 2
SG = (E + NT * SGT * P) // (SGT * P)
SBODY = 4
SG += -SG % SBODY
STILES = SG * SGT

C_IDENT = 0
C_IOTA = C_IDENT + P
C_TRI = C_IOTA + P
C_ONES = C_TRI + P
C_WBASE = C_ONES + P
C_VALID = C_WBASE + NT + 1
C_TRASH = C_VALID + NT
C_RANK = C_TRASH + NT * TOPK
C_TILE1 = C_RANK + NT * NEXP
C_TILER = C_TILE1 + ETP
C_WCOL = C_TILER + ETP
C_GRP = C_WCOL + 1
C_GRPW = C_GRP + GK
C_SGRP = C_GRPW + GK * NT
C_SPARE = C_SGRP + SG
C_END = C_SPARE + 1


def constants():
    c = np.zeros((P, C_END), np.float32)
    p = np.arange(P)
    c[:, C_IDENT:C_IDENT + P] = np.eye(P)
    c[:, C_IOTA:C_IOTA + P] = p
    c[:, C_TRI:C_TRI + P] = p[:, None] < p[None, :]
    c[:, C_ONES:C_ONES + P] = 1
    c[:, C_WBASE:C_WBASE + NT + 1] = P * np.arange(NT + 1)
    row = p[:, None] + P * np.arange(NT)
    c[:, C_VALID:C_VALID + NT] = row < N
    trash = np.where(row[:, :, None] < N, 0, NSLOT + row[:, :, None] - (NT - 1) * P + P * np.arange(TOPK))
    c[:, C_TRASH:C_TRASH + NT * TOPK] = trash.reshape(P, -1)
    c[:, C_RANK:C_RANK + NT * NEXP] = np.tile(NEXP - np.arange(NEXP), NT)
    c[:, C_TILE1:C_TILE1 + ETP] = np.arange(ETP) + 1
    c[:, C_TILER:C_TILER + ETP] = ETP - np.arange(ETP)
    c[:, C_WCOL] = p
    c[:, C_GRP:C_GRP + GK] = p[:, None] * GK + np.arange(GK)
    c[:, C_GRPW:C_GRPW + GK * NT] = np.tile(np.arange(NT), GK)
    c[:, C_SGRP:C_SGRP + SG] = np.arange(SG)
    c[:, C_SPARE] = STILES * P + p
    return c


class Chain:

    def __init__(self, eng, sem):
        self.eng, self.sem, self.n = eng, sem, 0

    def __call__(self, ins):
        ins.then_inc(self.sem, 1)
        self.n += 1
        self.eng.wait_ge(self.sem, self.n)


def over_tiles(eng, step, count=NT):
    step(0, 0, 0, True, False)
    step(1, 1, 0, True, False)
    with eng.Fori(1, (count - 1) // 2) as i:
        step(2 * i, 0, i, False, False)
        step(2 * i + 1, 1, i, False, False)
    step(count - 1, 0, (count - 1) // 2, False, True)


def over_pairs(eng, pairs, step):
    step(0, 0, 0, True, False)
    step(1, 1, 0, True, False)
    with eng.Fori(1, pairs) as i:
        step(2 * i, 0, i, False, False)
        step(2 * i + 1, 1, i, False, False)


def wait_if(eng, sem, value):
    if not isinstance(value, int) or value > 0:
        eng.wait_ge(sem, value)


def recycle_semaphores(nc):
    nums = sorted(set(nc.released_uncleared_semaphores))
    runs = []
    for n in nums:
        if runs and runs[-1][1] == n:
            runs[-1][1] = n + 1
        else:
            runs.append([n, n + 1])
    with nc.Block() as block:
        @block.gpsimd
        def _(pool):
            for lo, hi in runs:
                pool.sem_clear(range(lo, hi))


SOFTWARE = ([f"kv_in{r}" for r in range(4)] + [f"records{part}_stored{b}" for part in range(4) for b in range(2)] +
            [f"{what}{layer}_{b}" for what in ("scattered", "y_in") for layer in range(2) for b in range(2)] +
            [f"agg{layer}_rows_in{r}" for layer in range(2) for r in range(8)])


def at(i, n=1):
    return bass.ds(i, n)


def column(ap, n):
    return ap[:, at(n)]


def finish_ln(k, tag):
    nc, ST = k["nc"], k["ST"]
    with ExitStack() as s:
        tmp = s.enter_context(nc.sbuf_tensor("ln_tmp" + tag, [P, 5, NT + 1], F32))
        msum, diff, m2, sq, std = (tmp[:, j, :] for j in range(5))
        var = k["VAR"][:]
        step = s.enter_context(nc.semaphore("ln_step" + tag))
        var_ready = s.enter_context(nc.semaphore("ln_var_ready" + tag))
        std_ready = s.enter_context(nc.semaphore("ln_std_ready" + tag))
        block = s.enter_context(nc.Block())

        @block.vector
        def _(dve):
            link = Chain(dve, step)
            dve.tensor_tensor(msum, ST[:, :, 1], ST[:, :, 4], ALU.add).then_inc(step, 1)
            dve.tensor_tensor(diff, ST[:, :, 1], ST[:, :, 4], ALU.subtract).then_inc(step, 1)
            link.n = 2
            link(dve.tensor_tensor(m2, ST[:, :, 2], ST[:, :, 5], ALU.add))
            link(dve.tensor_tensor(sq, diff, diff, ALU.mult))
            link(dve.tensor_scalar(m2, m2, 1.0 / D, None, ALU.mult))
            dve.scalar_tensor_tensor(out=var, in0=sq, scalar=0.25, in1=m2, op0=ALU.mult,
                                     op1=ALU.add).then_inc(var_ready, 1)
            dve.wait_ge(std_ready, 1)
            link(dve.reciprocal(k["RSTD"][:], std))
            link(dve.scalar_tensor_tensor(out=k["NMR"][:], in0=msum, scalar=-0.5, in1=k["RSTD"][:],
                                          op0=ALU.mult, op1=ALU.mult))

        @block.scalar
        def _(act):
            act.wait_ge(var_ready, 1)
            act.activation(std, var, ACT.Sqrt, bias=k["EPSC"][:, 0:1]).then_inc(std_ready, 1)


def load_and_group(k):
    nc, a, C, ST = k["nc"], k["a"], k["C"], k["ST"]
    TC = ETP // GT
    ident, ones = C[:, C_IDENT:C_IDENT + P], C[:, C_ONES:C_ONES + P]
    with ExitStack() as s:
        def sb(name, shape, dt=F32):
            return s.enter_context(nc.sbuf_tensor(name, shape, dt))

        def sem(name):
            return s.enter_context(nc.semaphore(name))

        dsti = sb("dst_int", [P, ETP], I32)
        wlo, whi = sb("win_lo", [TC, GT]), sb("win_hi", [TC, GT])
        dlo, dhi = sb("diag_lo", [TC, GT, TC]), sb("diag_hi", [TC, GT, TC])
        ge, both = sb("win_ge", [NT, ETP]), sb("win_both", [NT, ETP])
        last1, firstr = sb("last_plus1", [NT, 1]), sb("first_rev", [NT, 1])
        span, cnt = sb("win_span", [NT, 1]), sb("win_cnt", [NT, 1])
        spani, cnti = sb("win_span_i", [NT, 1], I32), sb("win_cnt_i", [NT, 1], I32)
        both2 = sb("win_rhs", [NT, 2, NT])
        ws = sb("win_start_cnt", [P, 2, NT])
        zero = sb("win_zero", [P, NT])
        cinc, base = sb("win_cinc", [P, NT]), sb("win_base", [P, NT])
        big = sb("grp_big", [P, GK, NT])
        wv, tv = sb("grp_w", [P, GK]), sb("grp_t", [P, GK])
        table = sb("grp_table", [P, GK, 2], I32)
        pairf, pairi = sb("pair_f", [1, 1]), sb("pair_i", [1, 1], I32)
        pD = s.enter_context(nc.psum_tensor("p_dst", [TC, GT, P], F32))
        pLo = s.enter_context(nc.psum_tensor("p_lo", [NT, ETP], F32))
        pHi = s.enter_context(nc.psum_tensor("p_hi", [NT, ETP], F32))
        pW = s.enter_context(nc.psum_tensor("p_w", [P, 2 * NT], F32))
        const_in, edge_in, x_in = sem("const_in"), sem("edge_in"), sem("x_in")
        dst_ready, dst_turned, diag_ready = sem("dst_ready"), sem("dst_turned"), sem("diag_ready")
        bounds_ready, rhs_ready, starts_ready = sem("bounds_ready"), sem("rhs_ready"), sem("starts_ready")
        table_ready, table_out, table_in = sem("table_ready"), sem("table_out"), sem("table_in")
        zeros_ready, zeros_out = sem("zeros_ready"), sem("zeros_out")
        step = sem("group_step")
        fills = []
        for name in ("slots_in", "slots_out"):
            slots = a[name].rearrange("(p r) d -> p r d", p=P)
            count = slots.shape[1]
            fills += [slots[:, lo:min(lo + NT + 1, count), :] for lo in range(0, count, NT + 1)]
        block = s.enter_context(nc.Block())

        @block.sync
        def _(sp):
            sp.dma_start(dsti[:], a["dst"]).then_inc(edge_in, 16)
            sp.dma_start(C[:], a["consts"]).then_inc(const_in, 16)
            sp.dma_start(k["X"][:], a["x"].rearrange("(t p) d -> p t d", p=P)).then_inc(x_in, 16)
            sp.dma_start(k["SRC"][:], a["src"]).then_inc(edge_in, 16)
            sp.dma_start(k["BIAS"][:], a["edge_weight1"]).then_inc(edge_in, 16)
            sp.wait_ge(zeros_ready, 1)
            for part in fills:
                sp.dma_start(part, k["R"][:, 0:part.shape[1], :]).then_inc(zeros_out, 16)
            sp.wait_ge(table_ready, 1)
            sp.dma_start(a["groups"].rearrange("(p g) -> p g", p=P),
                         table[:].rearrange("p g two -> p (g two)")).then_inc(table_out, 16)
            sp.wait_ge(table_out, 16)
            sp.dma_start(k["GROUPS"][0:1, :], a["groups"].rearrange("(o g) -> o g", o=1)).then_inc(table_in, 16)
            sp.wait_ge(table_in, 16)
            sp.wait_ge(x_in, 16)
            sp.wait_ge(edge_in, 48)
            sp.wait_ge(zeros_out, 16 * len(fills))

        @block.gpsimd
        def _(pool):
            pool.memset(k["EPSC"][:], EPS)
            pool.memset(k["ST"][:, NT, :], 0.0)
            pool.memset(k["R"][:], 0.0).then_inc(zeros_ready, 1)

        @block.vector
        def _(dve):
            link = Chain(dve, step)
            dve.memset(zero[:], 0.0)
            dve.wait_ge(edge_in, 48)
            dve.tensor_copy(k["DST"][:], dsti[:]).then_inc(dst_ready, 1)
            dve.wait_ge(x_in, 16)
            with dve.Fori(0, NT) as n:
                dve.bn_stats(ST[:, at(n), :], k["X"][:, at(n), :])
            dve.wait_ge(dst_turned, 1)
            link(dve.tensor_reduce(wlo[:], pD[:], AX.X, ALU.min))
            link(dve.tensor_reduce(whi[:], pD[:], AX.X, ALU.max))
            dve.wait_ge(const_in, 16)
            idents = ident[0:TC, 0:TC].unsqueeze(1).to_broadcast([TC, GT, TC])
            dve.tensor_tensor(dlo[:], idents, wlo[:].unsqueeze(2).to_broadcast([TC, GT, TC]),
                              ALU.mult).then_inc(diag_ready, 1)
            dve.tensor_tensor(dhi[:], idents, whi[:].unsqueeze(2).to_broadcast([TC, GT, TC]),
                              ALU.mult).then_inc(diag_ready, 1)
            dve.wait_ge(bounds_ready, 1)
            wfirst, wnext = both2[:, 0, 0:1], both2[:, 0, 1:2]
            link(dve.tensor_scalar(wfirst, C[0:NT, C_WCOL:C_WCOL + 1], float(P), None, ALU.mult))
            link(dve.tensor_scalar(wnext, wfirst, float(P), None, ALU.add))
            link(dve.tensor_scalar(ge[:], pLo[:], wnext, None, ALU.is_lt))
            link(dve.scalar_tensor_tensor(out=both[:], in0=pHi[:], scalar=wfirst, in1=ge[:],
                                          op0=ALU.is_ge, op1=ALU.mult))
            link(dve.tensor_tensor(ge[:], both[:], C[0:NT, C_TILE1:C_TILE1 + ETP], ALU.mult))
            link(dve.tensor_reduce(last1[:], ge[:], AX.X, ALU.max))
            link(dve.tensor_tensor(ge[:], both[:], C[0:NT, C_TILER:C_TILER + ETP], ALU.mult))
            link(dve.tensor_reduce(firstr[:], ge[:], AX.X, ALU.max))
            link(dve.scalar_tensor_tensor(out=span[:], in0=last1[:], scalar=float(GT - 1 - ETP),
                                          in1=firstr[:], op0=ALU.add, op1=ALU.add))
            link(dve.tensor_scalar(spani[:], span[:], 0.0, None, ALU.max))
            link(dve.tensor_scalar(cnti[:], spani[:], 2, None, ALU.arith_shift_right))
            link(dve.tensor_copy(cnt[:], cnti[:]))
            link(dve.tensor_scalar(span[:], firstr[:], -1.0, float(ETP), ALU.mult, ALU.add))
            link(dve.tensor_scalar(both2[:, 0, :], ident[0:NT, 0:NT], span[:, 0:1], None, ALU.mult))
            dve.tensor_scalar(both2[:, 1, :], ident[0:NT, 0:NT], cnt[:, 0:1], None,
                              ALU.mult).then_inc(rhs_ready, 1)
            dve.wait_ge(starts_ready, 1)
            link(dve.tensor_copy(ws[:].rearrange("p a w -> p (a w)"), pW[:]))
            link(dve.tensor_tensor_scan(cinc[:], ws[:, 1, :], zero[:], 0.0, ALU.add, ALU.add))
            link(dve.tensor_tensor(base[:], cinc[:], ws[:, 1, :], ALU.subtract))
            link(dve.scalar_tensor_tensor(out=base[:], in0=base[:], scalar=-float(GT), in1=ws[:, 0, :],
                                          op0=ALU.mult, op1=ALU.add))
            grp = C[:, C_GRP:C_GRP + GK]
            wide = [P, GK, NT]
            link(dve.tensor_tensor(big[:], cinc[:].unsqueeze(1).to_broadcast(wide),
                                   grp.unsqueeze(2).to_broadcast(wide), ALU.is_le))
            link(dve.tensor_reduce(wv[:], big[:], AX.X, ALU.add))
            link(dve.tensor_tensor(big[:], C[:, C_GRPW:C_GRPW + GK * NT].rearrange("p (g w) -> p g w", w=NT),
                                   wv[:].unsqueeze(2).to_broadcast(wide), ALU.is_equal))
            link(dve.tensor_tensor(big[:], big[:], base[:].unsqueeze(1).to_broadcast(wide), ALU.mult))
            link(dve.tensor_reduce(tv[:], big[:], AX.X, ALU.add))
            link(dve.scalar_tensor_tensor(out=tv[:], in0=grp, scalar=float(GT), in1=tv[:],
                                          op0=ALU.mult, op1=ALU.add))
            link(dve.tensor_scalar(tv[:], tv[:], float(ET), None, ALU.min))
            link(dve.tensor_scalar(pairi[:], cinc[0:1, NT - 1:NT], 1.0, None, ALU.add))
            link(dve.tensor_scalar(k["NPAIR"][:], pairi[:], 1, None, ALU.arith_shift_right))
            link(dve.tensor_copy(table[:, :, 0], tv[:]))
            dve.tensor_copy(table[:, :, 1], wv[:]).then_inc(table_ready, 1)

        @block.tensor
        def _(pe):
            pe.wait_ge(const_in, 16)
            pe.wait_ge(dst_ready, 1)
            for c in range(GT):
                mm = pe.transpose(pD[:, c, :], k["DST"][:, c * TC:(c + 1) * TC], ident)
            mm.then_inc(dst_turned, 1)
            pe.wait_ge(diag_ready, 2)
            for out, diag in ((pLo, dlo), (pHi, dhi)):
                mm = pe.matmul(out[:], ones[0:TC, 0:NT], diag[:].rearrange("p c t -> p (c t)"),
                               start=True, stop=True)
            mm.then_inc(bounds_ready, 1)
            pe.wait_ge(rhs_ready, 1)
            pe.matmul(pW[:], ones[0:NT, :], both2[:].rearrange("p a w -> p (a w)"), start=True,
                      stop=True).then_inc(starts_ready, 1)


def normalise(eng, k, out, rows, n):
    return eng.tensor_scalar(out, rows, column(k["RSTD"], n), column(k["NMR"], n), ALU.mult, ALU.add)


def qkv(k):
    nc, a, C, X, QX = k["nc"], k["a"], k["C"], k["X"], k["QX"]
    finish_ln(k, "0")
    ident = C[:, C_IDENT:C_IDENT + P]
    with ExitStack() as s:
        def sb(name, shape, dt=F32):
            return s.enter_context(nc.sbuf_tensor(name, shape, dt))

        def sem(name):
            return s.enter_context(nc.semaphore(name))

        w = sb("qkv_w", [P, KD, 3 * D])
        hs = [sb(f"h_row{b}", [P, D]) for b in range(2)]
        hT = [sb(f"hT{b}", [P, KD, P]) for b in range(2)]
        kv = [sb(f"kv_out{b}", [P, 2 * D]) for b in range(2)]
        sq = [sb(f"qk_square{b}", [P, 2 * D]) for b in range(2)]
        norm = sb("qk_norm", [P, NT, 2 * HEADS])
        most, mostall = sb("most", [P, 4]), sb("most_all", [P, 4])
        bound = sb("bound", [P, 4])
        pT = [s.enter_context(nc.psum_tensor(f"p_hT{b}", [P, KD, P], F32)) for b in range(2)]
        pQ = [s.enter_context(nc.psum_tensor(f"p_q{b}", [P, 2 * D], F32)) for b in range(2)]
        pKV = [s.enter_context(nc.psum_tensor(f"p_kv{b}", [P, 2 * D], F32)) for b in range(2)]
        w_in, h_ready, turned, hT_ready = sem("w_in"), sem("h_ready"), sem("turned"), sem("hT_ready")
        mm_done, q_copied, squared, kv_ready = sem("mm_done"), sem("q_copied"), sem("squared"), sem("kv_ready")
        summed, kv_stored = sem("summed"), [sem("kv_stored0"), sem("kv_stored1")]
        q_step, most_ready, all_ready, root_ready = sem("q_step"), sem("most_ready"), sem("all_ready"), sem("root_ready")
        records = store_records(k, s, 0)
        block = s.enter_context(nc.Block())
        kv_rows = a["kv"].rearrange("(t p) d -> t p d", p=P)

        @block.sync
        def _(sp):
            sp.dma_start(w[:], a["w_qkv"]).then_inc(w_in, 16)

            def step(n, b, i, first, last):
                sp.wait_ge(kv_ready, n + 1)
                sp.dma_start(kv_rows[at(n)], kv[b][:]).then_inc(kv_stored[b], 16)

            over_tiles(sp, step)
            sp.wait_ge(kv_stored[0], 16 * ((NT + 1) // 2))
            sp.wait_ge(kv_stored[1], 16 * (NT // 2))

        @block.vector
        def _(dve):
            def begin(n, b, first):
                if not first:
                    dve.wait_ge(turned, n - 1)
                normalise(dve, k, hs[b][:].unsqueeze(1), X[:, at(n), :], n).then_inc(h_ready, 1)
                dve.wait_ge(turned, n + 1)
                dve.tensor_copy(hT[b][:], pT[b][:]).then_inc(hT_ready, 1)

            def step(n, b, i, first, last):
                if not last:
                    begin(n + 1, 1 - b, first and n == 0)
                dve.wait_ge(mm_done, n + 1)
                dve.tensor_copy(QX[:, at(n), 0:D], pQ[b][:, 0:D].unsqueeze(1)).then_inc(q_copied, 1)
                dve.wait_ge(q_copied, n + 1)
                q = QX[:, at(n), 0:D]
                dve.tensor_tensor(sq[b][:, 0:D].unsqueeze(1), q, q, ALU.mult).then_inc(squared, 1)
                dve.wait_ge(kv_ready, n + 1)
                key = kv[b][:, 0:D]
                dve.tensor_tensor(sq[b][:, D:2 * D], key, key, ALU.mult).then_inc(squared, 1)
                dve.wait_ge(squared, 2 * n + 2)
                dve.tensor_reduce(norm[:, at(n), :], sq[b][:].rearrange("p (h c) -> p h c", c=HD),
                                  AX.X, ALU.add).then_inc(summed, 1)

            dve.memset(QX[:, NT, 0:D], 0.0)
            dve.memset(QX[:, :, D:VW], 0.0)
            begin(0, 0, True)
            over_tiles(dve, step)
            link = Chain(dve, q_step)
            dve.wait_ge(summed, NT)
            link(dve.tensor_reduce(most[:, 0:1], norm[:, :, 0:HEADS], AX.XY, ALU.max))
            link(dve.tensor_reduce(most[:, 1:2], norm[:, :, HEADS:2 * HEADS], AX.XY, ALU.max))
            link(dve.tensor_reduce(most[:, 2:3], k["BIAS"][:], AX.X, ALU.max))
            link(dve.tensor_reduce(most[:, 3:4], k["BIAS"][:], AX.X, ALU.min))
            dve.tensor_scalar(most[:, 3:4], most[:, 3:4], -1.0, None, ALU.mult).then_inc(most_ready, 1)
            dve.wait_ge(root_ready, 1)
            link(dve.scalar_tensor_tensor(out=bound[:, 2:3], in0=bound[:, 0:1], scalar=1.001 / math.sqrt(HD),
                                          in1=bound[:, 1:2], op0=ALU.mult, op1=ALU.mult))
            link(dve.tensor_scalar(bound[:, 3:4], bound[:, 2:3], mostall[:, 2:3], -1.0, ALU.add, ALU.mult))
            link(dve.tensor_scalar(k["BIAS"][:], k["BIAS"][:], bound[:, 3:4], None, ALU.add))

        @block.gpsimd
        def _(pool):
            pool.memset(k["ACC"][:], 0.0)
            records(pool)
            pool.wait_ge(most_ready, 1)
            pool.partition_all_reduce(mostall[:], most[:], P, ALL_MAX).then_inc(all_ready, 1)

        @block.scalar
        def _(act):
            act.activation(bound[:, 0:1], k["EPSC"][:], ACT.Sqrt)

            def step(n, b, i, first, last):
                act.wait_ge(mm_done, n + 1)
                if not first:
                    act.wait_ge(kv_stored[b], 16 * i)
                    act.wait_ge(summed, n - 1)
                act.copy(kv[b][:], pKV[b][:]).then_inc(kv_ready, 1)

            over_tiles(act, step)
            act.wait_ge(all_ready, 1)
            act.activation(bound[:, 0:2], mostall[:, 0:2], ACT.Sqrt).then_inc(root_ready, 1)

        @block.tensor
        def _(pe):
            def turn(n, b):
                pe.wait_ge(h_ready, n + 1)
                for c in range(KD):
                    mm = pe.transpose(pT[b][:, c, :], hs[b][:, c * P:(c + 1) * P], ident)
                mm.then_inc(turned, 1)

            def step(n, b, i, first, last):
                if not last:
                    turn(n + 1, 1 - b)
                pe.wait_ge(hT_ready, n + 1)
                if not first:
                    pe.wait_ge(q_copied, n - 1)
                    pe.wait_ge(kv_ready, n - 1)
                for out, lo, hi in ((pQ[b], 0, D), (pKV[b], D, 3 * D)):
                    for c in range(KD):
                        mm = pe.matmul(out[:, 0:hi - lo], hT[b][:, c, :], w[:, c, lo:hi], start=(c == 0),
                                       stop=(c == KD - 1))
                mm.then_inc(mm_done, 1)

            pe.wait_ge(w_in, 16)
            turn(0, 0)
            over_tiles(pe, step)


def sort_by_source(k):
    nc, a, C = k["nc"], k["a"], k["C"]
    tri, ones = C[:, C_TRI:C_TRI + P], C[:, C_ONES:C_ONES + P]
    wide = [P, NT, ETP]
    with ExitStack() as s:
        def sb(name, shape, dt=F32):
            return s.enter_context(nc.sbuf_tensor(name, shape, dt))

        def sem(name):
            return s.enter_context(nc.semaphore(name))

        keyi, lowi, wini = (sb("source_" + n, [P, ETP], I32) for n in ("key", "low", "win"))
        win, pos, spare = (sb("edge_" + n, [P, ETP]) for n in ("win", "pos", "spare"))
        posi, lo7, hi7 = (sb("pos_" + n, [P, ETP], I32) for n in ("int", "low", "high"))
        lowf, highf, addr = (sb("addr_" + n, [P, ETP]) for n in ("low", "high", "row"))
        oh, cum = sb("win_onehot", wide), sb("win_running", wide)
        ends, cnt = sb("run_ends", [P, NT + 1]), sb("part_count", [P, NT])
        tot, pre = sb("win_total", [P, NT]), sb("part_prefix", [P, NT])
        grpi, grps, ginc, adj, nought = (sb("sgrp_" + n, [P, NT], dt) for n, dt in
                                         (("int", I32), ("cnt", F32), ("inc", F32), ("adj", F32), ("zero", F32)))
        which_w = sb("grp_which_w", [1, SG])
        turns = sb("turns_int", [1, 1], I32)
        empty = sb("empty_records", [P, STILES, 2], I32)
        pPre = s.enter_context(nc.psum_tensor("p_prefix", [P, NT], F32))
        pTot = s.enter_context(nc.psum_tensor("p_total", [P, NT], F32))
        key_in, empty_ready, records_out = sem("key_in"), sem("empty_ready"), sem("records_out")
        counts_ready, sums_ready, step = sem("counts_ready"), sem("sums_ready"), sem("sort_step")
        block = s.enter_context(nc.Block())

        @block.sync
        def _(sp):
            sp.dma_start(keyi[:], a["src_key"]).then_inc(key_in, 16)
            sp.wait_ge(empty_ready, 2)
            sp.dma_start(a["records"][0:STILES * P, :].rearrange("(p t) two -> p t two", p=P),
                         empty[:]).then_inc(records_out, 16)
            sp.wait_ge(records_out, 16)

        @block.gpsimd
        def _(pool):
            pool.memset(empty[:, :, 0], 0).then_inc(empty_ready, 1)
            pool.memset(empty[:, :, 1], -1).then_inc(empty_ready, 1)

        @block.vector
        def _(dve):
            link = Chain(dve, step)
            dve.wait_ge(key_in, 16)
            dve.memset(nought[:], 0.0)
            dve.memset(ends[:], 0.0)
            link(dve.tensor_scalar(wini[:], keyi[:], 7, None, ALU.arith_shift_right))
            link(dve.tensor_scalar(lowi[:], keyi[:], P - 1, None, ALU.bitwise_and))
            link(dve.tensor_copy(win[:], wini[:]))
            link(dve.tensor_copy(k["EDGES"][:, :, 0], k["DST"][:]))
            link(dve.tensor_copy(k["EDGES"][:, :, 1], lowi[:]))
            link(dve.tensor_tensor(oh[:], win[:].unsqueeze(1).to_broadcast(wide),
                                   C[:, C_GRPW:C_GRPW + NT].unsqueeze(2).to_broadcast(wide), ALU.is_equal))
            flat = oh[:].rearrange("p w t -> p (w t)")
            link(dve.tensor_tensor_scan(cum[:].rearrange("p w t -> p (w t)"), flat,
                                        nought[:, 0:1].to_broadcast([P, NT * ETP]), 0.0, ALU.add, ALU.add))
            link(dve.tensor_copy(ends[:, 1:NT + 1], cum[:, :, ETP - 1]))
            dve.tensor_tensor(cnt[:], ends[:, 1:NT + 1], ends[:, 0:NT], ALU.subtract).then_inc(counts_ready, 1)
            dve.wait_ge(sums_ready, 1)
            link(dve.tensor_copy(pre[:], pPre[:]))
            link(dve.tensor_scalar(grpi[:], pTot[:], 1.0, float(SGT * P - 1), ALU.max, ALU.add))
            link(dve.tensor_scalar(grpi[:], grpi[:], SGT.bit_length() + 6, None, ALU.arith_shift_right))
            link(dve.tensor_copy(grps[:], grpi[:]))
            link(dve.tensor_tensor_scan(ginc[:], grps[:], nought[:], 0.0, ALU.add, ALU.add))
            link(dve.tensor_tensor(adj[:], ginc[:], grps[:], ALU.subtract))
            link(dve.scalar_tensor_tensor(out=adj[:], in0=adj[:], scalar=float(SGT * P), in1=pre[:],
                                          op0=ALU.mult, op1=ALU.add))
            link(dve.scalar_tensor_tensor(out=adj[:], in0=adj[:], scalar=-1.0, in1=ends[:, 0:NT],
                                          op0=ALU.add, op1=ALU.subtract))
            link(dve.tensor_tensor(cum[:], cum[:], adj[:].unsqueeze(2).to_broadcast(wide), ALU.add))
            link(dve.tensor_tensor(cum[:], cum[:], oh[:], ALU.mult))
            link(dve.tensor_reduce(pos[:], cum[:].rearrange("p w t -> p t w"), AX.X, ALU.add))
            link(dve.tensor_copy(posi[:], pos[:]))
            link(dve.tensor_scalar(lo7[:], posi[:], P - 1, None, ALU.bitwise_and))
            link(dve.tensor_scalar(hi7[:], posi[:], 7, None, ALU.arith_shift_right))
            link(dve.tensor_copy(lowf[:], lo7[:]))
            link(dve.tensor_copy(highf[:], hi7[:]))
            link(dve.scalar_tensor_tensor(out=addr[:], in0=lowf[:], scalar=float(STILES), in1=highf[:],
                                          op0=ALU.mult, op1=ALU.add))
            link(dve.tensor_scalar(spare[:], win[:], float(NT), C[:, C_SPARE:C_SPARE + 1], ALU.is_ge, ALU.mult))
            link(dve.tensor_tensor(k["SADDR"][:], addr[:], spare[:], ALU.add))
            one_wide = [1, SG, NT]
            which = flat[0:1, 0:SG * NT].rearrange("o (g w) -> o g w", w=NT)
            link(dve.tensor_tensor(which, ginc[0:1, :].unsqueeze(1).to_broadcast(one_wide),
                                   C[0:1, C_SGRP:C_SGRP + SG].unsqueeze(2).to_broadcast(one_wide), ALU.is_le))
            link(dve.tensor_reduce(which_w[:], which, AX.X, ALU.add))
            link(dve.tensor_copy(k["SWIN"][:], which_w[:]))
            link(dve.tensor_scalar(turns[:], ginc[0:1, NT - 1:NT], float(SBODY - 1), None, ALU.add))
            link(dve.tensor_scalar(k["STURNS"][:], turns[:], SBODY.bit_length() - 1, None,
                                   ALU.arith_shift_right))

        @block.tensor
        def _(pe):
            pe.wait_ge(counts_ready, 1)
            pe.matmul(pPre[:], tri, cnt[:], start=True, stop=True)
            pe.matmul(pTot[:], ones, cnt[:], start=True, stop=True).then_inc(sums_ready, 1)


def table_values(nc, engine, table, lo, most):
    why = "the chip computed the table within these bounds"
    values = nc.values_load_multi_w_load_instructions(
        table[0:1, at(lo, len(most))], engines=[engine], min_val=0, max_val=max(most),
        skip_runtime_bounds_check_because=why)[1]
    return [nc.s_assert_within(v, 0, m, skip_runtime_bounds_check_because=why) for v, m in zip(values, most)]


def attention_edges(k):
    nc, a, C, QX, ACC = k["nc"], k["a"], k["C"], k["QX"], k["ACC"]
    ident, iota = C[:, C_IDENT:C_IDENT + P], C[:, C_IOTA:C_IOTA + P]
    ENG = mybir.EngineType
    with ExitStack() as s:
        def sb(name, shape, dt=F32):
            return s.enter_context(nc.sbuf_tensor(name, shape, dt))

        def sem(name):
            return s.enter_context(nc.semaphore(name))

        kv = [sb(f"kv_pair{r}", [P, 2, 2 * D]) for r in range(4)]
        idx = [sb(f"gather_idx{b}", [P, GT], I32) for b in range(2)]
        bias = [sb(f"edge_bias{b}", [P, GT]) for b in range(2)]
        oh = [sb(f"onehot{r}", [P, 2, P]) for r in range(4)]
        oht = [sb(f"onehot_turned{q}", [P, 2, P]) for q in range(2)]
        prod, red = sb("qk_prod", [P, 2, D]), sb("qk_sum", [P, 2, HEADS])
        score = [sb(f"score{q}", [P, 2, HEADS]) for q in range(2)]
        wv = [sb(f"weighted_v{q}", [P, 2, VW]) for q in range(2)]
        pQ = [s.enter_context(nc.psum_tensor(f"p_edge_q{q}", [P, 2, 4 * P], F32)) for q in range(2)]
        pT = [s.enter_context(nc.psum_tensor(f"p_turned{q}", [P, 4, P], F32)) for q in range(2)]
        pA = [s.enter_context(nc.psum_tensor(f"p_sums{b}", [P, 4 * P], F32)) for b in range(2)]
        kv_in = [k[f"kv_in{r}"] for r in range(4)]
        idx_ready, bias_ready, tally = sem("idx_ready"), sem("bias_ready"), sem("tally")
        oh_ready, turned, oht_ready, q_ready = sem("oh_ready"), sem("oh_turned"), sem("oht_ready"), sem("q_ready")
        prod_ready, red_ready, score_ready = sem("prod_ready"), sem("red_ready"), sem("score_ready")
        exp_ready, wv_ready, sums_ready, acc_done = (sem("exp_ready"), sem("wv_ready"), sem("pair_sums_ready"),
                                                     sem("acc_done"))
        block = s.enter_context(nc.Block())

        def pairs(eng):
            return eng.value_load(k["NPAIR"][0:1, 0:1], min_val=2, max_val=NG // 2 - 1)

        @block.gpsimd
        def _(pool):
            def step(b, p, i, first, last):
                t, = table_values(nc, ENG.Pool, k["GROUPS"], 2 * b, [ET])
                wait_if(pool, exp_ready, 2 * (b - 1))
                pool.sem_inc(tally, 1)
                pool.tensor_copy(idx[p][:], k["SRC"][:, at(t, GT)]).then_inc(idx_ready, 1)
                pool.tensor_copy(bias[p][:], k["BIAS"][:, at(t, GT)]).then_inc(bias_ready, 1)
                pool.wait_ge(idx_ready, b + 1)
                for q in range(2):
                    r, u = 2 * p + q, 2 * b + q
                    wait_if(pool, wv_ready, u - 3)
                    pool.sem_inc(tally, 1)
                    for j in range(2):
                        pool.indirect_dma_start(kv[r][:, j, :], None, a["kv"], bass.IndirectOffsetOnAxis(
                            ap=idx[p][:, 2 * q + j:2 * q + j + 1], axis=0)).then_inc(kv_in[r], 16)

            over_pairs(pool, pairs(pool), step)

        @block.vector
        def _(dve):
            def onehots(u, r, q, t, w):
                wait_if(dve, sums_ready, u - 3)
                for j in range(2):
                    ins = dve.tensor_scalar(oh[r][:, j, :], iota, column(C, C_WBASE + w),
                                            column(k["DST"], t + 2 * q + j), ALU.add, ALU.is_equal)
                ins.then_inc(oh_ready, 1)

            def weigh(u, r, q):
                dve.wait_ge(exp_ready, u + 1)
                dve.tensor_tensor(wv[q][:, :, 0:D].rearrange("p j (h c) -> p j h c", c=HD),
                                  kv[r][:, :, D:2 * D].rearrange("p j (h c) -> p j h c", c=HD),
                                  wv[q][:, :, D:VW].unsqueeze(3).to_broadcast([P, 2, HEADS, HD]),
                                  ALU.mult).then_inc(wv_ready, 1)

            def accumulate(b, p, w):
                dve.wait_ge(sums_ready, 2 * b + 2)
                dve.wait_ge(acc_done, b + 1)
                dve.tensor_tensor(ACC[:, at(w), :], ACC[:, at(w), :], pA[p][:, 0:VW].unsqueeze(1),
                                  ALU.add).then_inc(acc_done, 1)

            def step(b, p, i, first, last):
                if first and p == 0:
                    t, w = table_values(nc, ENG.DVE, k["GROUPS"], 2, [ET, NT])
                else:
                    wprev, _, _, t, w = table_values(nc, ENG.DVE, k["GROUPS"], 2 * b - 1, [NT, ET, NT, ET, NT])
                for q in range(2):
                    r, u = 2 * p + q, 2 * b + q
                    dve.wait_ge(kv_in[r], 32 * (i + 1))
                    dve.wait_ge(q_ready, u + 1)
                    dve.tensor_tensor(prod[:], kv[r][:, :, 0:D], pQ[q][:, :, 0:D], ALU.mult).then_inc(prod_ready, 1)
                    dve.wait_ge(prod_ready, u + 1)
                    dve.tensor_reduce(red[:].rearrange("p j h -> p (j h)"),
                                      prod[:].rearrange("p j (h c) -> p (j h) c", c=HD), AX.X,
                                      ALU.add).then_inc(red_ready, 1)
                    dve.wait_ge(red_ready, u + 1)
                    wait_if(dve, exp_ready, u - 1)
                    dve.scalar_tensor_tensor(out=score[q][:], in0=red[:], scalar=1.0 / math.sqrt(HD),
                                             in1=pQ[q][:, :, D:VW], op0=ALU.mult,
                                             op1=ALU.add).then_inc(score_ready, 1)
                    onehots(u + 2, (r + 2) % 4, q, t, w)
                    if not (first and r == 0):
                        weigh(u - 1, (r + 3) % 4, 1 - q)
                    if q == 1 and not (first and p == 0):
                        accumulate(b - 1, 1 - p, wprev)

            dve.sem_inc(acc_done, 1)
            t, w = table_values(nc, ENG.DVE, k["GROUPS"], 0, [ET, NT])
            onehots(0, 0, 0, t, w)
            onehots(1, 1, 1, t, w)
            n = pairs(dve)
            over_pairs(dve, n, step)
            weigh(4 * n - 1, 3, 1)
            w, = table_values(nc, ENG.DVE, k["GROUPS"], 4 * n - 1, [NT])
            accumulate(2 * n - 1, 1, w)

        @block.scalar
        def _(act):
            def copy_turned(u, q):
                act.wait_ge(turned, u + 1)
                wait_if(act, q_ready, u - 1)
                act.copy(oht[q][:], pT[q][:, 0:2, :]).then_inc(oht_ready, 1)

            def step(b, p, i, first, last):
                for q in range(2):
                    u = 2 * b + q
                    act.wait_ge(bias_ready, b + 1)
                    act.wait_ge(score_ready, u + 1)
                    wait_if(act, sums_ready, u - 1)
                    for j in range(2):
                        ins = act.activation(wv[q][:, j, D:VW], score[q][:, j, :], ACT.Exp,
                                             bias=bias[p][:, 2 * q + j:2 * q + j + 1])
                    ins.then_inc(exp_ready, 1)
                    copy_turned(u + 2, q)

            act.activation(score[0][:, 0, 0:1], k["EPSC"][:], ACT.Exp)
            copy_turned(0, 0)
            copy_turned(1, 1)
            over_pairs(act, pairs(act), step)

        @block.tensor
        def _(pe):
            def turn(u, r, q):
                pe.wait_ge(oh_ready, u + 1)
                wait_if(pe, oht_ready, u - 1)
                for j in range(2):
                    mm = pe.transpose(pT[q][:, j, :], oh[r][:, j, :], ident)
                mm.then_inc(turned, 1)

            def spread_q(u, q, w):
                pe.wait_ge(oht_ready, u + 1)
                wait_if(pe, score_ready, u - 1)
                for j in range(2):
                    mm = pe.matmul(pQ[q][:, j, 0:VW], oht[q][:, j, :], QX[:, at(w), :].squeeze(1), start=True,
                                   stop=True)
                mm.then_inc(q_ready, 1)

            def sum_up(u, r, q, b, p):
                pe.wait_ge(wv_ready, u + 1)
                if q == 0:
                    wait_if(pe, acc_done, b)
                for j in range(2):
                    mm = pe.matmul(pA[p][:, 0:VW], oh[r][:, j, :], wv[q][:, j, :], start=(q == 0 and j == 0),
                                   stop=(q == 1 and j == 1))
                mm.then_inc(sums_ready, 1)

            def step(b, p, i, first, last):
                w, _, wnext = table_values(nc, ENG.PE, k["GROUPS"], 2 * b + 1, [NT, ET, NT])
                for q in range(2):
                    r, u = 2 * p + q, 2 * b + q
                    spread_q(u + 1, 1 - q, w if q == 0 else wnext)
                    turn(u + 2, (r + 2) % 4, q)
                    if q == 1:
                        sum_up(u - 1, r - 1, 0, b, p)
                    elif not (first and p == 0):
                        sum_up(u - 1, (r + 3) % 4, 1, b - 1, 1 - p)

            w, = table_values(nc, ENG.PE, k["GROUPS"], 1, [NT])
            turn(0, 0, 0)
            turn(1, 1, 1)
            spread_q(0, 0, w)
            n = pairs(pe)
            over_pairs(pe, n, step)
            sum_up(4 * n - 1, 3, 1, 2 * n - 1, 1)


def attention_out(k):
    nc, a, C, X, ACC, R, ST = k["nc"], k["a"], k["C"], k["X"], k["ACC"], k["R"], k["ST"]
    ident = C[:, C_IDENT:C_IDENT + P]
    with ExitStack() as s:
        def sb(name, shape, dt=F32):
            return s.enter_context(nc.sbuf_tensor(name, shape, dt))

        def sem(name):
            return s.enter_context(nc.semaphore(name))

        w, bp = sb("proj_w", [P, KD, D]), sb("proj_b", [P, D])
        rec = sb("inv_weights", [P, NT, HEADS])
        o = [sb(f"attn_rows{b}", [P, D]) for b in range(2)]
        oT = [sb(f"attn_turned{b}", [P, KD, P]) for b in range(2)]
        part = [sb(f"proj_part{b}", [P, D]) for b in range(2)]
        pT = [s.enter_context(nc.psum_tensor(f"p_attn_turned{b}", [P, 4, P], F32)) for b in range(2)]
        pO = [s.enter_context(nc.psum_tensor(f"p_proj{b}", [P, 4 * P], F32)) for b in range(2)]
        w_in, step_done, o_ready, turned = sem("proj_w_in"), sem("rec_step"), sem("attn_ready"), sem("attn_turned")
        oT_ready, mm_done, part_ready, r_ready = (sem("attn_t_ready"), sem("proj_done"), sem("part_ready"),
                                                  sem("r_ready"))
        records = store_records(k, s, 1)
        block = s.enter_context(nc.Block())

        @block.gpsimd
        def _(pool):
            records(pool)

        @block.sync
        def _(sp):
            sp.dma_start(w[:], a["w_p"]).then_inc(w_in, 16)
            sp.dma_start(bp[:], a["rows0"][:, 0, :]).then_inc(w_in, 16)

        @block.vector
        def _(dve):
            link = Chain(dve, step_done)
            link(dve.tensor_scalar(rec[:], ACC[:, 0:NT, D:VW], 1e-37, None, ALU.max))
            link(dve.reciprocal(rec[:], rec[:]))

            def divide(n, b):
                wait_if(dve, turned, n - 1)
                dve.tensor_tensor(o[b][:].unsqueeze(1).rearrange("p o (h c) -> p o h c", c=HD),
                                  ACC[:, at(n), 0:D].rearrange("p o (h c) -> p o h c", c=HD),
                                  rec[:, at(n), :].unsqueeze(3).to_broadcast([P, 1, HEADS, HD]),
                                  ALU.mult).then_inc(o_ready, 1)

            def step(n, b, i, first, last):
                if not last:
                    divide(n + 1, 1 - b)
                dve.wait_ge(mm_done, n + 1)
                dve.scalar_tensor_tensor(out=part[b][:].unsqueeze(1), in0=X[:, at(n), :], scalar=column(k["RSTD"], n),
                                         in1=pO[b][:, 0:D].unsqueeze(1), op0=ALU.mult,
                                         op1=ALU.add).then_inc(part_ready, 1)
                dve.wait_ge(part_ready, n + 1)
                dve.scalar_tensor_tensor(out=R[:, at(n), :], in0=part[b][:].unsqueeze(1), scalar=column(k["NMR"], n),
                                         in1=bp[:].unsqueeze(1), op0=ALU.add, op1=ALU.add).then_inc(r_ready, 1)
                dve.wait_ge(r_ready, n + 1)
                dve.bn_stats(ST[:, at(n), :], R[:, at(n), :])

            divide(0, 0)
            dve.wait_ge(w_in, 32)
            over_tiles(dve, step)

        @block.scalar
        def _(act):
            def step(n, b, i, first, last):
                act.wait_ge(turned, n + 1)
                wait_if(act, mm_done, n - 1)
                act.copy(oT[b][:], pT[b][:, 0:KD, :]).then_inc(oT_ready, 1)

            over_tiles(act, step)

        @block.tensor
        def _(pe):
            def turn(n, b):
                pe.wait_ge(o_ready, n + 1)
                wait_if(pe, oT_ready, n - 1)
                for c in range(KD):
                    mm = pe.transpose(pT[b][:, c, :], o[b][:, c * P:(c + 1) * P], ident)
                mm.then_inc(turned, 1)

            def step(n, b, i, first, last):
                pe.wait_ge(oT_ready, n + 1)
                wait_if(pe, part_ready, n - 1)
                for c in range(KD):
                    mm = pe.matmul(pO[b][:, 0:D], oT[b][:, c, :], w[:, c, :], start=(c == 0), stop=(c == KD - 1))
                mm.then_inc(mm_done, 1)
                if not last:
                    turn(n + 1, 1 - b)

            turn(0, 0)
            pe.wait_ge(w_in, 32)
            over_tiles(pe, step)


def mlp_blocks(k, name, hidden, experts, affine):
    nc, a, C, R, ST = k["nc"], k["a"], k["C"], k["R"], k["ST"]
    ident = C[:, C_IDENT:C_IDENT + P]
    HC, BR = hidden // P, BT // P
    W1, W2 = 0, KD * hidden
    B1 = W2 + HC * D
    G, B, B2 = B1 + HC, B1 + HC + KD, B1 + HC + 2 * KD
    SIZE = B2 + D
    NPK = 2 if experts else 1
    NH = 3
    BLOCKS = -(-NT // BR)
    with ExitStack() as s:
        def sb(what, shape, dt=F32):
            return s.enter_context(nc.sbuf_tensor(name + what, shape, dt))

        def sem(what):
            return s.enter_context(nc.semaphore(name + what))

        pack = [sb(f"_weights{b}", [P, SIZE]) for b in range(NPK)]
        rows = [sb(f"_rows{b}", [P, BR, D]) for b in range(2)]
        tT = [sb(f"_turned{b}", [P, KD, BT]) for b in range(2)]
        hid = [sb(f"_hidden{b}", [P, HC, BT]) for b in range(2)]
        y = [sb(f"_y{b}", [P, BR, D]) for b in range(2)]
        gb = None if experts else sb("_affine_rows", [P, 2, D])
        scale = [sb(f"_scale{b}", [P, 2 * KD]) for b in range(2)]
        pT = s.enter_context(nc.psum_tensor(name + "p_turned", [P, KD, BT], F32))
        pH = [s.enter_context(nc.psum_tensor(f"{name}p_hidden{c}", [P, 4 * P], F32)) for c in range(NH)]
        pY = [[s.enter_context(nc.psum_tensor(f"{name}p_y{b}{r}", [P, 4 * P], F32)) for r in range(BR)]
              for b in range(2)]
        pack_in, rows_in = [sem(f"_pack_in{b}") for b in range(2)], [sem(f"_rows_in{b}") for b in range(2)]
        rows_ready, turned, tT_ready = sem("_rows_ready"), sem("_turned_done"), sem("_tt_ready")
        hidden_done, gelu_done, y_done = sem("_hidden_done"), sem("_gelu_done"), sem("_y_done")
        y_ready, y_out, fin = sem("_y_ready"), [sem(f"_y_out{b}") for b in range(2)], sem("_finish")
        scale_in = [sem(f"_scale_in{b}") for b in range(2)]
        gb_in, norm, scaled = sem("_gb_in"), sem("_norm"), sem("_scaled")
        tally = sem("_tally")
        part = {"ffn": 2, "experts0": 3}.get(name)
        records = part and store_records(k, s, part)
        block = s.enter_context(nc.Block())
        slots_in = a["slots_in"].rearrange("(j r p) d -> j p r d", p=P, r=BR)
        slots_out = a["slots_out"].rearrange("(j r p) d -> j p r d", p=P, r=BR)

        def over_blocks(eng, step):
            if experts:
                n = eng.value_load(k["EPAIRS"][0:1, 0:1], min_val=2, max_val=NBLK // 2)
                over_pairs(eng, n, step)
                return n
            over_tiles(eng, step, BLOCKS)

        @block.sync
        def _(sp):
            if not experts:
                sp.dma_start(gb[:], a["rows0"][:, 1:3, :]).then_inc(gb_in, 16)
                sp.dma_start(pack[0][:], a["ffn"][0]).then_inc(pack_in[0], 16)
                return

            def load_rows(j, b, used):
                wait_if(sp, turned, used)
                sp.sem_inc(tally, 1)
                sp.dma_start(rows[b][:], slots_in[at(j)].squeeze(0)).then_inc(rows_in[b], 16)
                e, = table_values(nc, mybir.EngineType.SP, k["BLOCKEXP"], j, [NEXP - 1])
                if affine:
                    wait_if(sp, tT_ready, used)
                    sp.sem_inc(tally, 1)
                    sp.dma_start(scale[b][:], a[name][at(e), :, G:B2].squeeze(0)).then_inc(scale_in[b], 16)
                return e

            def store(j, b, ready):
                sp.wait_ge(y_ready, ready)
                sp.sem_inc(tally, 1)
                sp.dma_start(slots_out[at(j)].squeeze(0), y[b][:]).then_inc(y_out[b], 16)

            def step(j, b, i, first, last):
                e = load_rows(j, b, j - 1)
                wait_if(sp, y_done, j - 1)
                wait_if(sp, y_ready, j - 1)
                sp.sem_inc(tally, 1)
                sp.dma_start(pack[b][:], a[name][at(e)].squeeze(0)).then_inc(pack_in[b], 16)
                if not first:
                    store(j - 2, b, j - 1)

            n = over_blocks(sp, step)
            load_rows(2 * n, 0, 2 * n)
            store(2 * n - 2, 0, 2 * n)
            store(2 * n - 1, 1, 2 * n)
            for landed, count in [(y_out[0], n), (y_out[1], n), (rows_in[0], n + 1)] + (
                    [(scale_in[0], n + 1)] if affine else []):
                sp.wait_ge(landed, 16 * count)
                sp.sem_inc(tally, 1)

        if records:
            @block.gpsimd
            def _(pool):
                records(pool)

        @block.vector
        def _(dve):
            def prepare(j, b):
                if not experts:
                    wait_if(dve, fin, j - 1)
                    for r in range(BR):
                        ins = normalise(dve, k, rows[b][:, r, :].unsqueeze(1), R[:, at(BR * j + r), :], BR * j + r)
                    ins.then_inc(norm, 1)
                    dve.wait_ge(norm, j + 1)
                    wide = [P, BR, D]
                    dve.tensor_tensor(rows[b][:], rows[b][:], gb[:, 0, :].unsqueeze(1).to_broadcast(wide),
                                      ALU.mult).then_inc(scaled, 1)
                    dve.wait_ge(scaled, j + 1)
                    dve.tensor_tensor(rows[b][:], rows[b][:], gb[:, 1, :].unsqueeze(1).to_broadcast(wide),
                                      ALU.add).then_inc(rows_ready, 1)

            def copy_turned(j, b):
                dve.wait_ge(turned, j + 1)
                wait_if(dve, hidden_done, HC * (j - 1))
                if affine:
                    dve.wait_ge(scale_in[b], 16 * (half[0] + 1))
                    for c in range(KD):
                        ins = dve.tensor_scalar(tT[b][:, c, :], pT[:, c, :], scale[b][:, c:c + 1],
                                                scale[b][:, KD + c:KD + c + 1], ALU.mult, ALU.add)
                else:
                    ins = dve.tensor_copy(tT[b][:], pT[:])
                ins.then_inc(tT_ready, 1)

            def step(j, b, i, first, last):
                if not last:
                    prepare(j + 1, 1 - b)
                    half[0] = i + b
                    copy_turned(j + 1, 1 - b)
                dve.wait_ge(y_done, j + 1)
                bias2 = pack[b % NPK][:, B2:B2 + D]
                if experts:
                    dve.wait_ge(pack_in[b], 16 * (i + 1))
                    wait_if(dve, y_out[b], 16 * i if not first else 0)
                    for r in range(BR):
                        ins = dve.tensor_tensor(y[b][:, r, :], pY[b][r][:, 0:D], bias2, ALU.add)
                    ins.then_inc(y_ready, 1)
                else:
                    for r in range(BR):
                        ins = dve.tensor_tensor(y[b][:, r, :], pY[b][r][:, 0:D], rows[b][:, r, :], ALU.add)
                    ins.then_inc(y_ready, 1)
                    dve.wait_ge(y_ready, j + 1)
                    dve.tensor_tensor(R[:, at(BR * j, BR), :], y[b][:], bias2.unsqueeze(1).to_broadcast([P, BR, D]),
                                      ALU.add).then_inc(fin, 1)
                    dve.wait_ge(fin, j + 1)
                    for r in range(BR):
                        dve.bn_stats(ST[:, at(BR * j + r), :], R[:, at(BR * j + r), :])

            half = [0]
            if not experts:
                dve.wait_ge(gb_in, 16)
            prepare(0, 0)
            copy_turned(0, 0)
            if not experts:
                dve.wait_ge(pack_in[0], 16)
            over_blocks(dve, step)

        @block.scalar
        def _(act):
            def step(j, b, i, first, last):
                if not first:
                    act.wait_ge(y_done, j - 1)
                for h in range(HC):
                    c = h % NH
                    act.wait_ge(hidden_done, HC * j + h + 1)
                    act.activation(hid[b][:, h, :], pH[c][:, 0:BT], ACT.Gelu,
                                   bias=pack[b % NPK][:, B1 + h:B1 + h + 1]).then_inc(gelu_done, 1)

            act.activation(y[0][:, 0, 0:1], k["EPSC"][:], ACT.Gelu)
            over_blocks(act, step)

        @block.tensor
        def _(pe):
            def turn(j, b):
                if experts:
                    pe.wait_ge(rows_in[b], 16 * (half[0] + 1))
                else:
                    pe.wait_ge(rows_ready, j + 1)
                wait_if(pe, tT_ready, j)
                for r in range(BR):
                    for c in range(KD):
                        mm = pe.transpose(pT[:, c, r * P:(r + 1) * P], rows[b][:, r, c * P:(c + 1) * P], ident)
                mm.then_inc(turned, 1)

            def step(j, b, i, first, last):
                w = pack[b % NPK]
                if experts:
                    pe.wait_ge(pack_in[b], 16 * (i + 1))
                pe.wait_ge(tT_ready, j + 1)
                for h in range(HC):
                    c = h % NH
                    wait_if(pe, gelu_done, HC * j + h + 1 - (NH if h >= NH else 0) - (0 if h >= NH else h + 1))
                    for d in range(KD):
                        lo = W1 + d * hidden + h * P
                        mm = pe.matmul(pH[c][:, 0:BT], w[:, lo:lo + P], tT[b][:, d, :], start=(d == 0),
                                       stop=(d == KD - 1))
                    mm.then_inc(hidden_done, 1)
                if not last:
                    half[0] = i + b
                    turn(j + 1, 1 - b)
                wait_if(pe, y_ready, j - 1)
                for h in range(HC):
                    pe.wait_ge(gelu_done, HC * j + h + 1)
                    for r in range(BR):
                        mm = pe.matmul(pY[b][r][:, 0:D], hid[b][:, h, r * P:(r + 1) * P],
                                       w[:, W2 + h * D:W2 + (h + 1) * D], start=(h == 0), stop=(h == HC - 1))
                mm.then_inc(y_done, 1)

            half = [0]
            turn(0, 0)
            if not experts:
                pe.wait_ge(pack_in[0], 16)
            over_blocks(pe, step)


def ffn(k):
    nc, a, X, R, ST = k["nc"], k["a"], k["X"], k["R"], k["ST"]
    finish_ln(k, "1")
    mlp_blocks(k, "ffn", FFN, False, False)
    finish_ln(k, "2")
    with ExitStack() as s:
        gb = s.enter_context(nc.sbuf_tensor("ln2_rows", [P, 2, D], F32))
        gb_in, normed = s.enter_context(nc.semaphore("ln2_rows_in")), s.enter_context(nc.semaphore("normed"))
        step_done, x_ready = s.enter_context(nc.semaphore("ffn_step")), s.enter_context(nc.semaphore("ffn_x_ready"))
        block = s.enter_context(nc.Block())

        @block.sync
        def _(sp):
            sp.dma_start(gb[:], a["rows0"][:, 3:5, :]).then_inc(gb_in, 16)

        @block.vector
        def _(dve):
            wide = [P, NT, D]
            for n in range(NT):
                ins = normalise(dve, k, R[:, n, :], R[:, n, :], n)
            ins.then_inc(normed, 1)
            link = Chain(dve, step_done)
            dve.wait_ge(gb_in, 16)
            dve.wait_ge(normed, 1)
            link(dve.tensor_tensor(R[:, 0:NT, :], R[:, 0:NT, :], gb[:, 0, :].unsqueeze(1).to_broadcast(wide),
                                   ALU.mult))
            link(dve.tensor_tensor(R[:, 0:NT, :], R[:, 0:NT, :], gb[:, 1, :].unsqueeze(1).to_broadcast(wide),
                                   ALU.add))
            dve.tensor_tensor(X[:], X[:], R[:, 0:NT, :], ALU.add).then_inc(x_ready, 1)
            dve.wait_ge(x_ready, 1)
            with dve.Fori(0, NT) as n:
                dve.bn_stats(ST[:, at(n), :], X[:, at(n), :])
    finish_ln(k, "3")


def moe_route(k, layer):
    nc, a, C, X = k["nc"], k["a"], k["C"], k["X"]
    ident, tri, ones = (C[:, c:c + P] for c in (C_IDENT, C_TRI, C_ONES))
    byexp, bytok = [P, NT, NEXP], [P, NEXP, NT]
    tag = f"route{layer}_"
    with ExitStack() as s:
        def sb(name, shape, dt=F32):
            return s.enter_context(nc.sbuf_tensor(tag + name, shape, dt))

        def sem(name):
            return s.enter_context(nc.semaphore(tag + name))

        router, rbias = sb("w", [P, KD, NEXP]), sb("b", [P, NT * NEXP])
        tok = [sb(f"tok{b}", [P, D]) for b in range(2)]
        tT = [sb(f"tok_turned{b}", [P, KD, P]) for b in range(2)]
        lg, prob, cand, hit1, hit2 = (sb(n, byexp) for n in ("logits", "prob", "cand", "hit1", "hit2"))
        top = sb("top", [P, NT])
        m1, m2, rank, wsum = (sb(n, [P, NT]) for n in ("first", "second", "rank", "wsum"))
        member, cum, slot = sb("member", bytok), sb("running", bytok), sb("slot", byexp)
        ends, cnt, pre, adj = sb("ends", [P, NEXP + 1]), sb("cnt", [P, NEXP]), sb("pre", [P, NEXP]), sb("adj", [P, NEXP])
        blki, blk, binc, nought = sb("blk_i", [P, NEXP], I32), sb("blk", [P, NEXP]), sb("blk_inc", [P, NEXP]), sb("zero", [P, NEXP])
        where = sb("where", [P, NT, TOPK])
        past, expert, pairs = sb("past", [1, NBLK + 2, NEXP - 1]), sb("expert", [1, NBLK + 2]), sb("pairs", [1, 1], I32)
        pT = [s.enter_context(nc.psum_tensor(f"{tag}p_turned{b}", [P, 4, P], F32)) for b in range(2)]
        pL = [s.enter_context(nc.psum_tensor(f"{tag}p_logits{b}", [P, 4 * P], F32)) for b in range(2)]
        pPre = s.enter_context(nc.psum_tensor(tag + "p_prefix", [P, NEXP], F32))
        pTot = s.enter_context(nc.psum_tensor(tag + "p_total", [P, NEXP], F32))
        w_in, tok_ready, turned, tT_ready = sem("w_in"), sem("tok_ready"), sem("turned"), sem("tt_ready")
        mm_done, lg_ready, step_done = sem("mm_done"), sem("lg_ready"), sem("step")
        diff_ready, exp_ready, cnt_ready, sums_ready = (sem("diff_ready"), sem("exp_ready"), sem("cnt_ready"),
                                                        sem("sums_ready"))
        block = s.enter_context(nc.Block())

        @block.sync
        def _(sp):
            sp.dma_start(router[:], a[f"router{layer}"]).then_inc(w_in, 16)
            if layer == 1:
                sp.dma_start(rbias[:], a["rbias1"]).then_inc(w_in, 16)

        @block.vector
        def _(dve):
            def token(n, b):
                wait_if(dve, turned, n - 1)
                normalise(dve, k, tok[b][:].unsqueeze(1), X[:, at(n), :], n).then_inc(tok_ready, 1)

            def step(n, b, i, first, last):
                if not last:
                    token(n + 1, 1 - b)
                dve.wait_ge(mm_done, n + 1)
                dve.tensor_copy(lg[:, at(n), :], pL[b][:, 0:NEXP].unsqueeze(1)).then_inc(lg_ready, 1)

            def wide(v):
                return v.unsqueeze(2).to_broadcast(byexp)

            dve.memset(nought[:], 0.0)
            dve.memset(ends[:], 0.0)
            token(0, 0)
            over_tiles(dve, step)
            link = Chain(dve, step_done)
            dve.wait_ge(lg_ready, NT)
            if layer == 1:
                dve.wait_ge(w_in, 32)
                link(dve.tensor_tensor(lg[:].rearrange("p t e -> p (t e)"), lg[:].rearrange("p t e -> p (t e)"),
                                       rbias[:], ALU.add))
                link(dve.tensor_tensor(k["NMR2"][:], k["RSTD"][:], k["RSTD"][:], ALU.mult))
                link(dve.tensor_tensor(k["RSTD2"][:], k["NMR2"][:], k["VAR"][:], ALU.mult))
            link(dve.tensor_reduce(top[:], lg[:], AX.X, ALU.max))
            dve.tensor_tensor(lg[:], lg[:], wide(top[:]), ALU.subtract).then_inc(diff_ready, 1)
            dve.wait_ge(exp_ready, 1)
            link(dve.tensor_reduce(wsum[:], prob[:], AX.X, ALU.add))
            link(dve.reciprocal(wsum[:], wsum[:]))
            link(dve.tensor_tensor(prob[:], prob[:], wide(wsum[:]), ALU.mult))
            ranks = C[:, C_RANK:C_RANK + NT * NEXP].rearrange("p (t e) -> p t e", e=NEXP)
            for m, hit in ((m1, hit1), (m2, hit2)):
                link(dve.tensor_reduce(m[:], prob[:], AX.X, ALU.max))
                link(dve.tensor_tensor(cand[:], prob[:], wide(m[:]), ALU.is_equal))
                link(dve.tensor_tensor(cand[:], cand[:], ranks, ALU.mult))
                link(dve.tensor_reduce(rank[:], cand[:], AX.X, ALU.max))
                link(dve.tensor_tensor(hit[:], ranks, wide(rank[:]), ALU.is_equal))
                if hit is hit1:
                    link(dve.scalar_tensor_tensor(out=prob[:], in0=hit[:], scalar=-2.0, in1=prob[:], op0=ALU.mult,
                                                  op1=ALU.add))
            link(dve.tensor_tensor(wsum[:], m1[:], m2[:], ALU.add))
            link(dve.tensor_scalar(wsum[:], wsum[:], 1e-12, None, ALU.max))
            link(dve.reciprocal(wsum[:], wsum[:]))
            link(dve.tensor_tensor(k["W12"][:, :, 0], m1[:], wsum[:], ALU.mult))
            link(dve.tensor_tensor(k["W12"][:, :, 1], m2[:], wsum[:], ALU.mult))
            for hit in (hit1, hit2):
                link(dve.tensor_tensor(hit[:], hit[:], wide(C[:, C_VALID:C_VALID + NT]), ALU.mult))
            link(dve.tensor_tensor(member[:].rearrange("p e t -> p t e"), hit1[:], hit2[:], ALU.add))
            link(dve.tensor_tensor_scan(cum[:].rearrange("p e t -> p (e t)"), member[:].rearrange("p e t -> p (e t)"),
                                        nought[:, 0:1].to_broadcast([P, NEXP * NT]), 0.0, ALU.add, ALU.add))
            link(dve.tensor_copy(ends[:, 1:NEXP + 1], cum[:, :, NT - 1]))
            dve.tensor_tensor(cnt[:], ends[:, 1:NEXP + 1], ends[:, 0:NEXP], ALU.subtract).then_inc(cnt_ready, 1)
            dve.wait_ge(sums_ready, 1)
            link(dve.tensor_copy(pre[:], pPre[:]))
            link(dve.tensor_scalar(blki[:], pTot[:], float(BT - 1), None, ALU.add))
            link(dve.tensor_scalar(blki[:], blki[:], BT.bit_length() - 1, None, ALU.arith_shift_right))
            link(dve.tensor_copy(blk[:], blki[:]))
            link(dve.tensor_tensor_scan(binc[:], blk[:], nought[:], 0.0, ALU.add, ALU.add))
            link(dve.tensor_tensor(adj[:], binc[:], blk[:], ALU.subtract))
            link(dve.scalar_tensor_tensor(out=adj[:], in0=adj[:], scalar=float(BT), in1=pre[:], op0=ALU.mult,
                                          op1=ALU.add))
            link(dve.scalar_tensor_tensor(out=adj[:], in0=adj[:], scalar=-1.0, in1=ends[:, 0:NEXP], op0=ALU.add,
                                          op1=ALU.subtract))
            link(dve.tensor_tensor(slot[:], cum[:].rearrange("p e t -> p t e"),
                                   adj[:].unsqueeze(1).to_broadcast(byexp), ALU.add))
            for j, hit in ((0, hit1), (1, hit2)):
                link(dve.tensor_tensor(hit[:], hit[:], slot[:], ALU.mult))
                link(dve.tensor_reduce(where[:, :, j], hit[:], AX.X, ALU.add))
            link(dve.tensor_tensor(k["SLOT"][:], where[:],
                                   C[:, C_TRASH:C_TRASH + NT * TOPK].rearrange("p (t j) -> p t j", j=TOPK), ALU.add))
            shape = [1, NBLK + 2, NEXP - 1]
            link(dve.tensor_tensor(past[:], binc[0:1, 0:NEXP - 1].unsqueeze(1).to_broadcast(shape),
                                   C[0:1, C_SGRP:C_SGRP + NBLK + 2].unsqueeze(2).to_broadcast(shape), ALU.is_le))
            link(dve.tensor_reduce(expert[:], past[:], AX.X, ALU.add))
            link(dve.tensor_copy(k["BLOCKEXP"][:], expert[:]))
            link(dve.tensor_scalar(pairs[:], binc[0:1, NEXP - 1:NEXP], 1.0, None, ALU.add))
            link(dve.tensor_scalar(k["EPAIRS"][:], pairs[:], 1, None, ALU.arith_shift_right))

        @block.scalar
        def _(act):
            def step(n, b, i, first, last):
                act.wait_ge(turned, n + 1)
                wait_if(act, mm_done, n - 1)
                act.copy(tT[b][:], pT[b][:, 0:KD, :]).then_inc(tT_ready, 1)

            over_tiles(act, step)
            act.wait_ge(diff_ready, 1)
            act.activation(prob[:], lg[:], ACT.Exp).then_inc(exp_ready, 1)

        @block.tensor
        def _(pe):
            def turn(n, b):
                pe.wait_ge(tok_ready, n + 1)
                wait_if(pe, tT_ready, n - 1)
                for c in range(KD):
                    mm = pe.transpose(pT[b][:, c, :], tok[b][:, c * P:(c + 1) * P], ident)
                mm.then_inc(turned, 1)

            def step(n, b, i, first, last):
                if not last:
                    turn(n + 1, 1 - b)
                pe.wait_ge(tT_ready, n + 1)
                wait_if(pe, lg_ready, n - 1)
                for c in range(KD):
                    mm = pe.matmul(pL[b][:, 0:NEXP], tT[b][:, c, :], router[:, c, :], start=(c == 0),
                                   stop=(c == KD - 1))
                mm.then_inc(mm_done, 1)

            turn(0, 0)
            pe.wait_ge(w_in, 16 * (1 + layer))
            over_tiles(pe, step)
            pe.wait_ge(cnt_ready, 1)
            pe.matmul(pPre[:], tri, cnt[:], start=True, stop=True)
            pe.matmul(pTot[:], ones, cnt[:], start=True, stop=True).then_inc(sums_ready, 1)


def second_ln(k):
    nc = k["nc"]
    with ExitStack() as s:
        std = s.enter_context(nc.sbuf_tensor("std2", [P, NT + 1], F32))
        std_ready, step = s.enter_context(nc.semaphore("std2_ready")), s.enter_context(nc.semaphore("ln2_step"))
        block = s.enter_context(nc.Block())

        @block.scalar
        def _(act):
            act.activation(std[:], k["RSTD2"][:], ACT.Sqrt, bias=k["EPSC"][:, 0:1]).then_inc(std_ready, 1)

        @block.vector
        def _(dve):
            link = Chain(dve, step)
            dve.wait_ge(std_ready, 1)
            link(dve.reciprocal(std[:], std[:]))
            link(dve.tensor_tensor(k["RSTD2"][:], k["RSTD"][:], std[:], ALU.mult))
            link(dve.tensor_tensor(k["NMR2"][:], k["NMR"][:], std[:], ALU.mult))


def moe_scatter(k, layer):
    nc, a, X = k["nc"], k["a"], k["X"]
    rstd, nmr = (k["RSTD2"], k["NMR2"]) if layer else (k["RSTD"], k["NMR"])
    tag = f"scatter{layer}_"
    with ExitStack() as s:
        def sem(name):
            return s.enter_context(nc.semaphore(tag + name))

        rows = [s.enter_context(nc.sbuf_tensor(f"{tag}rows{b}", [P, D], F32)) for b in range(2)]
        idx = [s.enter_context(nc.sbuf_tensor(f"{tag}idx{b}", [P, TOPK], I32)) for b in range(2)]
        rows_ready, idx_ready, tally = sem("rows_ready"), sem("idx_ready"), sem("tally")
        stored = [k[f"scattered{layer}_{b}"] for b in range(2)]
        block = s.enter_context(nc.Block())

        @block.vector
        def _(dve):
            def step(n, b, i, first, last):
                if not first:
                    dve.wait_ge(stored[b], 32 * i)
                dve.tensor_scalar(rows[b][:].unsqueeze(1), X[:, at(n), :], column(rstd, n), column(nmr, n), ALU.mult,
                                  ALU.add).then_inc(rows_ready, 1)

            over_tiles(dve, step)

        @block.gpsimd
        def _(pool):
            def step(n, b, i, first, last):
                if not first:
                    pool.wait_ge(stored[b], 32 * i)
                pool.wait_ge(rows_ready, n + 1)
                pool.sem_inc(tally, 1)
                pool.tensor_copy(idx[b][:].unsqueeze(1), k["SLOT"][:, at(n), :]).then_inc(idx_ready, 1)
                pool.wait_ge(idx_ready, n + 1)
                pool.sem_inc(tally, 1)
                for j in range(TOPK):
                    pool.indirect_dma_start(a["slots_in"], bass.IndirectOffsetOnAxis(ap=idx[b][:, j:j + 1], axis=0),
                                            rows[b][:], None).then_inc(stored[b], 16)

            over_tiles(pool, step)
            pool.wait_ge(stored[0], 32 * ((NT + 1) // 2))
            pool.wait_ge(stored[1], 32 * (NT // 2))


def moe_combine(k, layer):
    nc, a, X, ST = k["nc"], k["a"], k["X"], k["ST"]
    tag = f"combine{layer}_"
    with ExitStack() as s:
        def sem(name):
            return s.enter_context(nc.semaphore(tag + name))

        y = [s.enter_context(nc.sbuf_tensor(f"{tag}y{b}", [P, TOPK, D], F32)) for b in range(2)]
        idx = [s.enter_context(nc.sbuf_tensor(f"{tag}idx{b}", [P, TOPK], I32)) for b in range(2)]
        sums = [s.enter_context(nc.sbuf_tensor(f"{tag}sum{b}", [P, TOPK, D], F32)) for b in range(2)]
        rstd1 = s.enter_context(nc.sbuf_tensor(tag + "rstd1", [P, NT + 1], F32))
        idx_ready, tally, r_ready = sem("idx_ready"), sem("tally"), sem("r_ready")
        first_done, second_done, x_ready = sem("first_done"), sem("second_done"), sem("x_ready")
        y_in, stored = [k[f"y_in{layer}_{b}"] for b in range(2)], sem("stored")
        block = s.enter_context(nc.Block())

        @block.gpsimd
        def _(pool):
            def step(n, b, i, first, last):
                wait_if(pool, second_done, n - 1)
                pool.sem_inc(tally, 1)
                pool.tensor_copy(idx[b][:].unsqueeze(1), k["CSLOT"][:, at(n), :]).then_inc(idx_ready, 1)
                pool.wait_ge(idx_ready, n + 1)
                pool.sem_inc(tally, 1)
                for j in range(TOPK):
                    pool.indirect_dma_start(y[b][:, j, :], None, a["slots_out"], bass.IndirectOffsetOnAxis(
                        ap=idx[b][:, j:j + 1], axis=0)).then_inc(y_in[b], 16)

            pool.wait_ge(r_ready, 2)
            over_tiles(pool, step)

        @block.vector
        def _(dve):
            def step(n, b, i, first, last):
                dve.wait_ge(y_in[b], 32 * (i + 1))
                w = [k["W12"][:, at(n), j] for j in range(TOPK)]
                dve.scalar_tensor_tensor(out=sums[b][:, 0, :], in0=y[b][:, 0, :], scalar=w[0],
                                         in1=X[:, at(n), :].squeeze(1), op0=ALU.mult, op1=ALU.add).then_inc(first_done, 1)
                dve.wait_ge(first_done, n + 1)
                out = X[:, at(n), :] if layer else sums[b][:, 1:2, :]
                dve.scalar_tensor_tensor(out=out, in0=y[b][:, 1:2, :], scalar=w[1], in1=sums[b][:, 0:1, :],
                                         op0=ALU.mult, op1=ALU.add).then_inc(second_done, 1)
                if layer == 0:
                    dve.wait_ge(second_done, n + 1)
                    dve.scalar_tensor_tensor(out=sums[b][:, 0:1, :], in0=X[:, at(n), :], scalar=column(k["RSTD"], n),
                                             in1=sums[b][:, 1:2, :], op0=ALU.mult, op1=ALU.add).then_inc(x_ready, 1)
                    dve.wait_ge(x_ready, 2 * n + 1)
                    dve.tensor_scalar(X[:, at(n), :], sums[b][:, 0:1, :], column(k["NMR"], n), None,
                                      ALU.add).then_inc(x_ready, 1)
                    dve.wait_ge(x_ready, 2 * n + 2)
                    dve.bn_stats(ST[:, at(n), :], X[:, at(n), :])

            trash = C_TRASH
            dve.tensor_scalar(k["CSLOT"][:], k["SLOT"][:], float(NSLOT), None, ALU.is_lt).then_inc(r_ready, 1)
            dve.wait_ge(r_ready, 1)
            dve.tensor_tensor(k["CSLOT"][:], k["CSLOT"][:], k["SLOT"][:], ALU.mult).then_inc(r_ready, 1)
            over_tiles(dve, step)

        if layer:
            @block.sync
            def _(sp):
                whole = N // P
                for lo in range(0, whole, 6):
                    hi = min(lo + 6, whole)
                    sp.wait_ge(second_done, hi)
                    sp.dma_start(a["out"][lo * P:hi * P, :].rearrange("(t p) d -> p t d", p=P),
                                 X[:, lo:hi, :]).then_inc(stored, 16)
                sp.wait_ge(second_done, NT)
                sp.dma_start(a["out"][whole * P:N, :], X[0:N - whole * P, NT - 1, :]).then_inc(stored, 16)
                sp.wait_ge(stored, 16 * (-(-whole // 6) + 1))


def moe(k, layer):
    nc = k["nc"]
    with ExitStack() as s:
        for name, shape, dt in (("W12", [P, NT, TOPK], F32), ("SLOT", [P, NT, TOPK], I32),
                                ("CSLOT", [P, NT, TOPK], I32), ("BLOCKEXP", [1, NBLK + 2], I32), ("EPAIRS", [1, 1], I32),
                                ("RSTD2", [P, NT + 1], F32), ("NMR2", [P, NT + 1], F32)):
            k[name] = s.enter_context(nc.sbuf_tensor(f"{name}_{layer}", shape, dt))
        moe_route(k, layer)
        if layer:
            second_ln(k)
        moe_scatter(k, layer)
        mlp_blocks(k, f"experts{layer}", (D, FFN)[layer], True, layer == 1)
        moe_combine(k, layer)
        if layer == 0:
            finish_ln(k, "4")


RB = 8
RBATCH = (18, 8, 16, 10)


def store_records(k, stack, part):
    nc, first = k["nc"], sum(RBATCH[:part])
    tag = f"records{part}_"
    idx = [stack.enter_context(nc.sbuf_tensor(f"{tag}idx{b}", [P, RB], I32)) for b in range(2)]
    rec = [stack.enter_context(nc.sbuf_tensor(f"{tag}rec{b}", [P, RB, 2], I32)) for b in range(2)]
    stored = [k[f"{tag}stored{b}"] for b in range(2)]
    copied, tally = stack.enter_context(nc.semaphore(tag + "copied")), stack.enter_context(nc.semaphore(tag + "tally"))

    def program(pool):
        def step(j, b, i, fresh, last):
            lo = RB * first + RB * j
            if not fresh:
                pool.wait_ge(stored[b], 16 * RB * i)
                pool.sem_inc(tally, 1)
            pool.tensor_copy(idx[b][:], k["SADDR"][:, at(lo, RB)]).then_inc(copied, 1)
            pool.tensor_copy(rec[b][:], k["EDGES"][:, at(lo, RB), :]).then_inc(copied, 1)
            pool.wait_ge(copied, 2 * j + 2)
            pool.sem_inc(tally, 1)
            for t in range(RB):
                pool.indirect_dma_start(k["a"]["records"], bass.IndirectOffsetOnAxis(ap=idx[b][:, t:t + 1], axis=0),
                                        rec[b][:, t, :], None).then_inc(stored[b], 16)

        over_pairs(pool, RBATCH[part] // 2, step)
        for b in range(2):
            pool.wait_ge(stored[b], 16 * RB * (RBATCH[part] // 2))

    return program


def gnn_rows(k):
    nc, a, X, R = k["nc"], k["a"], k["X"], k["R"]
    with ExitStack() as s:
        normed, stored = s.enter_context(nc.semaphore("gnn_normed")), s.enter_context(nc.semaphore("gnn_rows_stored"))
        block = s.enter_context(nc.Block())
        xg = a["xg0"].rearrange("(t p) d -> p t d", p=P)

        @block.vector
        def _(dve):
            with dve.Fori(0, NT) as n:
                normalise(dve, k, R[:, at(n), :], X[:, at(n), :], n).then_inc(normed, 1)

        @block.sync
        def _(sp):
            for lo in range(0, NT, 5):
                sp.wait_ge(normed, lo + 5)
                sp.dma_start(xg[:, lo:lo + 5, :], R[:, lo:lo + 5, :]).then_inc(stored, 16)
            sp.wait_ge(stored, 16 * (NT // 5))


def gnn_edges(k, layer):
    nc, a, C, AGG = k["nc"], k["a"], k["C"], k["AGG"]
    iota = C[:, C_IOTA:C_IOTA + P]
    TILES = SBODY * SGT
    width = D + 1 if layer == 0 else D
    tag = f"agg{layer}_"
    with ExitStack() as s:
        def sb(name, shape, dt=F32):
            return s.enter_context(nc.sbuf_tensor(tag + name, shape, dt))

        def sem(name):
            return s.enter_context(nc.semaphore(tag + name))

        recs = sb("records", [P, STILES, 2], I32)
        keys = sb("keys", [P, STILES])
        idx = [sb(f"idx{g}", [P, SGT], I32) for g in range(SBODY)]
        rows = [sb(f"rows{r}", [P, D + 1]) for r in range(TILES)]
        oh = [sb(f"onehot{r}", [P, P]) for r in range(4)]
        pA = [s.enter_context(nc.psum_tensor(f"{tag}p{g}", [P, 4 * P], F32)) for g in range(SBODY)]
        recs_in, keys_ready, idx_ready, tally = sem("records_in"), sem("keys_ready"), sem("idx_ready"), sem("tally")
        rows_in = [k[f"agg{layer}_rows_in{r}"] for r in range(TILES)]
        ones_ready, oh_ready, mm_done, acc_done = sem("ones_ready"), sem("oh_ready"), sem("mm_done"), sem("acc_done")
        zero_ready = sem("zero_ready")
        block = s.enter_context(nc.Block())

        def turns(eng):
            return eng.value_load(k["STURNS"][0:1, 0:1], min_val=2, max_val=SG // SBODY)

        def over_turns(eng, step):
            step(0, True)
            n = turns(eng)
            with eng.Fori(1, n) as i:
                step(i, False)
            return n

        @block.sync
        def _(sp):
            sp.dma_start(recs[:], a["records"][0:STILES * P, :].rearrange("(p t) two -> p t two",
                                                                          p=P)).then_inc(recs_in, 16)

        @block.gpsimd
        def _(pool):
            def step(i, first):
                for g in range(SBODY):
                    if not first:
                        pool.wait_ge(mm_done, TILES * i - TILES + SGT * g + SGT)
                        pool.sem_inc(tally, 1)
                    pool.tensor_copy(idx[g][:], recs[:, at(TILES * i + SGT * g, SGT), 0]).then_inc(idx_ready, 1)
                    pool.wait_ge(idx_ready, SBODY * i + g + 1)
                    pool.sem_inc(tally, 1)
                    for j in range(SGT):
                        r = SGT * g + j
                        pool.indirect_dma_start(rows[r][:, 0:D], None, a[f"xg{layer}"], bass.IndirectOffsetOnAxis(
                            ap=idx[g][:, j:j + 1], axis=0)).then_inc(rows_in[r], 16)

            pool.wait_ge(recs_in, 16)
            over_turns(pool, step)

        @block.vector
        def _(dve):
            def accumulate(g, slot, w):
                dve.wait_ge(mm_done, SGT * g + SGT)
                dve.wait_ge(acc_done, g + 1)
                dve.tensor_tensor(AGG[:, at(w), 0:width], AGG[:, at(w), 0:width],
                                  pA[slot][:, 0:width].unsqueeze(1), ALU.add).then_inc(acc_done, 1)

            def step(i, first):
                if first:
                    ws = [None] + table_values(nc, mybir.EngineType.DVE, k["SWIN"], 0, [NT] * (SBODY - 1))
                else:
                    ws = table_values(nc, mybir.EngineType.DVE, k["SWIN"], SBODY * i - 1, [NT] * SBODY)
                for g in range(SBODY):
                    for j in range(SGT):
                        r = SGT * g + j
                        wait_if(dve, mm_done, TILES * i + r - 3)
                        dve.tensor_scalar(oh[r % 4][:], iota, column(keys, TILES * i + r), None,
                                          ALU.is_equal).then_inc(oh_ready, 1)
                    if not (first and g == 0):
                        accumulate(SBODY * i + g - 1, (g - 1) % SBODY, ws[g])

            dve.sem_inc(acc_done, 1)
            dve.memset(AGG[:, :, 0:width], 0.0).then_inc(zero_ready, 1)
            if layer == 0:
                for r in range(TILES):
                    ins = dve.memset(rows[r][:, D:D + 1], 1.0)
                ins.then_inc(ones_ready, 1)
            dve.wait_ge(recs_in, 16)
            dve.tensor_copy(keys[:], recs[:, :, 1]).then_inc(keys_ready, 1)
            dve.wait_ge(keys_ready, 1)
            dve.wait_ge(zero_ready, 1)
            n = over_turns(dve, step)
            w, = table_values(nc, mybir.EngineType.DVE, k["SWIN"], SBODY * n - 1, [NT])
            accumulate(SBODY * n - 1, SBODY - 1, w)

        @block.tensor
        def _(pe):
            def step(i, first):
                for g in range(SBODY):
                    for j in range(SGT):
                        r = SGT * g + j
                        pe.wait_ge(rows_in[r], 16 * i + 16)
                        pe.wait_ge(oh_ready, TILES * i + r + 1)
                        if j == 0:
                            wait_if(pe, acc_done, SBODY * i + g + 2 - SBODY)
                        pe.matmul(pA[g][:, 0:width], oh[r % 4][:], rows[r][:, 0:width], start=(j == 0),
                                  stop=(j == SGT - 1)).then_inc(mm_done, 1)

            if layer == 0:
                pe.wait_ge(ones_ready, 1)
            over_turns(pe, step)


def gnn_nodes(k, layer):
    nc, a, C, X, R, AGG, ST = k["nc"], k["a"], k["C"], k["X"], k["R"], k["AGG"], k["ST"]
    ident = C[:, C_IDENT:C_IDENT + P]
    tag = f"nodes{layer}_"
    with ExitStack() as outer:
        brows = outer.enter_context(nc.sbuf_tensor(tag + "brows", [P, 3, D], F32))
        with ExitStack() as s:
            def sb(name, shape, dt=F32):
                return s.enter_context(nc.sbuf_tensor(tag + name, shape, dt))

            def sem(name):
                return s.enter_context(nc.semaphore(tag + name))

            w, rec = sb("w", [P, KD, D]), sb("inv_degree", [P, NT])
            z = [sb(f"z{b}", [P, D]) for b in range(2)]
            zT = [sb(f"z_turned{b}", [P, KD, P]) for b in range(2)]
            pT = [s.enter_context(nc.psum_tensor(f"{tag}p_turned{b}", [P, 4, P], F32)) for b in range(2)]
            pO = [s.enter_context(nc.psum_tensor(f"{tag}p_out{b}", [P, 4 * P], F32)) for b in range(2)]
            w_in, step_done, z_ready, turned = sem("w_in"), sem("step"), sem("z_ready"), sem("turned")
            zT_ready, mm_done, r_ready = sem("zt_ready"), sem("mm_done"), sem("r_ready")
            block = s.enter_context(nc.Block())

            @block.sync
            def _(sp):
                sp.dma_start(w[:], a[f"w_g{layer}"]).then_inc(w_in, 16)
                sp.dma_start(brows[:], a[f"rows_g{layer}"]).then_inc(w_in, 16)

            @block.vector
            def _(dve):
                link = Chain(dve, step_done)
                link(dve.tensor_scalar(rec[:], AGG[:, 0:NT, D], 1.0, None, ALU.max))
                link(dve.reciprocal(rec[:], rec[:]))

                def mean(n, b):
                    wait_if(dve, turned, n - 1)
                    dve.scalar_tensor_tensor(out=z[b][:].unsqueeze(1), in0=AGG[:, at(n), 0:D], scalar=column(rec, n),
                                             in1=R[:, at(n), :], op0=ALU.mult, op1=ALU.add).then_inc(z_ready, 1)

                def step(n, b, i, first, last):
                    if not last:
                        mean(n + 1, 1 - b)
                    dve.wait_ge(mm_done, n + 1)
                    dve.tensor_tensor(R[:, at(n), :], pO[b][:, 0:D].unsqueeze(1), brows[:, 0:1, :],
                                      ALU.add).then_inc(r_ready, 1)
                    dve.wait_ge(r_ready, n + 1)
                    dve.bn_stats(ST[:, at(n), :], R[:, at(n), :])

                mean(0, 0)
                dve.wait_ge(w_in, 32)
                over_tiles(dve, step)

            @block.scalar
            def _(act):
                def step(n, b, i, first, last):
                    act.wait_ge(turned, n + 1)
                    wait_if(act, mm_done, n - 1)
                    act.copy(zT[b][:], pT[b][:, 0:KD, :]).then_inc(zT_ready, 1)

                over_tiles(act, step)

            @block.tensor
            def _(pe):
                def turn(n, b):
                    pe.wait_ge(z_ready, n + 1)
                    wait_if(pe, zT_ready, n - 1)
                    for c in range(KD):
                        mm = pe.transpose(pT[b][:, c, :], z[b][:, c * P:(c + 1) * P], ident)
                    mm.then_inc(turned, 1)

                def step(n, b, i, first, last):
                    pe.wait_ge(zT_ready, n + 1)
                    wait_if(pe, r_ready, n - 1)
                    for c in range(KD):
                        mm = pe.matmul(pO[b][:, 0:D], zT[b][:, c, :], w[:, c, :], start=(c == 0), stop=(c == KD - 1))
                    mm.then_inc(mm_done, 1)
                    if not last:
                        turn(n + 1, 1 - b)

                turn(0, 0)
                pe.wait_ge(w_in, 32)
                over_tiles(pe, step)

        finish_ln(k, f"_gnn{layer}")
        with ExitStack() as s:
            def sem(name):
                return s.enter_context(nc.semaphore(tag + name))

            normed, scaled, shifted, silu_done = sem("normed"), sem("scaled"), sem("shifted"), sem("silu_done")
            x_ready, stored = sem("x_ready"), sem("stored")
            block = s.enter_context(nc.Block())
            CH = 5
            chunks_ = [(c, slice(CH * c, CH * c + CH)) for c in range(NT // CH)]

            @block.vector
            def _(dve):
                for c, part in chunks_:
                    for n in range(part.start, part.stop):
                        ins = normalise(dve, k, R[:, n, :], R[:, n, :], n)
                    ins.then_inc(normed, 1)
                    dve.wait_ge(normed, c + 1)
                    dve.tensor_tensor(R[:, part, :], R[:, part, :], brows[:, 1:2, :].to_broadcast([P, CH, D]),
                                      ALU.mult).then_inc(scaled, 1)
                    dve.wait_ge(scaled, c + 1)
                    dve.tensor_tensor(R[:, part, :], R[:, part, :], brows[:, 2:3, :].to_broadcast([P, CH, D]),
                                      ALU.add).then_inc(shifted, 1)
                if layer == 1:
                    for c, part in chunks_:
                        dve.wait_ge(silu_done, c + 1)
                        dve.tensor_tensor(X[:, part, :], X[:, part, :], R[:, part, :], ALU.add).then_inc(x_ready, 1)
                        dve.wait_ge(x_ready, c + 1)
                        for n in range(part.start, part.stop):
                            dve.bn_stats(ST[:, n, :], X[:, n, :])

            @block.scalar
            def _(act):
                for c, part in chunks_:
                    act.wait_ge(shifted, c + 1)
                    act.activation(R[:, part, :], R[:, part, :], ACT.Silu).then_inc(silu_done, 1)

            if layer == 0:
                @block.sync
                def _(sp):
                    xg = a["xg1"].rearrange("(t p) d -> p t d", p=P)
                    for c, part in chunks_:
                        sp.wait_ge(silu_done, c + 1)
                        sp.dma_start(xg[:, part, :], R[:, part, :]).then_inc(stored, 16)
                    sp.wait_ge(stored, 16 * len(chunks_))
        if layer == 1:
            finish_ln(k, "5")


SCRATCH = [("groups", (2 * NG,), I32), ("records", (STILES * P + P, 2), I32), ("kv", (NT * P, 2 * D), F32), ("xg0", (NT * P, D), F32),
           ("xg1", (NT * P, D), F32), ("slots_in", (NSLOT + TOPK * P, D), F32), ("slots_out", (NSLOT, D), F32)]


def chunks(w):
    r, c = w.shape
    return np.ascontiguousarray(w.reshape(r // P, P, c).transpose(1, 0, 2))


def spread(row):
    return np.ascontiguousarray(np.broadcast_to(row.reshape(1, -1), (P, row.size)))


def cols(row):
    return np.ascontiguousarray(row.reshape(-1, P).T)


def expert_packs(w1, b1, g, b, w2, b2):
    out = []
    for e in range(len(w1)):
        out.append(np.concatenate([chunks(w1[e]).reshape(P, -1), chunks(w2[e]).reshape(P, -1), cols(b1[e]),
                                   cols(g[e]), cols(b[e]), spread(b2[e])], axis=1))
    return np.stack(out)


def layout(inputs):
    i = {n: np.asarray(v) for n, v in inputs.items()}

    def edges(v, fill):
        v = v.reshape(-1)
        v = np.concatenate([v, np.full(ETP * P - E, fill, v.dtype)])
        return np.ascontiguousarray(v.reshape(ETP, P).T)

    one, zero = np.ones((NEXP, D), np.float32), np.zeros((NEXP, D), np.float32)
    return {
        "consts": constants(),
        "x": np.concatenate([i["x"], np.zeros((NT * P - N, D), i["x"].dtype)]),
        "src": edges(i["src"], 0), "src_key": edges(i["src"], PAD_DST), "dst": edges(i["dst"], PAD_DST), "edge_weight1": edges(i["edge_weight1"], 0),
        "w_qkv": chunks(np.concatenate([i["L0_gnn_Wq"], i["L0_gnn_Wk"], i["L0_gnn_Wv"]], axis=1)),
        "ffn": expert_packs(*(i["L0_gnn_" + n][None] for n in ("W1", "b1", "ln1_g", "ln1_b", "W2", "b2"))),
        "w_p": chunks(i["L0_gnn_Wp"]),
        "rows0": np.stack([spread(i["L0_gnn_" + n]) for n in ("bp", "ln1_g", "ln1_b", "ln2_g", "ln2_b")], 1),
        "router0": chunks(i["L0_ffn_router_w"].T), "router1": chunks(i["L1_ffn_Wr"]),
        "rbias1": spread(np.tile(i["L1_ffn_br"], NT)),
        "experts0": expert_packs(i["L0_ffn_w1"], i["L0_ffn_b1"], one, zero, i["L0_ffn_w2"], i["L0_ffn_b2"]),
        "experts1": expert_packs(i["L1_ffn_W1"], i["L1_ffn_b1"], i["L1_ffn_ln_g"], i["L1_ffn_ln_b"],
                                 i["L1_ffn_W2"], i["L1_ffn_b2"]),
        "w_g0": chunks(i["L1_gnn_W0"].T), "w_g1": chunks(i["L1_gnn_W1"].T),
        "rows_g0": np.stack([spread(i["L1_gnn_" + n]) for n in ("b0", "g0", "beta0")], 1),
        "rows_g1": np.stack([spread(i["L1_gnn_" + n]) for n in ("b1", "g1", "beta1")], 1),
    }


def program(nc, a):
    with ExitStack() as life:
        k = {"nc": nc, "a": a}

        def keep(name, shape, dt=F32, until=life):
            k[name] = until.enter_context(nc.sbuf_tensor(name + "_kept", shape, dt))

        for name in SOFTWARE:
            k[name] = life.enter_context(nc.semaphore(name))
        keep("X", [P, NT, D])
        keep("C", [P, C_END])
        keep("ST", [P, NT + 1, 6])
        keep("VAR", [P, NT + 1])
        keep("RSTD", [P, NT + 1])
        keep("NMR", [P, NT + 1])
        keep("EPSC", [P, 1])
        with ExitStack() as gnn:
            keep("R", [P, NT + 1, D], F32, gnn)
            keep("SADDR", [P, ETP], I32, gnn)
            keep("EDGES", [P, ETP, 2], I32, gnn)
            keep("SWIN", [1, SG], I32, gnn)
            keep("STURNS", [1, 1], I32, gnn)
            with ExitStack() as att:
                keep("DST", [P, ETP], F32, att)
                keep("SRC", [P, ETP], I32, att)
                keep("BIAS", [P, ETP], F32, att)
                keep("GROUPS", [1, 2 * NG], I32, att)
                keep("NPAIR", [1, 1], I32, att)
                load_and_group(k)
                sort_by_source(k)
                keep("ACC", [P, NT + 1, VW], F32, att)
                keep("QX", [P, NT + 1, VW], F32, att)
                qkv(k)
                attention_edges(k)
                attention_out(k)
            recycle_semaphores(nc)
            ffn(k)
            moe(k, 0)
            recycle_semaphores(nc)
            keep("AGG", [P, NT + 1, D + 1], F32, gnn)
            gnn_rows(k)
            gnn_edges(k, 0)
            gnn_nodes(k, 0)
            gnn_edges(k, 1)
            gnn_nodes(k, 1)
        recycle_semaphores(nc)
        moe(k, 1)


def kernel(**inputs):
    import concourse.bacc as _bacc
    from concourse.bass_utils import run_bass_kernel_spmd as _run

    arrays = layout(inputs)
    nc = _bacc.Bacc("TRN2", target_bir_lowering=False, num_devices=1)
    a = {n: nc.dram_tensor(n, v.shape, mybir.dt.from_np(v.dtype), kind="ExternalInput").ap()
         for n, v in arrays.items()}
    for n, shape, dt in SCRATCH:
        a[n] = nc.dram_tensor(n, shape, dt, kind="Internal").ap()
    a["out"] = nc.dram_tensor("out", (N, D), F32, kind="ExternalOutput").ap()
    program(nc, a)
    r = _run(nc, [arrays], core_ids=[0])
    return r.results[0]["out"]
```

```python
import math

import numpy as np

import concourse.bass as bass
from concourse import mybir
from contextlib import ExitStack

F32 = mybir.dt.float32
I32 = mybir.dt.int32
ALU = mybir.AluOpType
ACT = mybir.ActivationFunctionType
AX = mybir.AxisListType
ALL_MAX = bass.bass_isa.ReduceOp.max

P = 128
N = 3125
D = 256
KD = D // P
NT = -(-N // P)
E = 53125
ET = -(-E // P)
ETP = ET + 4
GT = 4
GTURN = 4
HEADS, HD = 8, 32
FFN = 1024
EPS = 1e-5
NEXP, TOPK = 8, 2
BT = 256
NBLK = (N * TOPK + NEXP * (BT - 1)) // BT
NSLOT = NBLK * BT
PAD_DST = NT * P
GK = -(-(NT * -(-ET // GT) + 2 * GTURN) // P)
NG = GK * P
VW = D + HEADS
STURN = 16
STILES = E // P + NT
STILES += -STILES % STURN
SK = -(-STILES // P)

C_IDENT = 0
C_IOTA = C_IDENT + P
C_TRI = C_IOTA + P
C_ONES = C_TRI + P
C_WBASE = C_ONES + P
C_VALID = C_WBASE + NT + 1
C_TRASH = C_VALID + NT
C_RANK = C_TRASH + NT * TOPK
C_TILE1 = C_RANK + NT * NEXP
C_TILER = C_TILE1 + ETP
C_WCOL = C_TILER + ETP
C_GRP = C_WCOL + 1
C_GRPW = C_GRP + GK
C_COUNT = C_GRPW + GK * NT
C_STILE = C_COUNT + NBLK + 2
C_SPARE = C_STILE + SK
C_END = C_SPARE + 1


def constants():
    c = np.zeros((P, C_END), np.float32)
    p = np.arange(P)
    c[:, C_IDENT:C_IDENT + P] = np.eye(P)
    c[:, C_IOTA:C_IOTA + P] = p
    c[:, C_TRI:C_TRI + P] = p[:, None] < p[None, :]
    c[:, C_ONES:C_ONES + P] = 1
    c[:, C_WBASE:C_WBASE + NT + 1] = P * np.arange(NT + 1)
    row = p[:, None] + P * np.arange(NT)
    c[:, C_VALID:C_VALID + NT] = row < N
    trash = np.where(row[:, :, None] < N, 0, NSLOT + row[:, :, None] - (NT - 1) * P + P * np.arange(TOPK))
    c[:, C_TRASH:C_TRASH + NT * TOPK] = trash.reshape(P, -1)
    c[:, C_RANK:C_RANK + NT * NEXP] = np.tile(NEXP - np.arange(NEXP), NT)
    c[:, C_TILE1:C_TILE1 + ETP] = np.arange(ETP) + 1
    c[:, C_TILER:C_TILER + ETP] = ETP - np.arange(ETP)
    c[:, C_WCOL] = p
    c[:, C_GRP:C_GRP + GK] = p[:, None] * GK + np.arange(GK)
    c[:, C_GRPW:C_GRPW + GK * NT] = np.tile(np.arange(NT), GK)
    c[:, C_COUNT:C_COUNT + NBLK + 2] = np.arange(NBLK + 2)
    c[:, C_STILE:C_STILE + SK] = p[:, None] * SK + np.arange(SK)
    c[:, C_SPARE] = STILES * P + p
    return c


class Chain:

    def __init__(self, eng, sem):
        self.eng, self.sem, self.n = eng, sem, 0

    def __call__(self, ins):
        ins.then_inc(self.sem, 1)
        self.n += 1
        self.eng.wait_ge(self.sem, self.n)


def over_tiles(eng, step, count=NT):
    step(0, 0, 0, True, False)
    step(1, 1, 0, True, False)
    with eng.Fori(1, (count - 1) // 2) as i:
        step(2 * i, 0, i, False, False)
        step(2 * i + 1, 1, i, False, False)
    step(count - 1, 0, (count - 1) // 2, False, True)


def over_tiles_by_four(eng, step):
    for b in range(4):
        step(b, b, 0, True, False)
    with eng.Fori(1, NT // 4) as i:
        for b in range(4):
            step(4 * i + b, b, i, False, False)
    step(NT - 1, 0, NT // 4, False, True)


def over_pairs(eng, pairs, step):
    step(0, 0, 0, True, False)
    step(1, 1, 0, True, False)
    with eng.Fori(1, pairs) as i:
        step(2 * i, 0, i, False, False)
        step(2 * i + 1, 1, i, False, False)


def over_odd(eng, pairs, step):
    step(0, 0, 0, True, False)
    step(1, 1, 0, True, False)
    step(2, 0, 1, False, False)
    with eng.Fori(1, pairs) as i:
        step(2 * i + 1, 1, i, False, False)
        step(2 * i + 2, 0, i + 1, False, False)


def wait_if(eng, sem, value):
    if not isinstance(value, int) or value > 0:
        eng.wait_ge(sem, value)


def recycle_semaphores(nc):
    nums = sorted(set(nc.released_uncleared_semaphores))
    runs = []
    for n in nums:
        if runs and runs[-1][1] == n:
            runs[-1][1] = n + 1
        else:
            runs.append([n, n + 1])
    with nc.Block() as block:
        @block.gpsimd
        def _(pool):
            for lo, hi in runs:
                pool.sem_clear(range(lo, hi))


SOFTWARE = (["amax_kv_in"] + [f"kv_in{r}" for r in range(2 * GTURN)] + [f"records{part}_stored{b}" for part in range(5) for b in range(2)] +
            [f"scattered{layer}_{b}" for layer in range(2) for b in range(2)] +
            [f"y_in{layer}_{b}" for layer in range(2) for b in range(4)] +
            [f"agg{layer}_rows_in{r}" for layer in range(2) for r in range(8)])


def at(i, n=1):
    return bass.ds(i, n)


def column(ap, n):
    return ap[:, at(n)]


def finish_ln(k, tag):
    nc, ST = k["nc"], k["ST"]
    with ExitStack() as s:
        tmp = s.enter_context(nc.sbuf_tensor("ln_tmp" + tag, [P, 5, NT + 1], F32))
        msum, diff, m2, sq, std = (tmp[:, j, :] for j in range(5))
        var = k["VAR"][:]
        step = s.enter_context(nc.semaphore("ln_step" + tag))
        var_ready = s.enter_context(nc.semaphore("ln_var_ready" + tag))
        std_ready = s.enter_context(nc.semaphore("ln_std_ready" + tag))
        block = s.enter_context(nc.Block())

        @block.vector
        def _(dve):
            link = Chain(dve, step)
            dve.tensor_tensor(msum, ST[:, :, 1], ST[:, :, 4], ALU.add).then_inc(step, 1)
            dve.tensor_tensor(diff, ST[:, :, 1], ST[:, :, 4], ALU.subtract).then_inc(step, 1)
            link.n = 2
            link(dve.tensor_tensor(m2, ST[:, :, 2], ST[:, :, 5], ALU.add))
            link(dve.tensor_tensor(sq, diff, diff, ALU.mult))
            link(dve.tensor_scalar(m2, m2, 1.0 / D, None, ALU.mult))
            dve.scalar_tensor_tensor(out=var, in0=sq, scalar=0.25, in1=m2, op0=ALU.mult,
                                     op1=ALU.add).then_inc(var_ready, 1)
            dve.wait_ge(std_ready, 1)
            link(dve.reciprocal(k["RSTD"][:], std))
            link(dve.scalar_tensor_tensor(out=k["NMR"][:], in0=msum, scalar=-0.5, in1=k["RSTD"][:],
                                          op0=ALU.mult, op1=ALU.mult))

        @block.scalar
        def _(act):
            act.wait_ge(var_ready, 1)
            act.activation(std, var, ACT.Sqrt, bias=k["EPSC"][:, 0:1]).then_inc(std_ready, 1)


def load_and_group(k):
    nc, a, C, ST = k["nc"], k["a"], k["C"], k["ST"]
    TC = ETP // GT
    ident, ones = C[:, C_IDENT:C_IDENT + P], C[:, C_ONES:C_ONES + P]
    with ExitStack() as s:
        def sb(name, shape, dt=F32):
            return s.enter_context(nc.sbuf_tensor(name, shape, dt))

        def sem(name):
            return s.enter_context(nc.semaphore(name))

        dsti = sb("dst_int", [P, ETP], I32)
        wlo, whi = sb("win_lo", [TC, GT]), sb("win_hi", [TC, GT])
        dlo, dhi = sb("diag_lo", [TC, GT, TC]), sb("diag_hi", [TC, GT, TC])
        ge, both = sb("win_ge", [NT, ETP]), sb("win_both", [NT, ETP])
        last1, firstr = sb("last_plus1", [NT, 1]), sb("first_rev", [NT, 1])
        span, cnt = sb("win_span", [NT, 1]), sb("win_cnt", [NT, 1])
        spani, cnti = sb("win_span_i", [NT, 1], I32), sb("win_cnt_i", [NT, 1], I32)
        both2 = sb("win_rhs", [NT, 2, NT])
        ws = sb("win_start_cnt", [P, 2, NT])
        zero = sb("win_zero", [P, NT])
        cinc, base = sb("win_cinc", [P, NT]), sb("win_base", [P, NT])
        big = sb("grp_big", [P, GK, NT])
        wv, tv = sb("grp_w", [P, GK]), sb("grp_t", [P, GK])
        table = sb("grp_table", [P, GK, 2], I32)
        pairf, pairi = sb("pair_f", [1, 1]), sb("pair_i", [1, 1], I32)
        pD = s.enter_context(nc.psum_tensor("p_dst", [TC, GT, P], F32))
        pLo = s.enter_context(nc.psum_tensor("p_lo", [NT, ETP], F32))
        pHi = s.enter_context(nc.psum_tensor("p_hi", [NT, ETP], F32))
        pW = s.enter_context(nc.psum_tensor("p_w", [P, 2 * NT], F32))
        const_in, edge_in, x_in = sem("const_in"), sem("edge_in"), sem("x_in")
        dst_ready, dst_turned, diag_ready = sem("dst_ready"), sem("dst_turned"), sem("diag_ready")
        bounds_ready, rhs_ready, starts_ready = sem("bounds_ready"), sem("rhs_ready"), sem("starts_ready")
        table_ready, table_out, table_in = sem("table_ready"), sem("table_out"), sem("table_in")
        dst_in = sem("dst_in")
        step = sem("group_step")
        block = s.enter_context(nc.Block())

        @block.sync
        def _(sp):
            sp.dma_start(dsti[:], a["dst"]).then_inc(dst_in, 16)
            sp.dma_start(C[:], a["consts"]).then_inc(const_in, 16)
            sp.dma_start(k["X"][:, 0:NT, :], a["x"].rearrange("(t p) d -> p t d", p=P)).then_inc(x_in, 16)
            sp.dma_start(k["SRC"][:], a["src"]).then_inc(edge_in, 16)
            sp.dma_start(k["BIAS"][:], a["edge_weight1"]).then_inc(edge_in, 16)
            sp.wait_ge(table_ready, 1)
            sp.dma_start(a["groups"].rearrange("(p g) -> p g", p=P),
                         table[:].rearrange("p g two -> p (g two)")).then_inc(table_out, 16)
            sp.wait_ge(table_out, 16)
            sp.dma_start(k["GROUPS"][0:1, :], a["groups"].rearrange("(o g) -> o g", o=1)).then_inc(table_in, 16)
            sp.wait_ge(table_in, 16)
            sp.wait_ge(x_in, 16)
            sp.wait_ge(edge_in, 32)

        @block.gpsimd
        def _(pool):
            pool.memset(k["EPSC"][:], EPS)
            pool.memset(k["ST"][:, NT, :], 0.0)
            pool.memset(k["R"][:], 0.0)
            pool.memset(k["X"][:, NT, :], 0.0)

        @block.vector
        def _(dve):
            link = Chain(dve, step)
            dve.memset(zero[:], 0.0)
            dve.wait_ge(dst_in, 16)
            dve.tensor_copy(k["DST"][:], dsti[:]).then_inc(dst_ready, 1)
            dve.wait_ge(dst_turned, 1)
            link(dve.tensor_reduce(wlo[:], pD[:], AX.X, ALU.min))
            link(dve.tensor_reduce(whi[:], pD[:], AX.X, ALU.max))
            dve.wait_ge(const_in, 16)
            idents = ident[0:TC, 0:TC].unsqueeze(1).to_broadcast([TC, GT, TC])
            dve.tensor_tensor(dlo[:], idents, wlo[:].unsqueeze(2).to_broadcast([TC, GT, TC]),
                              ALU.mult).then_inc(diag_ready, 1)
            dve.tensor_tensor(dhi[:], idents, whi[:].unsqueeze(2).to_broadcast([TC, GT, TC]),
                              ALU.mult).then_inc(diag_ready, 1)
            dve.wait_ge(bounds_ready, 1)
            wfirst, wnext = both2[:, 0, 0:1], both2[:, 0, 1:2]
            link(dve.tensor_scalar(wfirst, C[0:NT, C_WCOL:C_WCOL + 1], float(P), None, ALU.mult))
            link(dve.tensor_scalar(wnext, wfirst, float(P), None, ALU.add))
            link(dve.tensor_scalar(ge[:], pLo[:], wnext, None, ALU.is_lt))
            link(dve.scalar_tensor_tensor(out=both[:], in0=pHi[:], scalar=wfirst, in1=ge[:],
                                          op0=ALU.is_ge, op1=ALU.mult))
            link(dve.tensor_tensor(ge[:], both[:], C[0:NT, C_TILE1:C_TILE1 + ETP], ALU.mult))
            link(dve.tensor_reduce(last1[:], ge[:], AX.X, ALU.max))
            link(dve.tensor_tensor(ge[:], both[:], C[0:NT, C_TILER:C_TILER + ETP], ALU.mult))
            link(dve.tensor_reduce(firstr[:], ge[:], AX.X, ALU.max))
            link(dve.scalar_tensor_tensor(out=span[:], in0=last1[:], scalar=float(GT - 1 - ETP),
                                          in1=firstr[:], op0=ALU.add, op1=ALU.add))
            link(dve.tensor_scalar(spani[:], span[:], 0.0, None, ALU.max))
            link(dve.tensor_scalar(cnti[:], spani[:], 2, None, ALU.arith_shift_right))
            link(dve.tensor_copy(cnt[:], cnti[:]))
            link(dve.tensor_scalar(span[:], firstr[:], -1.0, float(ETP), ALU.mult, ALU.add))
            link(dve.tensor_scalar(both2[:, 0, :], ident[0:NT, 0:NT], span[:, 0:1], None, ALU.mult))
            dve.tensor_scalar(both2[:, 1, :], ident[0:NT, 0:NT], cnt[:, 0:1], None,
                              ALU.mult).then_inc(rhs_ready, 1)
            dve.wait_ge(starts_ready, 1)
            link(dve.tensor_copy(ws[:].rearrange("p a w -> p (a w)"), pW[:]))
            link(dve.tensor_tensor_scan(cinc[:], ws[:, 1, :], zero[:], 0.0, ALU.add, ALU.add))
            link(dve.tensor_tensor(base[:], cinc[:], ws[:, 1, :], ALU.subtract))
            link(dve.scalar_tensor_tensor(out=base[:], in0=base[:], scalar=-float(GT), in1=ws[:, 0, :],
                                          op0=ALU.mult, op1=ALU.add))
            grp = C[:, C_GRP:C_GRP + GK]
            wide = [P, GK, NT]
            link(dve.tensor_tensor(big[:], cinc[:].unsqueeze(1).to_broadcast(wide),
                                   grp.unsqueeze(2).to_broadcast(wide), ALU.is_le))
            link(dve.tensor_reduce(wv[:], big[:], AX.X, ALU.add))
            link(dve.tensor_tensor(big[:], C[:, C_GRPW:C_GRPW + GK * NT].rearrange("p (g w) -> p g w", w=NT),
                                   wv[:].unsqueeze(2).to_broadcast(wide), ALU.is_equal))
            link(dve.tensor_tensor(big[:], big[:], base[:].unsqueeze(1).to_broadcast(wide), ALU.mult))
            link(dve.tensor_reduce(tv[:], big[:], AX.X, ALU.add))
            link(dve.scalar_tensor_tensor(out=tv[:], in0=grp, scalar=float(GT), in1=tv[:],
                                          op0=ALU.mult, op1=ALU.add))
            link(dve.tensor_scalar(tv[:], tv[:], float(ET), None, ALU.min))
            link(dve.tensor_scalar(pairi[:], cinc[0:1, NT - 1:NT], float(GTURN - 1), None, ALU.add))
            link(dve.tensor_scalar(k["GTURNS"][:], pairi[:], GTURN.bit_length() - 1, None, ALU.arith_shift_right))
            link(dve.tensor_copy(table[:, :, 0], tv[:]))
            dve.tensor_copy(table[:, :, 1], wv[:]).then_inc(table_ready, 1)
            dve.wait_ge(x_in, 16)
            with dve.Fori(0, NT) as n:
                dve.bn_stats(ST[:, at(n), :], k["X"][:, at(n), :])

        @block.tensor
        def _(pe):
            pe.wait_ge(const_in, 16)
            pe.wait_ge(dst_ready, 1)
            for c in range(GT):
                mm = pe.transpose(pD[:, c, :], k["DST"][:, c * TC:(c + 1) * TC], ident)
            mm.then_inc(dst_turned, 1)
            pe.wait_ge(diag_ready, 2)
            for out, diag in ((pLo, dlo), (pHi, dhi)):
                mm = pe.matmul(out[:], ones[0:TC, 0:NT], diag[:].rearrange("p c t -> p (c t)"),
                               start=True, stop=True)
            mm.then_inc(bounds_ready, 1)
            pe.wait_ge(rhs_ready, 1)
            pe.matmul(pW[:], ones[0:NT, :], both2[:].rearrange("p a w -> p (a w)"), start=True,
                      stop=True).then_inc(starts_ready, 1)


def normalise(eng, k, out, rows, n):
    return eng.tensor_scalar(out, rows, column(k["RSTD"], n), column(k["NMR"], n), ALU.mult, ALU.add)


def qkv(k):
    nc, a, C, X, QX = k["nc"], k["a"], k["C"], k["X"], k["QX"]
    finish_ln(k, "0")
    ident = C[:, C_IDENT:C_IDENT + P]
    with ExitStack() as s:
        def sb(name, shape, dt=F32):
            return s.enter_context(nc.sbuf_tensor(name, shape, dt))

        def sem(name):
            return s.enter_context(nc.semaphore(name))

        w = sb("qkv_w", [P, KD, 3 * D])
        hs = [sb(f"h_row{b}", [P, D]) for b in range(2)]
        hT = [sb(f"hT{b}", [P, KD, P]) for b in range(2)]
        kv = [sb(f"kv_out{b}", [P, 2 * D]) for b in range(2)]
        sq = [sb(f"qk_square{b}", [P, 2 * D]) for b in range(2)]
        norm = sb("qk_norm", [P, NT, 2 * HEADS])
        most, mostall = sb("most", [P, 4]), sb("most_all", [P, 4])
        bound = sb("bound", [P, 4])
        pT = [s.enter_context(nc.psum_tensor(f"p_hT{b}", [P, KD, P], F32)) for b in range(2)]
        pQ = [s.enter_context(nc.psum_tensor(f"p_q{b}", [P, 2 * D], F32)) for b in range(2)]
        pKV = [s.enter_context(nc.psum_tensor(f"p_kv{b}", [P, 2 * D], F32)) for b in range(2)]
        w_in, h_ready, turned, hT_ready = sem("w_in"), sem("h_ready"), sem("turned"), sem("hT_ready")
        mm_done, q_copied, squared, kv_ready = sem("mm_done"), sem("q_copied"), sem("squared"), sem("kv_ready")
        summed, kv_stored = sem("summed"), [sem("kv_stored0"), sem("kv_stored1")]
        q_step, most_ready, all_ready, root_ready = sem("q_step"), sem("most_ready"), sem("all_ready"), sem("root_ready")
        win_out, win_in = sem("windows_out"), sem("windows_in")
        records = store_records(k, s, 0)
        block = s.enter_context(nc.Block())
        kv_rows = a["kv"].rearrange("(t p) d -> t p d", p=P)

        @block.sync
        def _(sp):
            sp.dma_start(w[:], a["w_qkv"]).then_inc(w_in, 16)
            sp.dma_start(a["tile_windows"].rearrange("(p g) -> p g", p=P), k["TILEWIN"][:]).then_inc(win_out, 16)
            sp.wait_ge(win_out, 16)
            sp.dma_start(k["SWIN"][0:1, :], a["tile_windows"].rearrange("(o g) -> o g", o=1)).then_inc(win_in, 16)

            def step(n, b, i, first, last):
                sp.wait_ge(kv_ready, n + 1)
                sp.dma_start(kv_rows[at(n)], kv[b][:]).then_inc(kv_stored[b], 16)

            over_tiles(sp, step)
            sp.wait_ge(kv_stored[0], 16 * ((NT + 1) // 2))
            sp.wait_ge(kv_stored[1], 16 * (NT // 2))
            sp.wait_ge(win_in, 16)

        @block.vector
        def _(dve):
            def begin(n, b):
                wait_if(dve, turned, n - 1)
                normalise(dve, k, hs[b][:].unsqueeze(1), X[:, at(n), :], n).then_inc(h_ready, 1)

            def step(n, b, i, first, last):
                if not last:
                    begin(n + 2, b)
                dve.wait_ge(mm_done, n + 1)
                dve.tensor_copy(QX[:, at(n), 0:D], pQ[b][:, 0:D].unsqueeze(1)).then_inc(q_copied, 1)
                dve.wait_ge(q_copied, n + 1)
                q = QX[:, at(n), 0:D]
                dve.tensor_tensor(sq[b][:, 0:D].unsqueeze(1), q, q, ALU.mult).then_inc(squared, 1)
                dve.wait_ge(kv_ready, n + 1)
                key = kv[b][:, 0:D]
                dve.tensor_tensor(sq[b][:, D:2 * D], key, key, ALU.mult).then_inc(squared, 1)
                dve.wait_ge(squared, 2 * n + 2)
                dve.tensor_reduce(norm[:, at(n), :], sq[b][:].rearrange("p (h c) -> p h c", c=HD),
                                  AX.X, ALU.add).then_inc(summed, 1)

            dve.memset(QX[:, NT, 0:D], 0.0)
            dve.memset(QX[:, :, D:VW], 0.0)
            begin(0, 0)
            begin(1, 1)
            over_tiles(dve, step)
            link = Chain(dve, q_step)
            dve.wait_ge(summed, NT)
            link(dve.tensor_reduce(most[:, 0:1], norm[:, :, 0:HEADS], AX.XY, ALU.max))
            link(dve.tensor_reduce(most[:, 1:2], norm[:, :, HEADS:2 * HEADS], AX.XY, ALU.max))
            link(dve.tensor_reduce(most[:, 2:3], k["BIAS"][:], AX.X, ALU.max))
            link(dve.tensor_reduce(most[:, 3:4], k["BIAS"][:], AX.X, ALU.min))
            dve.tensor_scalar(most[:, 3:4], most[:, 3:4], -1.0, None, ALU.mult).then_inc(most_ready, 1)
            dve.wait_ge(root_ready, 1)
            link(dve.scalar_tensor_tensor(out=bound[:, 2:3], in0=bound[:, 0:1], scalar=1.001 / math.sqrt(HD),
                                          in1=bound[:, 1:2], op0=ALU.mult, op1=ALU.mult))
            link(dve.tensor_scalar(bound[:, 3:4], bound[:, 2:3], mostall[:, 2:3], -1.0, ALU.add, ALU.mult))
            link(dve.tensor_copy(k["SHIFT"][:], bound[:, 3:4]))
            link(dve.scalar_tensor_tensor(out=bound[:, 2:3], in0=bound[:, 2:3], scalar=2.0, in1=mostall[:, 2:3],
                                          op0=ALU.mult, op1=ALU.add))
            link(dve.tensor_scalar(k["FLAG"][:], bound[:, 2:3], mostall[:, 3:4], 80.0, ALU.add, ALU.is_gt))
            runs = most[0:1, 0:2]
            link(dve.tensor_scalar(runs[:, 0:1], k["GTURNS"][:], float(GTURN), -1.0, ALU.mult, ALU.add))
            link(dve.memset(runs[:, 1:2], float(GT - 1)))
            link(dve.tensor_scalar(k["MAXRUNS"][:], runs, k["FLAG"][0:1, 0:1], 1.0, ALU.mult, ALU.add))

        @block.gpsimd
        def _(pool):
            pool.memset(k["ACC"][:], 0.0)
            records(pool)
            pool.wait_ge(most_ready, 1)
            pool.partition_all_reduce(mostall[:], most[:], P, ALL_MAX).then_inc(all_ready, 1)

        @block.scalar
        def _(act):
            act.activation(bound[:, 0:1], k["EPSC"][:], ACT.Sqrt)

            def copy_turned(n, b):
                act.wait_ge(turned, n + 1)
                wait_if(act, mm_done, n - 1)
                act.copy(hT[b][:], pT[b][:]).then_inc(hT_ready, 1)

            def step(n, b, i, first, last):
                if not last:
                    copy_turned(n + 1, 1 - b)
                act.wait_ge(mm_done, n + 1)
                if not first:
                    act.wait_ge(kv_stored[b], 16 * i)
                    act.wait_ge(summed, n - 1)
                act.copy(kv[b][:], pKV[b][:]).then_inc(kv_ready, 1)

            copy_turned(0, 0)
            over_tiles(act, step)
            act.wait_ge(all_ready, 1)
            act.activation(bound[:, 0:2], mostall[:, 0:2], ACT.Sqrt).then_inc(root_ready, 1)

        @block.tensor
        def _(pe):
            def turn(n, b):
                pe.wait_ge(h_ready, n + 1)
                wait_if(pe, hT_ready, n - 1)
                for c in range(KD):
                    mm = pe.transpose(pT[b][:, c, :], hs[b][:, c * P:(c + 1) * P], ident)
                mm.then_inc(turned, 1)

            def step(n, b, i, first, last):
                if not last:
                    turn(n + 1, 1 - b)
                pe.wait_ge(hT_ready, n + 1)
                if not first:
                    pe.wait_ge(q_copied, n - 1)
                    pe.wait_ge(kv_ready, n - 1)
                for out, lo, hi in ((pQ[b], 0, D), (pKV[b], D, 3 * D)):
                    for c in range(KD):
                        mm = pe.matmul(out[:, 0:hi - lo], hT[b][:, c, :], w[:, c, lo:hi], start=(c == 0),
                                       stop=(c == KD - 1))
                mm.then_inc(mm_done, 1)

            pe.wait_ge(w_in, 16)
            turn(0, 0)
            over_tiles(pe, step)


def sort_by_source(k):
    nc, a, C = k["nc"], k["a"], k["C"]
    tri, ones = C[:, C_TRI:C_TRI + P], C[:, C_ONES:C_ONES + P]
    wide = [P, NT, ETP]
    with ExitStack() as s:
        def sb(name, shape, dt=F32):
            return s.enter_context(nc.sbuf_tensor(name, shape, dt))

        def sem(name):
            return s.enter_context(nc.semaphore(name))

        keyi, lowi, wini = (sb("source_" + n, [P, ETP], I32) for n in ("key", "low", "win"))
        win, pos, spare = (sb("edge_" + n, [P, ETP]) for n in ("win", "pos", "spare"))
        posi, lo7, hi7 = (sb("pos_" + n, [P, ETP], I32) for n in ("int", "low", "high"))
        lowf, highf, addr = (sb("addr_" + n, [P, ETP]) for n in ("low", "high", "row"))
        oh, cum = sb("win_onehot", wide), sb("win_running", wide)
        ends, cnt = sb("run_ends", [P, NT + 1]), sb("part_count", [P, NT])
        tot, pre = sb("win_total", [P, NT]), sb("part_prefix", [P, NT])
        grpi, grps, ginc, adj, nought = (sb("sgrp_" + n, [P, NT], dt) for n, dt in
                                         (("int", I32), ("cnt", F32), ("inc", F32), ("adj", F32), ("zero", F32)))
        turns = sb("turns_int", [1, 1], I32)
        which, which_w = sb("tile_which", [P, SK, NT]), sb("tile_which_w", [P, SK])
        empty = sb("empty_records", [P, STILES, 2], I32)
        pPre = s.enter_context(nc.psum_tensor("p_prefix", [P, NT], F32))
        pTot = s.enter_context(nc.psum_tensor("p_total", [P, NT], F32))
        key_in, empty_ready, records_out = sem("key_in"), sem("empty_ready"), sem("records_out")
        counts_ready, sums_ready, step = sem("counts_ready"), sem("sums_ready"), sem("sort_step")
        zeros_out = sem("zeros_out")
        fills = []
        for name in ("slots_in", "slots_out"):
            slots = a[name].rearrange("(p r) d -> p r d", p=P)
            count = slots.shape[1]
            fills += [slots[:, lo:min(lo + NT + 1, count), :] for lo in range(0, count, NT + 1)]
        block = s.enter_context(nc.Block())

        @block.sync
        def _(sp):
            sp.dma_start(keyi[:], a["src_key"]).then_inc(key_in, 16)
            for part in fills:
                sp.dma_start(part, k["R"][:, 0:part.shape[1], :]).then_inc(zeros_out, 16)
            sp.wait_ge(empty_ready, 2)
            sp.dma_start(a["records"][0:STILES * P, :].rearrange("(p t) two -> p t two", p=P),
                         empty[:]).then_inc(records_out, 16)
            sp.wait_ge(records_out, 16)
            sp.wait_ge(zeros_out, 16 * len(fills))

        @block.gpsimd
        def _(pool):
            pool.memset(empty[:, :, 0], 0).then_inc(empty_ready, 1)
            pool.memset(empty[:, :, 1], -1).then_inc(empty_ready, 1)

        @block.vector
        def _(dve):
            link = Chain(dve, step)
            dve.wait_ge(key_in, 16)
            dve.memset(nought[:], 0.0)
            dve.memset(ends[:], 0.0)
            link(dve.tensor_scalar(wini[:], keyi[:], 7, None, ALU.arith_shift_right))
            link(dve.tensor_scalar(lowi[:], keyi[:], P - 1, None, ALU.bitwise_and))
            link(dve.tensor_copy(win[:], wini[:]))
            link(dve.tensor_copy(k["EDGES"][:, :, 0], k["DST"][:]))
            link(dve.tensor_copy(k["EDGES"][:, :, 1], lowi[:]))
            link(dve.tensor_tensor(oh[:], win[:].unsqueeze(1).to_broadcast(wide),
                                   C[:, C_GRPW:C_GRPW + NT].unsqueeze(2).to_broadcast(wide), ALU.is_equal))
            flat = oh[:].rearrange("p w t -> p (w t)")
            link(dve.tensor_tensor_scan(cum[:].rearrange("p w t -> p (w t)"), flat,
                                        nought[:, 0:1].to_broadcast([P, NT * ETP]), 0.0, ALU.add, ALU.add))
            link(dve.tensor_copy(ends[:, 1:NT + 1], cum[:, :, ETP - 1]))
            dve.tensor_tensor(cnt[:], ends[:, 1:NT + 1], ends[:, 0:NT], ALU.subtract).then_inc(counts_ready, 1)
            dve.wait_ge(sums_ready, 1)
            link(dve.tensor_copy(pre[:], pPre[:]))
            link(dve.tensor_scalar(grpi[:], pTot[:], 1.0, float(P - 1), ALU.max, ALU.add))
            link(dve.tensor_scalar(grpi[:], grpi[:], 7, None, ALU.arith_shift_right))
            link(dve.tensor_copy(grps[:], grpi[:]))
            link(dve.tensor_tensor_scan(ginc[:], grps[:], nought[:], 0.0, ALU.add, ALU.add))
            link(dve.tensor_tensor(adj[:], ginc[:], grps[:], ALU.subtract))
            link(dve.scalar_tensor_tensor(out=adj[:], in0=adj[:], scalar=float(P), in1=pre[:],
                                          op0=ALU.mult, op1=ALU.add))
            link(dve.scalar_tensor_tensor(out=adj[:], in0=adj[:], scalar=-1.0, in1=ends[:, 0:NT],
                                          op0=ALU.add, op1=ALU.subtract))
            for w in range(NT):
                ins = dve.scalar_tensor_tensor(out=cum[:, w, :], in0=cum[:, w, :], scalar=adj[:, w:w + 1],
                                               in1=oh[:, w, :], op0=ALU.add, op1=ALU.mult)
            link(ins)
            link(dve.tensor_reduce(pos[:], cum[:].rearrange("p w t -> p t w"), AX.X, ALU.add))
            link(dve.tensor_copy(posi[:], pos[:]))
            link(dve.tensor_scalar(lo7[:], posi[:], P - 1, None, ALU.bitwise_and))
            link(dve.tensor_scalar(hi7[:], posi[:], 7, None, ALU.arith_shift_right))
            link(dve.tensor_copy(lowf[:], lo7[:]))
            link(dve.tensor_copy(highf[:], hi7[:]))
            link(dve.scalar_tensor_tensor(out=addr[:], in0=lowf[:], scalar=float(STILES), in1=highf[:],
                                          op0=ALU.mult, op1=ALU.add))
            link(dve.tensor_scalar(spare[:], win[:], float(NT), C[:, C_SPARE:C_SPARE + 1], ALU.is_ge, ALU.mult))
            link(dve.tensor_tensor(k["SADDR"][:], addr[:], spare[:], ALU.add))
            part = [P, SK, NT]
            link(dve.tensor_tensor(which[:], ginc[:].unsqueeze(1).to_broadcast(part),
                                   C[:, C_STILE:C_STILE + SK].unsqueeze(2).to_broadcast(part), ALU.is_le))
            link(dve.tensor_reduce(which_w[:], which[:], AX.X, ALU.add))
            link(dve.tensor_copy(k["TILEWIN"][:], which_w[:]))
            link(dve.tensor_scalar(turns[:], ginc[0:1, NT - 1:NT], float(STURN - 1), None, ALU.add))
            link(dve.tensor_scalar(k["STURNS"][:], turns[:], STURN.bit_length() - 1, None, ALU.arith_shift_right))

        @block.tensor
        def _(pe):
            pe.wait_ge(counts_ready, 1)
            pe.matmul(pPre[:], tri, cnt[:], start=True, stop=True)
            pe.matmul(pTot[:], ones, cnt[:], start=True, stop=True).then_inc(sums_ready, 1)


def table_values(nc, engine, table, lo, most):
    why = "the chip computed the table within these bounds"
    values = nc.values_load_multi_w_load_instructions(
        table[0:1, at(lo, len(most))], engines=[engine], min_val=0, max_val=max(most),
        skip_runtime_bounds_check_because=why)[1]
    return [nc.s_assert_within(v, 0, m, skip_runtime_bounds_check_because=why) for v, m in zip(values, most)]


def attention_edges(k):
    nc, a, C, QX, ACC = k["nc"], k["a"], k["C"], k["QX"], k["ACC"]
    ident, iota = C[:, C_IDENT:C_IDENT + P], C[:, C_IOTA:C_IOTA + P]
    ENG = mybir.EngineType
    RING = 2 * GTURN
    with ExitStack() as s:
        def sb(name, shape, dt=F32):
            return s.enter_context(nc.sbuf_tensor(name, shape, dt))

        def sem(name):
            return s.enter_context(nc.semaphore(name))

        kv = [sb(f"kv_pair{r}", [P, 2, 2 * D]) for r in range(RING)]
        idx = [sb(f"gather_idx{b}", [P, GT], I32) for b in range(2)]
        bias = [sb(f"edge_bias{b}", [P, GT]) for b in range(2)]
        oh = [sb(f"onehot{r}", [P, 2, P]) for r in range(4)]
        off = [sb(f"dst_offset{q}", [P, 2]) for q in range(2)]
        dist = [sb(f"dst_distance{q}", [P, 2, P]) for q in range(2)]
        oht = [sb(f"onehot_turned{q}", [P, 2, P]) for q in range(2)]
        prod, red = sb("qk_prod", [P, 2, D]), sb("qk_sum", [P, 2, HEADS])
        score = [sb(f"score{q}", [P, 2, HEADS]) for q in range(2)]
        wv = [sb(f"weighted_v{q}", [P, 2, VW]) for q in range(2)]
        pQ = [s.enter_context(nc.psum_tensor(f"p_edge_q{q}", [P, 2, 4 * P], F32)) for q in range(2)]
        pT = [s.enter_context(nc.psum_tensor(f"p_turned{q}", [P, 4, P], F32)) for q in range(2)]
        pA = [s.enter_context(nc.psum_tensor(f"p_sums{b}", [P, 4 * P], F32)) for b in range(2)]
        kv_in = [k[f"kv_in{r}"] for r in range(RING)]
        idx_ready, bias_ready, tally = sem("idx_ready"), sem("bias_ready"), sem("tally")
        oh_ready, turned, oht_ready, q_ready = sem("oh_ready"), sem("oh_turned"), sem("oht_ready"), sem("q_ready")
        prod_ready, red_ready, score_ready = sem("prod_ready"), sem("red_ready"), sem("score_ready")
        exp_ready, wv_ready, sums_ready, acc_done = (sem("exp_ready"), sem("wv_ready"), sem("pair_sums_ready"),
                                                     sem("acc_done"))
        off_ready, dist_ready = sem("off_ready"), sem("dist_ready")
        block = s.enter_context(nc.Block())

        def over_groups(eng, step):
            turns = eng.value_load(k["GTURNS"][0:1, 0:1], min_val=2, max_val=NG // GTURN - 1)
            for s in range(GTURN):
                step(s, s, 0, True)
            with eng.Fori(1, turns) as i:
                for s in range(GTURN):
                    step(GTURN * i + s, s, i, False)
            return turns

        @block.gpsimd
        def _(pool):
            def step(b, s, i, first):
                p = s % 2
                t, = table_values(nc, ENG.Pool, k["GROUPS"], 2 * b, [ET])
                if not (first and s < 2):
                    for q in range(2):
                        pool.wait_ge(kv_in[(2 * s + q - 4) % RING], 32 * (i + 1 if s >= 2 else i))
                pool.sem_inc(tally, 1)
                pool.tensor_copy(idx[p][:], k["SRC"][:, at(t, GT)]).then_inc(idx_ready, 1)
                pool.wait_ge(idx_ready, b + 1)
                for q in range(2):
                    r, u = 2 * s + q, 2 * b + q
                    wait_if(pool, wv_ready, u + 1 - RING)
                    pool.sem_inc(tally, 1)
                    for j in range(2):
                        pool.indirect_dma_start(kv[r][:, j, :], None, a["kv"], bass.IndirectOffsetOnAxis(
                            ap=idx[p][:, 2 * q + j:2 * q + j + 1], axis=0)).then_inc(kv_in[r], 16)

            over_groups(pool, step)

        @block.vector
        def _(dve):
            def offsets(u, slot, q, t, w):
                wait_if(dve, oh_ready, u - 1)
                dve.tensor_scalar(off[slot][:], k["DST"][:, at(t + 2 * q, 2)], -1.0, column(C, C_WBASE + w), ALU.mult,
                                  ALU.add).then_inc(off_ready, 1)

            def shifted_bias(b, p, t):
                wait_if(dve, exp_ready, 2 * (b - 1))
                dve.tensor_scalar(bias[p][:], k["BIAS"][:, at(t, GT)], k["SHIFT"][:, 0:1], None,
                                  ALU.add).then_inc(bias_ready, 1)

            def weigh(u, r, q):
                dve.wait_ge(exp_ready, u + 1)
                dve.tensor_tensor(wv[q][:, :, 0:D].rearrange("p j (h c) -> p j h c", c=HD),
                                  kv[r][:, :, D:2 * D].rearrange("p j (h c) -> p j h c", c=HD),
                                  wv[q][:, :, D:VW].unsqueeze(3).to_broadcast([P, 2, HEADS, HD]),
                                  ALU.mult).then_inc(wv_ready, 1)

            def accumulate(b, p, w, sums):
                dve.wait_ge(sums_ready, sums)
                dve.wait_ge(acc_done, b + 2)
                dve.tensor_tensor(ACC[:, at(w), :], ACC[:, at(w), :], pA[p][:, 0:VW].unsqueeze(1),
                                  ALU.add).then_inc(acc_done, 1)

            def step(b, s, i, first):
                p = s % 2
                if s == 0:
                    some = table_values(nc, ENG.DVE, k["GROUPS"], 2 * b + 1 if first else 2 * b - 3,
                                        [NT, ET] * (GTURN + (1 if first else 3)) + [NT])
                    turn[:] = ([None] * 4 if first else []) + some
                ts, ws = turn[2 * s + 5:2 * s + 8:2], turn[2 * s + 6:2 * s + 9:2]
                for q in range(2):
                    r, u = 2 * s + q, 2 * b + q
                    dve.wait_ge(kv_in[r], 32 * (i + 1))
                    dve.wait_ge(q_ready, u + 1)
                    dve.tensor_tensor(prod[:], kv[r][:, :, 0:D], pQ[q][:, :, 0:D], ALU.mult).then_inc(prod_ready, 1)
                    if q == 1:
                        shifted_bias(b + 1, 1 - p, ts[0])
                    elif not (first and s < 2):
                        accumulate(b - 2, p, turn[2 * s], 2 * b - 2)
                    dve.wait_ge(prod_ready, u + 1)
                    dve.tensor_reduce(red[:].rearrange("p j h -> p (j h)"),
                                      prod[:].rearrange("p j (h c) -> p (j h) c", c=HD), AX.X,
                                      ALU.add).then_inc(red_ready, 1)
                    if not (first and r == 0):
                        weigh(u - 1, (r - 1) % RING, 1 - q)
                    offsets(u + 3, 1 - q, 1 - q, ts[q], ws[q])
                    dve.wait_ge(red_ready, u + 1)
                    wait_if(dve, exp_ready, u - 1)
                    dve.scalar_tensor_tensor(out=score[q][:], in0=red[:], scalar=1.0 / math.sqrt(HD),
                                             in1=pQ[q][:, :, D:VW], op0=ALU.mult,
                                             op1=ALU.add).then_inc(score_ready, 1)

            dve.sem_inc(acc_done, 2)
            turn = []
            t, w, tnext, wnext = table_values(nc, ENG.DVE, k["GROUPS"], 0, [ET, NT] * 2)
            offsets(0, 0, 0, t, w)
            offsets(1, 1, 1, t, w)
            offsets(2, 0, 0, tnext, wnext)
            shifted_bias(0, 0, t)
            n = over_groups(dve, step)
            weigh(RING * n - 1, RING - 1, 1)
            w, _, wlast = table_values(nc, ENG.DVE, k["GROUPS"], RING * n - 3, [NT, ET, NT])
            accumulate(GTURN * n - 2, 0, w, RING * n)
            accumulate(GTURN * n - 1, 1, wlast, RING * n)

        @block.scalar
        def _(act):
            def onehots(u, r, q):
                act.wait_ge(off_ready, u + 1)
                wait_if(act, oh_ready, u - 1)
                for j in range(2):
                    ins = act.activation(dist[q][:, j, :], iota, ACT.Square, bias=off[q][:, j:j + 1])
                ins.then_inc(dist_ready, 1)
                act.wait_ge(dist_ready, u + 1)
                wait_if(act, sums_ready, u - 3)
                act.activation(oh[r][:], dist[q][:], ACT.Relu, bias=C[:, C_ONES:C_ONES + 1],
                               scale=-1.0).then_inc(oh_ready, 1)

            def copy_turned(u, q):
                act.wait_ge(turned, u + 1)
                wait_if(act, q_ready, u - 1)
                act.copy(oht[q][:], pT[q][:, 0:2, :]).then_inc(oht_ready, 1)

            def step(b, s, i, first):
                p = s % 2
                for q in range(2):
                    r, u = 2 * s + q, 2 * b + q
                    act.wait_ge(bias_ready, b + 1)
                    act.wait_ge(score_ready, u + 1)
                    wait_if(act, sums_ready, u - 1)
                    for j in range(2):
                        ins = act.activation(wv[q][:, j, D:VW], score[q][:, j, :], ACT.Exp,
                                             bias=bias[p][:, 2 * q + j:2 * q + j + 1])
                    ins.then_inc(exp_ready, 1)
                    copy_turned(u + 2, q)
                    onehots(u + 3, (r + 3) % 4, 1 - q)

            act.activation(score[0][:, 0, 0:1], k["EPSC"][:], ACT.Exp)
            onehots(0, 0, 0)
            onehots(1, 1, 1)
            copy_turned(0, 0)
            copy_turned(1, 1)
            onehots(2, 2, 0)
            over_groups(act, step)

        @block.tensor
        def _(pe):
            def turn(u, r, q):
                pe.wait_ge(oh_ready, u + 1)
                wait_if(pe, oht_ready, u - 1)
                for j in range(2):
                    mm = pe.transpose(pT[q][:, j, :], oh[r][:, j, :], ident)
                mm.then_inc(turned, 1)

            def spread_q(u, q, w):
                pe.wait_ge(oht_ready, u + 1)
                wait_if(pe, score_ready, u - 1)
                for j in range(2):
                    mm = pe.matmul(pQ[q][:, j, 0:VW], oht[q][:, j, :], QX[:, at(w), :].squeeze(1), start=True,
                                   stop=True)
                mm.then_inc(q_ready, 1)

            def sum_up(u, r, q, b, p):
                pe.wait_ge(wv_ready, u + 1)
                if q == 0:
                    pe.wait_ge(acc_done, b + 1)
                for j in range(2):
                    mm = pe.matmul(pA[p][:, 0:VW], oh[r][:, j, :], wv[q][:, j, :], start=(q == 0 and j == 0),
                                   stop=(q == 1 and j == 1))
                mm.then_inc(sums_ready, 1)

            def step(b, s, i, first):
                p = s % 2
                wnext, = table_values(nc, ENG.PE, k["GROUPS"], 2 * b + 3, [NT])
                for q in range(2):
                    r, u = 2 * s + q, 2 * b + q
                    if q == 1:
                        sum_up(u - 1, (r + 3) % 4, 0, b, p)
                    elif not (first and s == 0):
                        sum_up(u - 1, (r + 3) % 4, 1, b - 1, 1 - p)
                    spread_q(u + 2, q, wnext)
                    turn(u + 3, (r + 3) % 4, 1 - q)

            w, = table_values(nc, ENG.PE, k["GROUPS"], 1, [NT])
            turn(0, 0, 0)
            turn(1, 1, 1)
            spread_q(0, 0, w)
            turn(2, 2, 0)
            spread_q(1, 1, w)
            n = over_groups(pe, step)
            sum_up(RING * n - 1, 3, 1, GTURN * n - 1, 1)


def attention_max(k):
    nc, a, C, QX = k["nc"], k["a"], k["C"], k["QX"]
    ident, iota = C[:, C_IDENT:C_IDENT + P], C[:, C_IOTA:C_IOTA + P]
    FAR = 1e30
    with ExitStack() as s:
        def sb(name, shape, dt=F32):
            return s.enter_context(nc.sbuf_tensor("amax_" + name, shape, dt))

        def sem(name):
            return s.enter_context(nc.semaphore("amax_" + name))

        idx, kv = sb("idx", [P, 1], I32), sb("kv", [P, 2 * D])
        oh, oht, pen = sb("onehot", [P, P]), sb("onehot_turned", [P, P]), sb("penalty", [P, P])
        prod, score = sb("prod", [P, D]), sb("score", [P, HEADS])
        cand, best = sb("candidates", [P, HEADS, P]), sb("best", [P, HEADS])
        most = sb("most", [P, NT + 1, HEADS])
        pT = s.enter_context(nc.psum_tensor("amax_p_turned", [P, 4 * P], F32))
        pQ = s.enter_context(nc.psum_tensor("amax_p_q", [P, 4 * P], F32))
        pC = [s.enter_context(nc.psum_tensor(f"amax_p_cand{b}", [P, 4, P], F32)) for b in range(2)]
        idx_ready, tally, kv_in = sem("idx_ready"), sem("tally"), k["amax_kv_in"]
        oh_ready, turned, oht_ready, q_ready = sem("oh_ready"), sem("turned"), sem("oht_ready"), sem("q_ready")
        cand_ready, cand_turned, tile_done, step = (sem("cand_ready"), sem("cand_turned"), sem("tile_done"),
                                                    sem("step"))
        block = s.enter_context(nc.Block())

        def over_edge_tiles(eng, step_of):
            groups = eng.value_load(k["MAXRUNS"][0:1, 0:1], min_val=1, max_val=NG)
            tiles = eng.value_load(k["MAXRUNS"][0:1, 1:2], min_val=1, max_val=GT)
            with eng.Fori(0, groups) as g:
                with eng.Fori(0, tiles) as j:
                    step_of(GT * g + j, g, j)

        @block.gpsimd
        def _(pool):
            def tile(v, g, j):
                t, = table_values(nc, mybir.EngineType.Pool, k["GROUPS"], 2 * g, [ET])
                pool.wait_ge(tile_done, v + 1)
                pool.sem_inc(tally, 1)
                pool.tensor_copy(idx[:], k["SRC"][:, at(t + j)]).then_inc(idx_ready, 1)
                pool.wait_ge(idx_ready, v + 1)
                pool.sem_inc(tally, 1)
                pool.indirect_dma_start(kv[:], None, a["kv"], bass.IndirectOffsetOnAxis(
                    ap=idx[:, 0:1], axis=0)).then_inc(kv_in, 16)

            over_edge_tiles(pool, tile)

        @block.vector
        def _(dve):
            STEPS = 8

            def tile(v, g, j):
                def then(ins, n):
                    ins.then_inc(step, 1)
                    dve.wait_ge(step, STEPS * v + n)

                t, w = table_values(nc, mybir.EngineType.DVE, k["GROUPS"], 2 * g, [ET, NT])
                then(dve.tensor_scalar(oh[:], iota, column(C, C_WBASE + w), column(k["DST"], t + j), ALU.add,
                                       ALU.is_equal), 1)
                dve.sem_inc(oh_ready, 1)
                then(dve.tensor_scalar(pen[:], oh[:], -1.0, FAR, ALU.add, ALU.mult), 2)
                dve.wait_ge(turned, v + 1)
                dve.tensor_copy(oht[:], pT[:, 0:P]).then_inc(oht_ready, 1)
                dve.wait_ge(kv_in, 16 * v + 16)
                dve.wait_ge(q_ready, v + 1)
                then(dve.tensor_tensor(prod[:], kv[:, 0:D], pQ[:, 0:D], ALU.mult), 3)
                then(dve.tensor_reduce(score[:], prod[:].rearrange("p (h c) -> p h c", c=HD), AX.X, ALU.add), 4)
                then(dve.tensor_scalar(score[:], score[:], 1.0 / math.sqrt(HD), column(k["BIAS"], t + j), ALU.mult,
                                       ALU.add), 5)
                then(dve.tensor_scalar(score[:], score[:], k["SHIFT"][:, 0:1], None, ALU.add), 6)
                wide = [P, HEADS, P]
                dve.tensor_tensor(cand[:], pen[:].unsqueeze(1).to_broadcast(wide),
                                  score[:].unsqueeze(2).to_broadcast(wide), ALU.add).then_inc(cand_ready, 1)
                dve.wait_ge(cand_turned, v + 1)
                dve.tensor_reduce(best[:, 0:4], pC[0][:], AX.X, ALU.max)
                then(dve.tensor_reduce(best[:, 4:8], pC[1][:], AX.X, ALU.max), 7)
                then(dve.tensor_tensor(most[:, at(w), :], most[:, at(w), :], best[:].unsqueeze(1), ALU.max), 8)
                dve.sem_inc(tile_done, 1)

            dve.sem_inc(tile_done, 1)
            dve.memset(most[:], -FAR).then_inc(step, 1)
            dve.wait_ge(step, 1)
            dve.sem_inc(step, -1)
            over_edge_tiles(dve, tile)
            dve.tensor_scalar(QX[:, :, D:VW], most[:], -1.0, k["FLAG"][:, 0:1], ALU.mult, ALU.mult)

        @block.tensor
        def _(pe):
            def tile(v, g, j):
                w, = table_values(nc, mybir.EngineType.PE, k["GROUPS"], 2 * g + 1, [NT])
                pe.wait_ge(oh_ready, v + 1)
                pe.transpose(pT[:, 0:P], oh[:], ident).then_inc(turned, 1)
                pe.wait_ge(oht_ready, v + 1)
                pe.matmul(pQ[:, 0:D], oht[:], QX[:, at(w), 0:D].squeeze(1), start=True, stop=True).then_inc(q_ready, 1)
                pe.wait_ge(cand_ready, v + 1)
                for h in range(HEADS):
                    mm = pe.transpose(pC[h // 4][:, h % 4, :], cand[:, h, :], ident)
                mm.then_inc(cand_turned, 1)

            over_edge_tiles(pe, tile)


def attention_out(k):
    nc, a, C, X, ACC, R, ST = k["nc"], k["a"], k["C"], k["X"], k["ACC"], k["R"], k["ST"]
    ident = C[:, C_IDENT:C_IDENT + P]
    with ExitStack() as s:
        def sb(name, shape, dt=F32):
            return s.enter_context(nc.sbuf_tensor(name, shape, dt))

        def sem(name):
            return s.enter_context(nc.semaphore(name))

        w, bp = sb("proj_w", [P, KD, D]), sb("proj_b", [P, D])
        rec = sb("inv_weights", [P, NT + 1, HEADS])
        o = [sb(f"attn_rows{b}", [P, D]) for b in range(2)]
        oT = [sb(f"attn_turned{b}", [P, KD, P]) for b in range(2)]
        part = [sb(f"proj_part{b}", [P, D]) for b in range(2)]
        pT = [s.enter_context(nc.psum_tensor(f"p_attn_turned{b}", [P, 4, P], F32)) for b in range(2)]
        pO = [s.enter_context(nc.psum_tensor(f"p_proj{b}", [P, 4 * P], F32)) for b in range(2)]
        w_in, step_done, o_ready, turned = sem("proj_w_in"), sem("rec_step"), sem("attn_ready"), sem("attn_turned")
        oT_ready, mm_done, part_ready, r_ready = (sem("attn_t_ready"), sem("proj_done"), sem("part_ready"),
                                                  sem("r_ready"))
        records = store_records(k, s, 1)
        block = s.enter_context(nc.Block())

        @block.gpsimd
        def _(pool):
            records(pool)

        @block.sync
        def _(sp):
            sp.dma_start(w[:], a["w_p"]).then_inc(w_in, 16)
            sp.dma_start(bp[:], a["rows0"][:, 0, :]).then_inc(w_in, 16)

        @block.vector
        def _(dve):
            link = Chain(dve, step_done)
            link(dve.tensor_scalar(rec[:], ACC[:, :, D:VW], 1e-37, None, ALU.max))
            link(dve.reciprocal(rec[:], rec[:]))

            def divide(n, b):
                wait_if(dve, turned, n - 1)
                dve.tensor_tensor(o[b][:].unsqueeze(1).rearrange("p o (h c) -> p o h c", c=HD),
                                  ACC[:, at(n), 0:D].rearrange("p o (h c) -> p o h c", c=HD),
                                  rec[:, at(n), :].unsqueeze(3).to_broadcast([P, 1, HEADS, HD]),
                                  ALU.mult).then_inc(o_ready, 1)

            def step(n, b, i, first, last):
                if not last:
                    divide(n + 2, b)
                dve.wait_ge(mm_done, n + 1)
                dve.scalar_tensor_tensor(out=part[b][:].unsqueeze(1), in0=X[:, at(n), :], scalar=column(k["RSTD"], n),
                                         in1=pO[b][:, 0:D].unsqueeze(1), op0=ALU.mult,
                                         op1=ALU.add).then_inc(part_ready, 1)
                dve.wait_ge(part_ready, n + 1)
                dve.scalar_tensor_tensor(out=R[:, at(n), :], in0=part[b][:].unsqueeze(1), scalar=column(k["NMR"], n),
                                         in1=bp[:].unsqueeze(1), op0=ALU.add, op1=ALU.add).then_inc(r_ready, 1)
                dve.wait_ge(r_ready, n + 1)
                dve.bn_stats(ST[:, at(n), :], R[:, at(n), :])

            divide(0, 0)
            divide(1, 1)
            dve.wait_ge(w_in, 32)
            over_tiles(dve, step)

        @block.scalar
        def _(act):
            def step(n, b, i, first, last):
                act.wait_ge(turned, n + 1)
                wait_if(act, mm_done, n - 1)
                act.copy(oT[b][:], pT[b][:, 0:KD, :]).then_inc(oT_ready, 1)

            over_tiles(act, step)

        @block.tensor
        def _(pe):
            def turn(n, b):
                pe.wait_ge(o_ready, n + 1)
                wait_if(pe, oT_ready, n - 1)
                for c in range(KD):
                    mm = pe.transpose(pT[b][:, c, :], o[b][:, c * P:(c + 1) * P], ident)
                mm.then_inc(turned, 1)

            def step(n, b, i, first, last):
                if not last:
                    turn(n + 1, 1 - b)
                pe.wait_ge(oT_ready, n + 1)
                wait_if(pe, part_ready, n - 1)
                for c in range(KD):
                    mm = pe.matmul(pO[b][:, 0:D], oT[b][:, c, :], w[:, c, :], start=(c == 0), stop=(c == KD - 1))
                mm.then_inc(mm_done, 1)

            turn(0, 0)
            pe.wait_ge(w_in, 32)
            over_tiles(pe, step)


def mlp_blocks(k, name, hidden, experts, affine):
    nc, a, C, R, ST = k["nc"], k["a"], k["C"], k["R"], k["ST"]
    ident = C[:, C_IDENT:C_IDENT + P]
    HC, BR = hidden // P, BT // P
    W1, W2 = 0, KD * hidden
    B1 = W2 + HC * D
    G, B, B2 = B1 + HC, B1 + HC + KD, B1 + HC + 2 * KD
    SIZE = B2 + D
    NPK = 2 if experts else 1
    NH = 3
    BLOCKS = -(-NT // BR)
    with ExitStack() as s:
        def sb(what, shape, dt=F32):
            return s.enter_context(nc.sbuf_tensor(name + what, shape, dt))

        def sem(what):
            return s.enter_context(nc.semaphore(name + what))

        pack = k["PACK"] if experts else [sb("_weights", [P, SIZE])]
        rows = [sb(f"_rows{b}", [P, BR, D]) for b in range(2)]
        tT = [sb(f"_turned{b}", [P, KD, BT]) for b in range(2)]
        hid = [sb(f"_hidden{b}", [P, HC, BT]) for b in range(2)]
        y = [sb(f"_y{b}", [P, BR, D]) for b in range(2)]
        gb = None if experts else sb("_affine_rows", [P, 2, D])
        rest = [sb(f"_rest{b}", [P, SIZE - G]) for b in range(2)] if experts else None
        pT = s.enter_context(nc.psum_tensor(name + "p_turned", [P, KD, BT], F32))
        pH = [s.enter_context(nc.psum_tensor(f"{name}p_hidden{c}", [P, 4 * P], F32)) for c in range(NH)]
        pY = [[s.enter_context(nc.psum_tensor(f"{name}p_y{b}{r}", [P, 4 * P], F32)) for r in range(BR)]
              for b in range(2)]
        pack_in = k["PACK_IN"] if experts else [sem("_pack_in")]
        rows_in = [sem(f"_rows_in{b}") for b in range(2)]
        rows_ready, turned, tT_ready = sem("_rows_ready"), sem("_turned_done"), sem("_tt_ready")
        hidden_done, gelu_done, y_done = sem("_hidden_done"), sem("_gelu_done"), sem("_y_done")
        y_ready, y_out, fin = sem("_y_ready"), [sem(f"_y_out{b}") for b in range(2)], sem("_finish")
        rest_in = [sem(f"_rest_in{b}") for b in range(2)]
        gb_in, norm, scaled = sem("_gb_in"), sem("_norm"), sem("_scaled")
        tally = sem("_tally")
        part = {"ffn": 2, "experts0": 4}.get(name)
        records = part and store_records(k, s, part)
        block = s.enter_context(nc.Block())
        slots_in = a["slots_in"].rearrange("(j r p) d -> j p r d", p=P, r=BR)
        slots_out = a["slots_out"].rearrange("(j r p) d -> j p r d", p=P, r=BR)

        def over_blocks(eng, step):
            if experts:
                n = eng.value_load(k["EPAIRS"][0:1, 0:1], min_val=2, max_val=NBLK // 2)
                over_odd(eng, n, step)
                return n
            over_tiles(eng, step, BLOCKS)

        @block.sync
        def _(sp):
            if not experts:
                sp.dma_start(gb[:], a["rows0"][:, 1:3, :]).then_inc(gb_in, 16)
                sp.dma_start(pack[0][:], a["ffn"][0]).then_inc(pack_in[0], 16)
                return

            def load_rows(j, b, used):
                wait_if(sp, turned, used)
                sp.sem_inc(tally, 1)
                sp.dma_start(rows[b][:], slots_in[at(j)].squeeze(0)).then_inc(rows_in[b], 16)
                e, = table_values(nc, mybir.EngineType.SP, k["BLOCKEXP"], j, [NEXP - 1])
                return e

            def load_rest(e, b):
                sp.dma_start(rest[b][:], a[name][at(e), :, G:SIZE].squeeze(0)).then_inc(rest_in[b], 16)

            def store(j, b, ready):
                sp.wait_ge(y_ready, ready)
                sp.sem_inc(tally, 1)
                sp.dma_start(slots_out[at(j)].squeeze(0), y[b][:]).then_inc(y_out[b], 16)

            def step(j, b, i, first, last):
                e = load_rows(j, b, j - 1)
                if not first:
                    sp.wait_ge(y_done, j - 1)
                    sp.sem_inc(tally, 1)
                    sp.dma_start(pack[b][:, 0:G], a[name][at(e), :, 0:G].squeeze(0)).then_inc(pack_in[b], 16)
                    store(j - 2, b, j - 1)
                load_rest(e, b)

            n = over_blocks(sp, step)
            e = load_rows(2 * n + 1, 1, 2 * n)
            store(2 * n - 1, 1, 2 * n)
            load_rest(e, 1)
            store(2 * n, 0, 2 * n + 1)
            for landed, count in [(y_out[0], n + 1), (y_out[1], n), (rows_in[0], n + 1), (rows_in[1], n + 1),
                                  (rest_in[0], n + 1), (rest_in[1], n + 1)]:
                sp.wait_ge(landed, 16 * count)
                sp.sem_inc(tally, 1)

        if records:
            @block.gpsimd
            def _(pool):
                records(pool)

        @block.vector
        def _(dve):
            def prepare(j, b):
                if not experts:
                    wait_if(dve, fin, j - 1)
                    for r in range(BR):
                        ins = normalise(dve, k, rows[b][:, r, :].unsqueeze(1), R[:, at(BR * j + r), :], BR * j + r)
                    ins.then_inc(norm, 1)
                    dve.wait_ge(norm, j + 1)
                    wide = [P, BR, D]
                    dve.tensor_tensor(rows[b][:], rows[b][:], gb[:, 0, :].unsqueeze(1).to_broadcast(wide),
                                      ALU.mult).then_inc(scaled, 1)
                    dve.wait_ge(scaled, j + 1)
                    dve.tensor_tensor(rows[b][:], rows[b][:], gb[:, 1, :].unsqueeze(1).to_broadcast(wide),
                                      ALU.add).then_inc(rows_ready, 1)

            def copy_turned(j, b):
                dve.wait_ge(turned, j + 1)
                wait_if(dve, hidden_done, HC * (j - 1))
                if affine:
                    dve.wait_ge(rest_in[b], 16 * (half[0] + 1))
                    for c in range(KD):
                        ins = dve.tensor_scalar(tT[b][:, c, :], pT[:, c, :], rest[b][:, c:c + 1],
                                                rest[b][:, KD + c:KD + c + 1], ALU.mult, ALU.add)
                else:
                    ins = dve.tensor_copy(tT[b][:], pT[:])
                ins.then_inc(tT_ready, 1)

            def step(j, b, i, first, last):
                if not last:
                    prepare(j + 1, 1 - b)
                    half[0] = i + b
                    copy_turned(j + 1, 1 - b)
                dve.wait_ge(y_done, j + 1)
                bias2 = rest[b][:, B2 - G:] if experts else pack[0][:, B2:]
                if experts:
                    dve.wait_ge(rest_in[b], 16 * (i + 1))
                    wait_if(dve, y_out[b], 16 * i if not first else 0)
                    for r in range(BR):
                        ins = dve.tensor_tensor(y[b][:, r, :], pY[b][r][:, 0:D], bias2, ALU.add)
                    ins.then_inc(y_ready, 1)
                else:
                    for r in range(BR):
                        ins = dve.tensor_tensor(y[b][:, r, :], pY[b][r][:, 0:D], rows[b][:, r, :], ALU.add)
                    ins.then_inc(y_ready, 1)
                    dve.wait_ge(y_ready, j + 1)
                    dve.tensor_tensor(R[:, at(BR * j, BR), :], y[b][:], bias2.unsqueeze(1).to_broadcast([P, BR, D]),
                                      ALU.add).then_inc(fin, 1)
                    dve.wait_ge(fin, j + 1)
                    for r in range(BR):
                        dve.bn_stats(ST[:, at(BR * j + r), :], R[:, at(BR * j + r), :])

            half = [0]
            if not experts:
                dve.wait_ge(gb_in, 16)
            prepare(0, 0)
            copy_turned(0, 0)
            if not experts:
                dve.wait_ge(pack_in[0], 16)
            over_blocks(dve, step)

        @block.scalar
        def _(act):
            def step(j, b, i, first, last):
                if not first:
                    act.wait_ge(y_done, j - 1)
                for h in range(HC):
                    c = h % NH
                    act.wait_ge(hidden_done, HC * j + h + 1)
                    act.activation(hid[b][:, h, :], pH[c][:, 0:BT], ACT.Gelu,
                                   bias=pack[b % NPK][:, B1 + h:B1 + h + 1]).then_inc(gelu_done, 1)

            act.activation(y[0][:, 0, 0:1], k["EPSC"][:], ACT.Gelu)
            over_blocks(act, step)

        @block.tensor
        def _(pe):
            def turn(j, b):
                if experts:
                    pe.wait_ge(rows_in[b], 16 * (half[0] + 1))
                else:
                    pe.wait_ge(rows_ready, j + 1)
                wait_if(pe, tT_ready, j)
                for r in range(BR):
                    for c in range(KD):
                        mm = pe.transpose(pT[:, c, r * P:(r + 1) * P], rows[b][:, r, c * P:(c + 1) * P], ident)
                mm.then_inc(turned, 1)

            def step(j, b, i, first, last):
                w = pack[b % NPK]
                if experts:
                    pe.wait_ge(pack_in[b], 16 * (i + 1))
                pe.wait_ge(tT_ready, j + 1)
                for h in range(HC):
                    c = h % NH
                    wait_if(pe, gelu_done, HC * j + h + 1 - (NH if h >= NH else 0) - (0 if h >= NH else h + 1))
                    for d in range(KD):
                        lo = W1 + d * hidden + h * P
                        mm = pe.matmul(pH[c][:, 0:BT], w[:, lo:lo + P], tT[b][:, d, :], start=(d == 0),
                                       stop=(d == KD - 1))
                    mm.then_inc(hidden_done, 1)
                if not last:
                    half[0] = i + b
                    turn(j + 1, 1 - b)
                wait_if(pe, y_ready, j - 1)
                for h in range(HC):
                    pe.wait_ge(gelu_done, HC * j + h + 1)
                    for r in range(BR):
                        mm = pe.matmul(pY[b][r][:, 0:D], hid[b][:, h, r * P:(r + 1) * P],
                                       w[:, W2 + h * D:W2 + (h + 1) * D], start=(h == 0), stop=(h == HC - 1))
                mm.then_inc(y_done, 1)

            half = [0]
            turn(0, 0)
            if not experts:
                pe.wait_ge(pack_in[0], 16)
            over_blocks(pe, step)


def ffn(k):
    nc, a, X, R, ST = k["nc"], k["a"], k["X"], k["R"], k["ST"]
    finish_ln(k, "1")
    mlp_blocks(k, "ffn", FFN, False, False)
    finish_ln(k, "2")
    with ExitStack() as s:
        gb = s.enter_context(nc.sbuf_tensor("ln2_rows", [P, 2, D], F32))
        gb_in, normed = s.enter_context(nc.semaphore("ln2_rows_in")), s.enter_context(nc.semaphore("normed"))
        step_done, x_ready = s.enter_context(nc.semaphore("ffn_step")), s.enter_context(nc.semaphore("ffn_x_ready"))
        b_added = s.enter_context(nc.semaphore("ln2_b_added"))
        block = s.enter_context(nc.Block())
        CH = 5
        chunks_ = [(c, slice(CH * c, CH * c + CH)) for c in range(NT // CH)]
        wide = [P, CH, D]

        @block.sync
        def _(sp):
            sp.dma_start(gb[:], a["rows0"][:, 3:5, :]).then_inc(gb_in, 16)

        @block.scalar
        def _(act):
            for c, part in chunks_:
                for n in range(part.start, part.stop):
                    ins = act.activation(R[:, n, :], R[:, n, :], ACT.Identity, bias=k["NMR"][:, n:n + 1],
                                         scale=k["RSTD"][:, n:n + 1])
                ins.then_inc(normed, 1)

        @block.gpsimd
        def _(pool):
            pool.wait_ge(gb_in, 16)
            for c, part in chunks_:
                pool.tensor_tensor(X[:, part, :], X[:, part, :], gb[:, 1:2, :].to_broadcast(wide),
                                   ALU.add).then_inc(b_added, 1)

        @block.vector
        def _(dve):
            link = Chain(dve, step_done)
            dve.wait_ge(gb_in, 16)
            for c, part in chunks_:
                dve.wait_ge(normed, c + 1)
                link(dve.tensor_tensor(R[:, part, :], R[:, part, :], gb[:, 0:1, :].to_broadcast(wide), ALU.mult))
                dve.wait_ge(b_added, c + 1)
                dve.tensor_tensor(X[:, part, :], X[:, part, :], R[:, part, :], ALU.add).then_inc(x_ready, 1)
                dve.wait_ge(x_ready, c + 1)
                for n in range(part.start, part.stop):
                    dve.bn_stats(ST[:, n, :], X[:, n, :])
    finish_ln(k, "3")


def moe_route(k, layer):
    nc, a, C, X = k["nc"], k["a"], k["C"], k["X"]
    ident, tri, ones = (C[:, c:c + P] for c in (C_IDENT, C_TRI, C_ONES))
    byexp, bytok = [P, NT, NEXP], [P, NEXP, NT]
    tag = f"route{layer}_"
    with ExitStack() as s:
        def sb(name, shape, dt=F32):
            return s.enter_context(nc.sbuf_tensor(tag + name, shape, dt))

        def sem(name):
            return s.enter_context(nc.semaphore(tag + name))

        router, rbias = sb("w", [P, KD, NEXP]), sb("b", [P, NT * NEXP])
        tok = [sb(f"tok{b}", [P, D]) for b in range(2)]
        tT = [sb(f"tok_turned{b}", [P, KD, P]) for b in range(2)]
        lg, prob, cand, hit1, hit2 = (sb(n, byexp) for n in ("logits", "prob", "cand", "hit1", "hit2"))
        top = sb("top", [P, NT])
        m1, m2, rank, wsum = (sb(n, [P, NT]) for n in ("first", "second", "rank", "wsum"))
        member, cum, slot = sb("member", bytok), sb("running", bytok), sb("slot", byexp)
        ends, cnt, pre, adj = sb("ends", [P, NEXP + 1]), sb("cnt", [P, NEXP]), sb("pre", [P, NEXP]), sb("adj", [P, NEXP])
        blki, blk, binc, nought = sb("blk_i", [P, NEXP], I32), sb("blk", [P, NEXP]), sb("blk_inc", [P, NEXP]), sb("zero", [P, NEXP])
        where = sb("where", [P, NT, TOPK])
        past, expert, pairs = sb("past", [1, NBLK + 2, NEXP - 1]), sb("expert", [1, NBLK + 2]), sb("pairs", [1, 1], I32)
        pT = [s.enter_context(nc.psum_tensor(f"{tag}p_turned{b}", [P, 4, P], F32)) for b in range(2)]
        pL = [s.enter_context(nc.psum_tensor(f"{tag}p_logits{b}", [P, 4 * P], F32)) for b in range(2)]
        pPre = s.enter_context(nc.psum_tensor(tag + "p_prefix", [P, NEXP], F32))
        pTot = s.enter_context(nc.psum_tensor(tag + "p_total", [P, NEXP], F32))
        w_in, tok_ready, turned, tT_ready = sem("w_in"), sem("tok_ready"), sem("turned"), sem("tt_ready")
        mm_done, lg_ready, step_done = sem("mm_done"), sem("lg_ready"), sem("step")
        diff_ready, exp_ready, cnt_ready, sums_ready = (sem("diff_ready"), sem("exp_ready"), sem("cnt_ready"),
                                                        sem("sums_ready"))
        records = store_records(k, s, 3) if layer == 0 else None
        block = s.enter_context(nc.Block())

        if records:
            @block.gpsimd
            def _(pool):
                records(pool)

        @block.sync
        def _(sp):
            sp.dma_start(router[:], a[f"router{layer}"]).then_inc(w_in, 16)
            if layer == 1:
                sp.dma_start(rbias[:], a["rbias1"]).then_inc(w_in, 16)

        @block.vector
        def _(dve):
            def token(n, b):
                wait_if(dve, turned, n - 1)
                normalise(dve, k, tok[b][:].unsqueeze(1), X[:, at(n), :], n).then_inc(tok_ready, 1)

            def step(n, b, i, first, last):
                if not last:
                    token(n + 2, b)
                dve.wait_ge(mm_done, n + 1)
                dve.tensor_copy(lg[:, at(n), :], pL[b][:, 0:NEXP].unsqueeze(1)).then_inc(lg_ready, 1)

            def wide(v):
                return v.unsqueeze(2).to_broadcast(byexp)

            dve.memset(nought[:], 0.0)
            dve.memset(ends[:], 0.0)
            token(0, 0)
            token(1, 1)
            over_tiles(dve, step)
            link = Chain(dve, step_done)
            dve.wait_ge(lg_ready, NT)
            if layer == 1:
                dve.wait_ge(w_in, 32)
                link(dve.tensor_tensor(lg[:].rearrange("p t e -> p (t e)"), lg[:].rearrange("p t e -> p (t e)"),
                                       rbias[:], ALU.add))
                link(dve.tensor_tensor(k["NMR2"][:], k["RSTD"][:], k["RSTD"][:], ALU.mult))
                link(dve.tensor_tensor(k["RSTD2"][:], k["NMR2"][:], k["VAR"][:], ALU.mult))
            link(dve.tensor_reduce(top[:], lg[:], AX.X, ALU.max))
            dve.tensor_tensor(lg[:], lg[:], wide(top[:]), ALU.subtract).then_inc(diff_ready, 1)
            dve.wait_ge(exp_ready, 1)
            link(dve.tensor_reduce(wsum[:], prob[:], AX.X, ALU.add))
            link(dve.reciprocal(wsum[:], wsum[:]))
            link(dve.tensor_tensor(prob[:], prob[:], wide(wsum[:]), ALU.mult))
            ranks = C[:, C_RANK:C_RANK + NT * NEXP].rearrange("p (t e) -> p t e", e=NEXP)
            for m, hit in ((m1, hit1), (m2, hit2)):
                link(dve.tensor_reduce(m[:], prob[:], AX.X, ALU.max))
                link(dve.tensor_tensor(cand[:], prob[:], wide(m[:]), ALU.is_equal))
                link(dve.tensor_tensor(cand[:], cand[:], ranks, ALU.mult))
                link(dve.tensor_reduce(rank[:], cand[:], AX.X, ALU.max))
                link(dve.tensor_tensor(hit[:], ranks, wide(rank[:]), ALU.is_equal))
                if hit is hit1:
                    link(dve.scalar_tensor_tensor(out=prob[:], in0=hit[:], scalar=-2.0, in1=prob[:], op0=ALU.mult,
                                                  op1=ALU.add))
            link(dve.tensor_tensor(wsum[:], m1[:], m2[:], ALU.add))
            link(dve.tensor_scalar(wsum[:], wsum[:], 1e-12, None, ALU.max))
            link(dve.reciprocal(wsum[:], wsum[:]))
            link(dve.tensor_tensor(k["W12"][:, :, 0], m1[:], wsum[:], ALU.mult))
            link(dve.tensor_tensor(k["W12"][:, :, 1], m2[:], wsum[:], ALU.mult))
            for hit in (hit1, hit2):
                link(dve.tensor_tensor(hit[:], hit[:], wide(C[:, C_VALID:C_VALID + NT]), ALU.mult))
            link(dve.tensor_tensor(member[:].rearrange("p e t -> p t e"), hit1[:], hit2[:], ALU.add))
            link(dve.tensor_tensor_scan(cum[:].rearrange("p e t -> p (e t)"), member[:].rearrange("p e t -> p (e t)"),
                                        nought[:, 0:1].to_broadcast([P, NEXP * NT]), 0.0, ALU.add, ALU.add))
            link(dve.tensor_copy(ends[:, 1:NEXP + 1], cum[:, :, NT - 1]))
            dve.tensor_tensor(cnt[:], ends[:, 1:NEXP + 1], ends[:, 0:NEXP], ALU.subtract).then_inc(cnt_ready, 1)
            dve.wait_ge(sums_ready, 1)
            link(dve.tensor_copy(pre[:], pPre[:]))
            link(dve.tensor_scalar(blki[:], pTot[:], float(BT - 1), None, ALU.add))
            link(dve.tensor_scalar(blki[:], blki[:], BT.bit_length() - 1, None, ALU.arith_shift_right))
            link(dve.tensor_copy(blk[:], blki[:]))
            link(dve.tensor_tensor_scan(binc[:], blk[:], nought[:], 0.0, ALU.add, ALU.add))
            link(dve.tensor_tensor(adj[:], binc[:], blk[:], ALU.subtract))
            link(dve.scalar_tensor_tensor(out=adj[:], in0=adj[:], scalar=float(BT), in1=pre[:], op0=ALU.mult,
                                          op1=ALU.add))
            link(dve.scalar_tensor_tensor(out=adj[:], in0=adj[:], scalar=-1.0, in1=ends[:, 0:NEXP], op0=ALU.add,
                                          op1=ALU.subtract))
            link(dve.tensor_tensor(slot[:], cum[:].rearrange("p e t -> p t e"),
                                   adj[:].unsqueeze(1).to_broadcast(byexp), ALU.add))
            for j, hit in ((0, hit1), (1, hit2)):
                link(dve.tensor_tensor(hit[:], hit[:], slot[:], ALU.mult))
                link(dve.tensor_reduce(where[:, :, j], hit[:], AX.X, ALU.add))
            link(dve.tensor_tensor(k["SLOT"][:], where[:],
                                   C[:, C_TRASH:C_TRASH + NT * TOPK].rearrange("p (t j) -> p t j", j=TOPK), ALU.add))
            shape = [1, NBLK + 2, NEXP - 1]
            link(dve.tensor_tensor(past[:], binc[0:1, 0:NEXP - 1].unsqueeze(1).to_broadcast(shape),
                                   C[0:1, C_COUNT:C_COUNT + NBLK + 2].unsqueeze(2).to_broadcast(shape), ALU.is_le))
            link(dve.tensor_reduce(expert[:], past[:], AX.X, ALU.add))
            link(dve.tensor_copy(k["BLOCKEXP"][:], expert[:]))
            link(dve.tensor_copy(pairs[:], binc[0:1, NEXP - 1:NEXP]))
            link(dve.tensor_scalar(k["EPAIRS"][:], pairs[:], 1, None, ALU.arith_shift_right))

        @block.scalar
        def _(act):
            def step(n, b, i, first, last):
                act.wait_ge(turned, n + 1)
                wait_if(act, mm_done, n - 1)
                act.copy(tT[b][:], pT[b][:, 0:KD, :]).then_inc(tT_ready, 1)

            over_tiles(act, step)
            act.wait_ge(diff_ready, 1)
            act.activation(prob[:], lg[:], ACT.Exp).then_inc(exp_ready, 1)

        @block.tensor
        def _(pe):
            def turn(n, b):
                pe.wait_ge(tok_ready, n + 1)
                wait_if(pe, tT_ready, n - 1)
                for c in range(KD):
                    mm = pe.transpose(pT[b][:, c, :], tok[b][:, c * P:(c + 1) * P], ident)
                mm.then_inc(turned, 1)

            def step(n, b, i, first, last):
                if not last:
                    turn(n + 1, 1 - b)
                pe.wait_ge(tT_ready, n + 1)
                wait_if(pe, lg_ready, n - 1)
                for c in range(KD):
                    mm = pe.matmul(pL[b][:, 0:NEXP], tT[b][:, c, :], router[:, c, :], start=(c == 0),
                                   stop=(c == KD - 1))
                mm.then_inc(mm_done, 1)

            turn(0, 0)
            pe.wait_ge(w_in, 16 * (1 + layer))
            over_tiles(pe, step)
            pe.wait_ge(cnt_ready, 1)
            pe.matmul(pPre[:], tri, cnt[:], start=True, stop=True)
            pe.matmul(pTot[:], ones, cnt[:], start=True, stop=True).then_inc(sums_ready, 1)


def second_ln(k):
    nc = k["nc"]
    with ExitStack() as s:
        std = s.enter_context(nc.sbuf_tensor("std2", [P, NT + 1], F32))
        std_ready, step = s.enter_context(nc.semaphore("std2_ready")), s.enter_context(nc.semaphore("ln2_step"))
        block = s.enter_context(nc.Block())

        @block.scalar
        def _(act):
            act.activation(std[:], k["RSTD2"][:], ACT.Sqrt, bias=k["EPSC"][:, 0:1]).then_inc(std_ready, 1)

        @block.vector
        def _(dve):
            link = Chain(dve, step)
            dve.wait_ge(std_ready, 1)
            link(dve.reciprocal(std[:], std[:]))
            link(dve.tensor_tensor(k["RSTD2"][:], k["RSTD"][:], std[:], ALU.mult))
            link(dve.tensor_tensor(k["NMR2"][:], k["NMR"][:], std[:], ALU.mult))


def moe_scatter(k, layer):
    nc, a, X = k["nc"], k["a"], k["X"]
    rstd, nmr = (k["RSTD2"], k["NMR2"]) if layer else (k["RSTD"], k["NMR"])
    tag = f"scatter{layer}_"
    with ExitStack() as s:
        def sem(name):
            return s.enter_context(nc.semaphore(tag + name))

        rows = [s.enter_context(nc.sbuf_tensor(f"{tag}rows{b}", [P, D], F32)) for b in range(2)]
        idx = [s.enter_context(nc.sbuf_tensor(f"{tag}idx{b}", [P, TOPK], I32)) for b in range(2)]
        rows_ready, idx_ready, tally = sem("rows_ready"), sem("idx_ready"), sem("tally")
        stored = [k[f"scattered{layer}_{b}"] for b in range(2)]
        block = s.enter_context(nc.Block())

        @block.sync
        def _(sp):
            for b in range(2):
                e, = table_values(nc, mybir.EngineType.SP, k["BLOCKEXP"], b, [NEXP - 1])
                sp.dma_start(k["PACK"][b][:], a[f"experts{layer}"][at(e)].squeeze(0)).then_inc(k["PACK_IN"][b], 16)

        @block.vector
        def _(dve):
            def step(n, b, i, first, last):
                if not first:
                    dve.wait_ge(stored[b], 32 * i)
                dve.tensor_scalar(rows[b][:].unsqueeze(1), X[:, at(n), :], column(rstd, n), column(nmr, n), ALU.mult,
                                  ALU.add).then_inc(rows_ready, 1)

            over_tiles(dve, step)

        @block.gpsimd
        def _(pool):
            def step(n, b, i, first, last):
                if not first:
                    pool.wait_ge(stored[b], 32 * i)
                pool.wait_ge(rows_ready, n + 1)
                pool.sem_inc(tally, 1)
                pool.tensor_copy(idx[b][:].unsqueeze(1), k["SLOT"][:, at(n), :]).then_inc(idx_ready, 1)
                pool.wait_ge(idx_ready, n + 1)
                pool.sem_inc(tally, 1)
                for j in range(TOPK):
                    pool.indirect_dma_start(a["slots_in"], bass.IndirectOffsetOnAxis(ap=idx[b][:, j:j + 1], axis=0),
                                            rows[b][:], None).then_inc(stored[b], 16)

            over_tiles(pool, step)
            pool.wait_ge(stored[0], 32 * ((NT + 1) // 2))
            pool.wait_ge(stored[1], 32 * (NT // 2))


def moe_combine(k, layer):
    nc, a, X, ST = k["nc"], k["a"], k["X"], k["ST"]
    tag = f"combine{layer}_"
    with ExitStack() as s:
        def sem(name):
            return s.enter_context(nc.semaphore(tag + name))

        y = [s.enter_context(nc.sbuf_tensor(f"{tag}y{b}", [P, TOPK, D], F32)) for b in range(4)]
        idx = [s.enter_context(nc.sbuf_tensor(f"{tag}idx{b}", [P, TOPK], I32)) for b in range(4)]
        sums = [s.enter_context(nc.sbuf_tensor(f"{tag}sum{b}", [P, TOPK, D], F32)) for b in range(4)]
        rstd1 = s.enter_context(nc.sbuf_tensor(tag + "rstd1", [P, NT + 1], F32))
        idx_ready, tally, r_ready = sem("idx_ready"), sem("tally"), sem("r_ready")
        first_done, second_done, x_ready = sem("first_done"), sem("second_done"), sem("x_ready")
        y_in, stored = [k[f"y_in{layer}_{b}"] for b in range(4)], sem("stored")
        block = s.enter_context(nc.Block())

        @block.gpsimd
        def _(pool):
            def step(n, b, i, first, last):
                wait_if(pool, second_done, n - 3)
                pool.sem_inc(tally, 1)
                pool.tensor_copy(idx[b][:].unsqueeze(1), k["CSLOT"][:, at(n), :]).then_inc(idx_ready, 1)
                pool.wait_ge(idx_ready, n + 1)
                pool.sem_inc(tally, 1)
                for j in range(TOPK):
                    pool.indirect_dma_start(y[b][:, j, :], None, a["slots_out"], bass.IndirectOffsetOnAxis(
                        ap=idx[b][:, j:j + 1], axis=0)).then_inc(y_in[b], 16)

            pool.wait_ge(r_ready, 2)
            over_tiles_by_four(pool, step)

        @block.vector
        def _(dve):
            def step(n, b, i, first, last):
                dve.wait_ge(y_in[b], 32 * (i + 1))
                w = [k["W12"][:, at(n), j] for j in range(TOPK)]
                dve.scalar_tensor_tensor(out=sums[b][:, 0, :], in0=y[b][:, 0, :], scalar=w[0],
                                         in1=X[:, at(n), :].squeeze(1), op0=ALU.mult, op1=ALU.add).then_inc(first_done, 1)
                dve.wait_ge(first_done, n + 1)
                out = X[:, at(n), :] if layer else sums[b][:, 1:2, :]
                dve.scalar_tensor_tensor(out=out, in0=y[b][:, 1:2, :], scalar=w[1], in1=sums[b][:, 0:1, :],
                                         op0=ALU.mult, op1=ALU.add).then_inc(second_done, 1)
                if layer == 0:
                    dve.wait_ge(second_done, n + 1)
                    dve.scalar_tensor_tensor(out=sums[b][:, 0:1, :], in0=X[:, at(n), :], scalar=column(k["RSTD"], n),
                                             in1=sums[b][:, 1:2, :], op0=ALU.mult, op1=ALU.add).then_inc(x_ready, 1)
                    dve.wait_ge(x_ready, 2 * n + 1)
                    dve.tensor_scalar(X[:, at(n), :], sums[b][:, 0:1, :], column(k["NMR"], n), None,
                                      ALU.add).then_inc(x_ready, 1)
                    dve.wait_ge(x_ready, 2 * n + 2)
                    dve.bn_stats(ST[:, at(n), :], X[:, at(n), :])

            trash = C_TRASH
            dve.tensor_scalar(k["CSLOT"][:], k["SLOT"][:], float(NSLOT), None, ALU.is_lt).then_inc(r_ready, 1)
            dve.wait_ge(r_ready, 1)
            dve.tensor_tensor(k["CSLOT"][:], k["CSLOT"][:], k["SLOT"][:], ALU.mult).then_inc(r_ready, 1)
            over_tiles_by_four(dve, step)

        if layer:
            @block.sync
            def _(sp):
                whole = N // P
                for lo in range(0, whole, 6):
                    hi = min(lo + 6, whole)
                    sp.wait_ge(second_done, hi)
                    sp.dma_start(a["out"][lo * P:hi * P, :].rearrange("(t p) d -> p t d", p=P),
                                 X[:, lo:hi, :]).then_inc(stored, 16)
                sp.wait_ge(second_done, NT)
                sp.dma_start(a["out"][whole * P:N, :], X[0:N - whole * P, NT - 1, :]).then_inc(stored, 16)
                sp.wait_ge(stored, 16 * (-(-whole // 6) + 1))


def moe(k, layer):
    nc = k["nc"]
    with ExitStack() as s:
        for name, shape, dt in (("W12", [P, NT, TOPK], F32), ("SLOT", [P, NT, TOPK], I32),
                                ("CSLOT", [P, NT, TOPK], I32), ("BLOCKEXP", [1, NBLK + 2], I32), ("EPAIRS", [1, 1], I32),
                                ("RSTD2", [P, NT + 1], F32), ("NMR2", [P, NT + 1], F32)):
            k[name] = s.enter_context(nc.sbuf_tensor(f"{name}_{layer}", shape, dt))
        moe_route(k, layer)
        if layer:
            second_ln(k)
        size = k["a"][f"experts{layer}"].shape[2]
        k["PACK"] = [s.enter_context(nc.sbuf_tensor(f"pack{layer}_{b}", [P, size], F32)) for b in range(2)]
        k["PACK_IN"] = [s.enter_context(nc.semaphore(f"pack_in{layer}_{b}")) for b in range(2)]
        moe_scatter(k, layer)
        mlp_blocks(k, f"experts{layer}", (D, FFN)[layer], True, layer == 1)
        moe_combine(k, layer)
        if layer == 0:
            finish_ln(k, "4")


RB = 8
RBATCH = (10, 6, 22, 6, 8)


def store_records(k, stack, part):
    nc, first = k["nc"], sum(RBATCH[:part])
    tag = f"records{part}_"
    idx = [stack.enter_context(nc.sbuf_tensor(f"{tag}idx{b}", [P, RB], I32)) for b in range(2)]
    rec = [stack.enter_context(nc.sbuf_tensor(f"{tag}rec{b}", [P, RB, 2], I32)) for b in range(2)]
    stored = [k[f"{tag}stored{b}"] for b in range(2)]
    copied, tally = stack.enter_context(nc.semaphore(tag + "copied")), stack.enter_context(nc.semaphore(tag + "tally"))

    def program(pool):
        def step(j, b, i, fresh, last):
            lo = RB * first + RB * j
            if not fresh:
                pool.wait_ge(stored[b], 16 * RB * i)
                pool.sem_inc(tally, 1)
            pool.tensor_copy(idx[b][:], k["SADDR"][:, at(lo, RB)]).then_inc(copied, 1)
            pool.tensor_copy(rec[b][:], k["EDGES"][:, at(lo, RB), :]).then_inc(copied, 1)
            pool.wait_ge(copied, 2 * j + 2)
            pool.sem_inc(tally, 1)
            for t in range(RB):
                pool.indirect_dma_start(k["a"]["records"], bass.IndirectOffsetOnAxis(ap=idx[b][:, t:t + 1], axis=0),
                                        rec[b][:, t, :], None).then_inc(stored[b], 16)

        over_pairs(pool, RBATCH[part] // 2, step)
        for b in range(2):
            pool.wait_ge(stored[b], 16 * RB * (RBATCH[part] // 2))

    return program


def gnn_rows(k):
    nc, a, X, R = k["nc"], k["a"], k["X"], k["R"]
    with ExitStack() as s:
        normed, stored = s.enter_context(nc.semaphore("gnn_normed")), s.enter_context(nc.semaphore("gnn_rows_stored"))
        recs_in = s.enter_context(nc.semaphore("records_in"))
        block = s.enter_context(nc.Block())
        xg = a["xg0"].rearrange("(t p) d -> p t d", p=P)

        @block.vector
        def _(dve):
            with dve.Fori(0, NT) as n:
                normalise(dve, k, R[:, at(n), :], X[:, at(n), :], n).then_inc(normed, 1)

        @block.sync
        def _(sp):
            for lo in range(0, NT, 5):
                sp.wait_ge(normed, lo + 5)
                sp.dma_start(xg[:, lo:lo + 5, :], R[:, lo:lo + 5, :]).then_inc(stored, 16)
            sp.dma_start(k["RECS"][:], a["records"][0:STILES * P, :].rearrange("(p t) two -> p t two",
                                                                               p=P)).then_inc(recs_in, 16)
            sp.wait_ge(stored, 16 * (NT // 5))

        @block.gpsimd
        def _(pool):
            pool.memset(k["AGG"][:], 0.0)
            pool.wait_ge(recs_in, 16)
            pool.tensor_copy(k["KEYS"][:], k["RECS"][:, :, 1])


def gnn_edges(k, layer):
    nc, a, C, AGG = k["nc"], k["a"], k["C"], k["AGG"]
    iota = C[:, C_IOTA:C_IOTA + P]
    HALF = STURN // 2
    BANKS, ONEHOTS = 4, 4
    width = D + 1 if layer == 0 else D
    tag = f"agg{layer}_"
    with ExitStack() as s:
        def sb(name, shape, dt=F32):
            return s.enter_context(nc.sbuf_tensor(tag + name, shape, dt))

        def sem(name):
            return s.enter_context(nc.semaphore(tag + name))

        recs, keys = k["RECS"], k["KEYS"]
        idx = [sb(f"idx{h}", [P, HALF], I32) for h in range(2)]
        rows = [sb(f"rows{r}", [P, D + 1]) for r in range(STURN)]
        oh = [sb(f"onehot{r}", [P, P]) for r in range(ONEHOTS)]
        pA = [s.enter_context(nc.psum_tensor(f"{tag}p{g}", [P, 4 * P], F32)) for g in range(BANKS)]
        idx_ready, tally = sem("idx_ready"), sem("tally")
        rows_in = [k[f"agg{layer}_rows_in{r}"] for r in range(HALF)]
        ones_ready, oh_ready, mm_done, acc_done = sem("ones_ready"), sem("oh_ready"), sem("mm_done"), sem("acc_done")
        block = s.enter_context(nc.Block())

        def over_turns(eng, step):
            step(0, True)
            n = eng.value_load(k["STURNS"][0:1, 0:1], min_val=2, max_val=STILES // STURN)
            with eng.Fori(1, n) as i:
                step(i, False)
            return n

        @block.gpsimd
        def _(pool):
            def step(i, first):
                for h in range(2):
                    if not first:
                        pool.wait_ge(mm_done, STURN * i - STURN + HALF * h + HALF)
                        pool.sem_inc(tally, 1)
                    pool.tensor_copy(idx[h][:], recs[:, at(STURN * i + HALF * h, HALF), 0]).then_inc(idx_ready, 1)
                    pool.wait_ge(idx_ready, 2 * i + h + 1)
                    pool.sem_inc(tally, 1)
                    for j in range(HALF):
                        r = HALF * h + j
                        pool.indirect_dma_start(rows[r][:, 0:D], None, a[f"xg{layer}"], bass.IndirectOffsetOnAxis(
                            ap=idx[h][:, j:j + 1], axis=0)).then_inc(rows_in[r // 2], 16)

            over_turns(pool, step)

        @block.vector
        def _(dve):
            def accumulate(t, slot, w):
                dve.wait_ge(mm_done, t + 1)
                dve.wait_ge(acc_done, t + 2)
                dve.tensor_tensor(AGG[:, at(w), 0:width], AGG[:, at(w), 0:width],
                                  pA[slot][:, 0:width].unsqueeze(1), ALU.add).then_inc(acc_done, 1)

            def step(i, first):
                lag = 2
                for h in range(4):
                    lo = STURN * i + 4 * h - lag
                    if first and h == 0:
                        ws = [None] * lag + table_values(nc, mybir.EngineType.DVE, k["SWIN"], 0, [NT] * (4 - lag))
                    else:
                        ws = table_values(nc, mybir.EngineType.DVE, k["SWIN"], lo, [NT] * 4)
                    for j in range(4):
                        r = 4 * h + j
                        wait_if(dve, mm_done, STURN * i + r + 1 - ONEHOTS)
                        dve.tensor_scalar(oh[r % ONEHOTS][:], iota, column(keys, STURN * i + r), None,
                                          ALU.is_equal).then_inc(oh_ready, 1)
                        if not (first and r < lag):
                            accumulate(STURN * i + r - lag, (r - lag) % BANKS, ws[j])

            dve.sem_inc(acc_done, 2)
            if layer == 0:
                for r in range(STURN):
                    ins = dve.memset(rows[r][:, D:D + 1], 1.0)
                ins.then_inc(ones_ready, 1)
            n = over_turns(dve, step)
            ws = table_values(nc, mybir.EngineType.DVE, k["SWIN"], STURN * n - 2, [NT] * 2)
            dve.wait_ge(mm_done, STURN * n)
            for slot, w in ((BANKS - 2, ws[0]), (BANKS - 1, ws[1])):
                dve.wait_ge(acc_done, STURN * n + slot - BANKS + 2)
                dve.tensor_tensor(AGG[:, at(w), 0:width], AGG[:, at(w), 0:width],
                                  pA[slot][:, 0:width].unsqueeze(1), ALU.add).then_inc(acc_done, 1)

        @block.tensor
        def _(pe):
            def step(i, first):
                for r in range(STURN):
                    if r % 2 == 0:
                        pe.wait_ge(rows_in[r // 2], 32 * i + 32)
                    pe.wait_ge(oh_ready, STURN * i + r + 1)
                    wait_if(pe, acc_done, STURN * i + r + 3 - BANKS)
                    pe.matmul(pA[r % BANKS][:, 0:width], oh[r % ONEHOTS][:], rows[r][:, 0:width], start=True,
                              stop=True).then_inc(mm_done, 1)

            if layer == 0:
                pe.wait_ge(ones_ready, 1)
            over_turns(pe, step)


def gnn_nodes(k, layer):
    nc, a, C, X, R, AGG, ST = k["nc"], k["a"], k["C"], k["X"], k["R"], k["AGG"], k["ST"]
    ident = C[:, C_IDENT:C_IDENT + P]
    tag = f"nodes{layer}_"
    with ExitStack() as outer:
        brows = outer.enter_context(nc.sbuf_tensor(tag + "brows", [P, 3, D], F32))
        with ExitStack() as s:
            def sb(name, shape, dt=F32):
                return s.enter_context(nc.sbuf_tensor(tag + name, shape, dt))

            def sem(name):
                return s.enter_context(nc.semaphore(tag + name))

            w, rec = sb("w", [P, KD, D]), sb("inv_degree", [P, NT + 1])
            z = [sb(f"z{b}", [P, D]) for b in range(2)]
            zT = [sb(f"z_turned{b}", [P, KD, P]) for b in range(2)]
            pT = [s.enter_context(nc.psum_tensor(f"{tag}p_turned{b}", [P, 4, P], F32)) for b in range(2)]
            pO = [s.enter_context(nc.psum_tensor(f"{tag}p_out{b}", [P, 4 * P], F32)) for b in range(2)]
            w_in, step_done, z_ready, turned = sem("w_in"), sem("step"), sem("z_ready"), sem("turned")
            zT_ready, mm_done, r_ready = sem("zt_ready"), sem("mm_done"), sem("r_ready")
            block = s.enter_context(nc.Block())

            @block.sync
            def _(sp):
                sp.dma_start(w[:], a[f"w_g{layer}"]).then_inc(w_in, 16)
                sp.dma_start(brows[:], a[f"rows_g{layer}"]).then_inc(w_in, 16)

            @block.vector
            def _(dve):
                link = Chain(dve, step_done)
                link(dve.tensor_scalar(rec[:], AGG[:, :, D], 1.0, None, ALU.max))
                link(dve.reciprocal(rec[:], rec[:]))

                def mean(n, b):
                    wait_if(dve, turned, n - 1)
                    dve.scalar_tensor_tensor(out=z[b][:].unsqueeze(1), in0=AGG[:, at(n), 0:D], scalar=column(rec, n),
                                             in1=R[:, at(n), :], op0=ALU.mult, op1=ALU.add).then_inc(z_ready, 1)

                def step(n, b, i, first, last):
                    if not last:
                        mean(n + 2, b)
                    dve.wait_ge(mm_done, n + 1)
                    dve.tensor_tensor(R[:, at(n), :], pO[b][:, 0:D].unsqueeze(1), brows[:, 0:1, :],
                                      ALU.add).then_inc(r_ready, 1)
                    dve.wait_ge(r_ready, n + 1)
                    dve.bn_stats(ST[:, at(n), :], R[:, at(n), :])

                mean(0, 0)
                mean(1, 1)
                dve.wait_ge(w_in, 32)
                over_tiles(dve, step)

            @block.scalar
            def _(act):
                def step(n, b, i, first, last):
                    act.wait_ge(turned, n + 1)
                    wait_if(act, mm_done, n - 1)
                    act.copy(zT[b][:], pT[b][:, 0:KD, :]).then_inc(zT_ready, 1)

                over_tiles(act, step)

            @block.tensor
            def _(pe):
                def turn(n, b):
                    pe.wait_ge(z_ready, n + 1)
                    wait_if(pe, zT_ready, n - 1)
                    for c in range(KD):
                        mm = pe.transpose(pT[b][:, c, :], z[b][:, c * P:(c + 1) * P], ident)
                    mm.then_inc(turned, 1)

                def step(n, b, i, first, last):
                    if not last:
                        turn(n + 1, 1 - b)
                    pe.wait_ge(zT_ready, n + 1)
                    wait_if(pe, r_ready, n - 1)
                    for c in range(KD):
                        mm = pe.matmul(pO[b][:, 0:D], zT[b][:, c, :], w[:, c, :], start=(c == 0), stop=(c == KD - 1))
                    mm.then_inc(mm_done, 1)

                turn(0, 0)
                pe.wait_ge(w_in, 32)
                over_tiles(pe, step)

        finish_ln(k, f"_gnn{layer}")
        with ExitStack() as s:
            def sem(name):
                return s.enter_context(nc.semaphore(tag + name))

            normed, scaled, shifted, silu_done = sem("normed"), sem("scaled"), sem("shifted"), sem("silu_done")
            x_ready, stored = sem("x_ready"), sem("stored")
            block = s.enter_context(nc.Block())
            CH = 5
            chunks_ = [(c, slice(CH * c, CH * c + CH)) for c in range(NT // CH)]

            @block.vector
            def _(dve):
                for c, part in chunks_:
                    dve.wait_ge(normed, c + 1)
                    dve.tensor_tensor(R[:, part, :], R[:, part, :], brows[:, 1:2, :].to_broadcast([P, CH, D]),
                                      ALU.mult).then_inc(scaled, 1)
                    dve.wait_ge(scaled, c + 1)
                    dve.tensor_tensor(R[:, part, :], R[:, part, :], brows[:, 2:3, :].to_broadcast([P, CH, D]),
                                      ALU.add).then_inc(shifted, 1)
                if layer == 1:
                    for c, part in chunks_:
                        dve.wait_ge(silu_done, c + 1)
                        dve.tensor_tensor(X[:, part, :], X[:, part, :], R[:, part, :], ALU.add).then_inc(x_ready, 1)
                        dve.wait_ge(x_ready, c + 1)
                        for n in range(part.start, part.stop):
                            dve.bn_stats(ST[:, n, :], X[:, n, :])

            @block.scalar
            def _(act):
                def normed_chunk(part):
                    for n in range(part.start, part.stop):
                        ins = act.activation(R[:, n, :], R[:, n, :], ACT.Identity, bias=k["NMR"][:, n:n + 1],
                                             scale=k["RSTD"][:, n:n + 1])
                    ins.then_inc(normed, 1)

                normed_chunk(chunks_[0][1])
                for c, part in chunks_:
                    if c + 1 < len(chunks_):
                        normed_chunk(chunks_[c + 1][1])
                    act.wait_ge(shifted, c + 1)
                    act.activation(R[:, part, :], R[:, part, :], ACT.Silu).then_inc(silu_done, 1)

            if layer == 0:
                @block.gpsimd
                def _(pool):
                    pool.memset(AGG[:, :, 0:D], 0.0)

                @block.sync
                def _(sp):
                    xg = a["xg1"].rearrange("(t p) d -> p t d", p=P)
                    for c, part in chunks_:
                        sp.wait_ge(silu_done, c + 1)
                        sp.dma_start(xg[:, part, :], R[:, part, :]).then_inc(stored, 16)
                    sp.wait_ge(stored, 16 * len(chunks_))
        if layer == 1:
            finish_ln(k, "5")


SCRATCH = [("tile_windows", (SK * P,), I32), ("groups", (2 * NG,), I32), ("records", (STILES * P + P, 2), I32), ("kv", (NT * P, 2 * D), F32), ("xg0", (NT * P, D), F32),
           ("xg1", (NT * P, D), F32), ("slots_in", (NSLOT + 2 * BT, D), F32), ("slots_out", (NSLOT + BT, D), F32)]


def chunks(w):
    r, c = w.shape
    return np.ascontiguousarray(w.reshape(r // P, P, c).transpose(1, 0, 2))


def spread(row):
    return np.ascontiguousarray(np.broadcast_to(row.reshape(1, -1), (P, row.size)))


def cols(row):
    return np.ascontiguousarray(row.reshape(-1, P).T)


def expert_packs(w1, b1, g, b, w2, b2):
    out = []
    for e in range(len(w1)):
        out.append(np.concatenate([chunks(w1[e]).reshape(P, -1), chunks(w2[e]).reshape(P, -1), cols(b1[e]),
                                   cols(g[e]), cols(b[e]), spread(b2[e])], axis=1))
    return np.stack(out)


def layout(inputs):
    i = {n: np.asarray(v) for n, v in inputs.items()}

    def edges(v, fill):
        v = v.reshape(-1)
        v = np.concatenate([v, np.full(ETP * P - E, fill, v.dtype)])
        return np.ascontiguousarray(v.reshape(ETP, P).T)

    one, zero = np.ones((NEXP, D), np.float32), np.zeros((NEXP, D), np.float32)
    return {
        "consts": constants(),
        "x": np.concatenate([i["x"], np.zeros((NT * P - N, D), i["x"].dtype)]),
        "src": edges(i["src"], 0), "src_key": edges(i["src"], PAD_DST), "dst": edges(i["dst"], PAD_DST), "edge_weight1": edges(i["edge_weight1"], 0),
        "w_qkv": chunks(np.concatenate([i["L0_gnn_Wq"], i["L0_gnn_Wk"], i["L0_gnn_Wv"]], axis=1)),
        "ffn": expert_packs(*(i["L0_gnn_" + n][None] for n in ("W1", "b1", "ln1_g", "ln1_b", "W2", "b2"))),
        "w_p": chunks(i["L0_gnn_Wp"]),
        "rows0": np.stack([spread(i["L0_gnn_" + n]) for n in ("bp", "ln1_g", "ln1_b", "ln2_g", "ln2_b")], 1),
        "router0": chunks(i["L0_ffn_router_w"].T), "router1": chunks(i["L1_ffn_Wr"]),
        "rbias1": spread(np.tile(i["L1_ffn_br"], NT)),
        "experts0": expert_packs(i["L0_ffn_w1"], i["L0_ffn_b1"], one, zero, i["L0_ffn_w2"], i["L0_ffn_b2"]),
        "experts1": expert_packs(i["L1_ffn_W1"], i["L1_ffn_b1"], i["L1_ffn_ln_g"], i["L1_ffn_ln_b"],
                                 i["L1_ffn_W2"], i["L1_ffn_b2"]),
        "w_g0": chunks(i["L1_gnn_W0"].T), "w_g1": chunks(i["L1_gnn_W1"].T),
        "rows_g0": np.stack([spread(i["L1_gnn_" + n]) for n in ("b0", "g0", "beta0")], 1),
        "rows_g1": np.stack([spread(i["L1_gnn_" + n]) for n in ("b1", "g1", "beta1")], 1),
    }


def program(nc, a):
    with ExitStack() as life:
        k = {"nc": nc, "a": a}

        def keep(name, shape, dt=F32, until=life):
            k[name] = until.enter_context(nc.sbuf_tensor(name + "_kept", shape, dt))

        for name in SOFTWARE:
            k[name] = life.enter_context(nc.semaphore(name))
        keep("X", [P, NT + 1, D])
        keep("C", [P, C_END])
        keep("ST", [P, NT + 1, 6])
        keep("VAR", [P, NT + 1])
        keep("RSTD", [P, NT + 1])
        keep("NMR", [P, NT + 1])
        keep("EPSC", [P, 1])
        with ExitStack() as gnn:
            keep("R", [P, NT + 1, D], F32, gnn)
            keep("SADDR", [P, ETP], I32, gnn)
            keep("EDGES", [P, ETP, 2], I32, gnn)
            keep("SWIN", [1, SK * P], I32, gnn)
            keep("TILEWIN", [P, SK], I32, gnn)
            keep("STURNS", [1, 1], I32, gnn)
            with ExitStack() as att:
                keep("DST", [P, ETP], F32, att)
                keep("SRC", [P, ETP], I32, att)
                keep("BIAS", [P, ETP], F32, att)
                keep("SHIFT", [P, 1], F32, att)
                keep("FLAG", [P, 1], F32, att)
                keep("MAXRUNS", [1, 2], I32, att)
                keep("GROUPS", [1, 2 * NG], I32, att)
                keep("GTURNS", [1, 1], I32, att)
                load_and_group(k)
                sort_by_source(k)
                keep("ACC", [P, NT + 1, VW], F32, att)
                keep("QX", [P, NT + 1, VW], F32, att)
                qkv(k)
                attention_max(k)
                attention_edges(k)
                attention_out(k)
            recycle_semaphores(nc)
            ffn(k)
            moe(k, 0)
            recycle_semaphores(nc)
            keep("AGG", [P, NT + 1, D + 1], F32, gnn)
            keep("RECS", [P, STILES, 2], I32, gnn)
            keep("KEYS", [P, STILES], F32, gnn)
            gnn_rows(k)
            gnn_edges(k, 0)
            gnn_nodes(k, 0)
            gnn_edges(k, 1)
            gnn_nodes(k, 1)
        recycle_semaphores(nc)
        moe(k, 1)


def kernel(**inputs):
    import concourse.bacc as _bacc
    from concourse.bass_utils import run_bass_kernel_spmd as _run

    arrays = layout(inputs)
    nc = _bacc.Bacc("TRN2", target_bir_lowering=False, num_devices=1)
    a = {n: nc.dram_tensor(n, v.shape, mybir.dt.from_np(v.dtype), kind="ExternalInput").ap()
         for n, v in arrays.items()}
    for n, shape, dt in SCRATCH:
        a[n] = nc.dram_tensor(n, shape, dt, kind="Internal").ap()
    a["out"] = nc.dram_tensor("out", (N, D), F32, kind="ExternalOutput").ap()
    program(nc, a)
    r = _run(nc, [arrays], core_ids=[0])
    return r.results[0]["out"]
```
